# Optimizing a Trainium2 kernel written in Bass

```python
import numpy as np
import jax
import jax.numpy as jnp

def _softmax(x, axis=-1):
    return jax.nn.softmax(x, axis=axis)

def _gelu(x):
    return jax.nn.gelu(x, approximate=True)

def _silu(x):
    return jax.nn.silu(x)

def _sigmoid(x):
    return jax.nn.sigmoid(x)

def _layernorm(x, axis=-1, eps=1e-05):
    m = jnp.mean(x, axis=axis, keepdims=True)
    v = jnp.var(x, axis=axis, keepdims=True)
    return (x - m) / jnp.sqrt(v + eps)

def _scatter_add(tgt, idx, src, axis=0):
    return tgt.at[idx].add(src)

def _segment_sum(src, seg, n):
    return jax.ops.segment_sum(src, seg, n)
kernel_name = 'mk_early_fusion_d1_tok_img512_r4_1567cb'

def setup_inputs(seed: int=0):
    np.random.seed(seed)
    _w = jnp.asarray

    def _rec_inputs():
        import jax
        import jax.numpy as jnp
        _rk = jax.random.key(seed)
        x = 7.57192e-06 + 1.00007 * jax.random.normal(jax.random.fold_in(_rk, 1), (64, 3, 224, 224), jnp.float32)
        txt = -1.28643e-11 + 0.999988 * jax.random.normal(jax.random.fold_in(_rk, 2), (64, 32, 128), jnp.float32)
        return (x, txt)
    x, txt = _rec_inputs()

    def _L0_tok_setup():
        import jax, jax.numpy as jnp
        import numpy as np
        DEPTH = 4
        HEADS = 8
        DIM = 128
        HID = 256
        P = 16
        IMG = 224
        GRID = IMG // P
        NPATCH = GRID * GRID
        NTOK = NPATCH + 1
        BATCH = 64
        EPS = 1e-05

        def layernorm(x, w, b):
            mu = jnp.mean(x, axis=-1, keepdims=True)
            var = jnp.mean(jnp.square(x - mu), axis=-1, keepdims=True)
            return (x - mu) * jax.lax.rsqrt(var + EPS) * w + b
        key = jax.random.key(seed)
        ks = jax.random.split(key, 12)
        s = 0.02
        inp = {'x': jax.random.normal(ks[0], (BATCH, 3, IMG, IMG), jnp.float32), 'conv_w': jax.random.normal(ks[1], (3 * P * P, DIM), jnp.float32) * s, 'conv_b': jnp.zeros((DIM,), jnp.float32), 'cls_token': jax.random.normal(ks[2], (1, 1, DIM), jnp.float32) * s, 'pos_embed': jax.random.normal(ks[3], (1, NTOK, DIM), jnp.float32) * s, 'ln1_w': jnp.ones((DEPTH, DIM), jnp.float32), 'ln1_b': jnp.zeros((DEPTH, DIM), jnp.float32), 'qkv_w': jax.random.normal(ks[4], (DEPTH, DIM, 3 * DIM), jnp.float32) * s, 'qkv_b': jnp.zeros((DEPTH, 3 * DIM), jnp.float32), 'proj_w': jax.random.normal(ks[5], (DEPTH, DIM, DIM), jnp.float32) * s, 'proj_b': jnp.zeros((DEPTH, DIM), jnp.float32), 'ln2_w': jnp.ones((DEPTH, DIM), jnp.float32), 'ln2_b': jnp.zeros((DEPTH, DIM), jnp.float32), 'fc1_w': jax.random.normal(ks[6], (DEPTH, DIM, HID), jnp.float32) * s, 'fc1_b': jnp.zeros((DEPTH, HID), jnp.float32), 'fc2_w': jax.random.normal(ks[7], (DEPTH, HID, DIM), jnp.float32) * s, 'fc2_b': jnp.zeros((DEPTH, DIM), jnp.float32), 'norm_w': jnp.ones((DIM,), jnp.float32), 'norm_b': jnp.zeros((DIM,), jnp.float32)}
        return inp
    _L0_tok_all = _L0_tok_setup()
    _L0_tok_in = {k: v for k, v in _L0_tok_all.items() if k in ('conv_w', 'conv_b', 'cls_token', 'pos_embed', 'ln1_w', 'ln1_b', 'qkv_w', 'qkv_b', 'proj_w', 'proj_b', 'ln2_w', 'ln2_b', 'fc1_w', 'fc1_b', 'fc2_w', 'fc2_b', 'norm_w', 'norm_b')}
    del _L0_tok_all

    def _L0_attn_setup():
        import jax, jax.numpy as jnp
        import numpy as np
        from jax import lax
        B, L, D = (8, 512, 128)

        def _mlp(x, w1, w2):
            return x + jax.nn.gelu(x @ w1, approximate=False) @ w2

        def _l2norm(t):
            n = jnp.linalg.norm(t, axis=-1, keepdims=True)
            return t / jnp.maximum(n, 1e-12)

        def _forward(x, conv_w, conv_b, q_w, mem_w1, mem_w2, eta_w1, eta_w2, alpha_w1, alpha_w2):
            xc = lax.conv_general_dilated(jnp.transpose(x, (0, 2, 1)), conv_w, window_strides=(1,), padding=[(3, 0)], feature_group_count=D, dimension_numbers=('NCH', 'OIH', 'NCH')) + conv_b[None, :, None]
            xc = jnp.transpose(xc, (0, 2, 1))
            q = _l2norm(xc @ q_w.T)
            eta_mean = jax.nn.sigmoid(_mlp(xc, eta_w1, eta_w2)).mean(axis=(0, 2))
            alpha_mean = jax.nn.sigmoid(_mlp(xc, alpha_w1, alpha_w2)).mean(axis=(0, 2))

            def step(carry, inp):
                w1, w2 = carry
                q_t, a_t, e_t = inp
                o_t = _mlp(q_t, w1, w2)
                new_w1 = w1 * a_t - e_t * 0.01
                new_w2 = w2 * a_t - e_t * 0.01
                return ((new_w1, new_w2), o_t)
            qs = jnp.transpose(q, (1, 0, 2))
            (_, _), outs = lax.scan(step, (mem_w1, mem_w2), (qs, alpha_mean, eta_mean))
            return jnp.transpose(outs, (1, 0, 2))
        key = jax.random.key(seed)
        ks = jax.random.split(key, 12)
        s = 0.02
        return {'x': jax.random.normal(ks[0], (B, L, D), jnp.float32), 'conv_w': jax.random.normal(ks[1], (D, 1, 4), jnp.float32) * s, 'conv_b': jax.random.normal(ks[2], (D,), jnp.float32) * s, 'q_w': jax.random.normal(ks[3], (D, D), jnp.float32) * s, 'mem_w1': jax.random.normal(ks[4], (D, D), jnp.float32) * s, 'mem_w2': jax.random.normal(ks[5], (D, D), jnp.float32) * s, 'eta_w1': jax.random.normal(ks[6], (D, D), jnp.float32) * s, 'eta_w2': jax.random.normal(ks[7], (D, D), jnp.float32) * s, 'alpha_w1': jax.random.normal(ks[8], (D, D), jnp.float32) * s, 'alpha_w2': jax.random.normal(ks[9], (D, D), jnp.float32) * s}
    _L0_attn_all = _L0_attn_setup()
    _L0_attn_in = {k: v for k, v in _L0_attn_all.items() if k in ('conv_w', 'conv_b', 'q_w', 'mem_w1', 'mem_w2', 'eta_w1', 'eta_w2', 'alpha_w1', 'alpha_w2')}
    del _L0_attn_all

    def _L0_ffn_setup():
        import jax, jax.numpy as jnp
        import numpy as np
        D, H, E, B, S = (128, 512, 16, 8, 2048)
        MAX_GROUP_SIZE = 1024
        MIN_CAPACITY = 8
        CAPACITY_FACTOR = 1.0

        def _group_dims(num_tokens, num_experts):
            num_groups = -(-num_tokens // MAX_GROUP_SIZE)
            while num_tokens % num_groups != 0 or num_groups % num_experts != 0:
                num_groups += 1
            return (num_tokens // num_groups, num_groups)
        key = jax.random.key(seed)
        ks = jax.random.split(key, 6)
        s = 0.02
        return {'x': jax.random.normal(ks[0], (B, S, D), jnp.float32), 'gate_w': jax.random.normal(ks[1], (D, E), jnp.float32) * s, 'w1': jax.random.normal(ks[2], (E, D, H), jnp.float32) * s, 'b1': jnp.zeros((E, H), jnp.float32), 'w2': jax.random.normal(ks[3], (E, H, D), jnp.float32) * s, 'b2': jnp.zeros((E, D), jnp.float32), 'sw1': jax.random.normal(ks[4], (D, H), jnp.float32) * s, 'sb1': jnp.zeros((H,), jnp.float32), 'sw2': jax.random.normal(ks[5], (H, D), jnp.float32) * s, 'sb2': jnp.zeros((D,), jnp.float32)}
    _L0_ffn_all = _L0_ffn_setup()
    _L0_ffn_in = {k: v for k, v in _L0_ffn_all.items() if k in ('gate_w', 'w1', 'b1', 'w2', 'b2', 'sw1', 'sb1', 'sw2', 'sb2')}
    del _L0_ffn_all
    return {'x': x, 'txt': txt, 'L0_tok_conv_w': _L0_tok_in['conv_w'], 'L0_tok_conv_b': _L0_tok_in['conv_b'], 'L0_tok_cls_token': _L0_tok_in['cls_token'], 'L0_tok_pos_embed': _L0_tok_in['pos_embed'], 'L0_tok_ln1_w': _L0_tok_in['ln1_w'], 'L0_tok_ln1_b': _L0_tok_in['ln1_b'], 'L0_tok_qkv_w': _L0_tok_in['qkv_w'], 'L0_tok_qkv_b': _L0_tok_in['qkv_b'], 'L0_tok_proj_w': _L0_tok_in['proj_w'], 'L0_tok_proj_b': _L0_tok_in['proj_b'], 'L0_tok_ln2_w': _L0_tok_in['ln2_w'], 'L0_tok_ln2_b': _L0_tok_in['ln2_b'], 'L0_tok_fc1_w': _L0_tok_in['fc1_w'], 'L0_tok_fc1_b': _L0_tok_in['fc1_b'], 'L0_tok_fc2_w': _L0_tok_in['fc2_w'], 'L0_tok_fc2_b': _L0_tok_in['fc2_b'], 'L0_tok_norm_w': _L0_tok_in['norm_w'], 'L0_tok_norm_b': _L0_tok_in['norm_b'], 'L0_attn_conv_w': _L0_attn_in['conv_w'], 'L0_attn_conv_b': _L0_attn_in['conv_b'], 'L0_attn_q_w': _L0_attn_in['q_w'], 'L0_attn_mem_w1': _L0_attn_in['mem_w1'], 'L0_attn_mem_w2': _L0_attn_in['mem_w2'], 'L0_attn_eta_w1': _L0_attn_in['eta_w1'], 'L0_attn_eta_w2': _L0_attn_in['eta_w2'], 'L0_attn_alpha_w1': _L0_attn_in['alpha_w1'], 'L0_attn_alpha_w2': _L0_attn_in['alpha_w2'], 'L0_ffn_gate_w': _L0_ffn_in['gate_w'], 'L0_ffn_w1': _L0_ffn_in['w1'], 'L0_ffn_b1': _L0_ffn_in['b1'], 'L0_ffn_w2': _L0_ffn_in['w2'], 'L0_ffn_b2': _L0_ffn_in['b2'], 'L0_ffn_sw1': _L0_ffn_in['sw1'], 'L0_ffn_sb1': _L0_ffn_in['sb1'], 'L0_ffn_sw2': _L0_ffn_in['sw2'], 'L0_ffn_sb2': _L0_ffn_in['sb2']}

def reference(x, txt, L0_tok_conv_w, L0_tok_conv_b, L0_tok_cls_token, L0_tok_pos_embed, L0_tok_ln1_w, L0_tok_ln1_b, L0_tok_qkv_w, L0_tok_qkv_b, L0_tok_proj_w, L0_tok_proj_b, L0_tok_ln2_w, L0_tok_ln2_b, L0_tok_fc1_w, L0_tok_fc1_b, L0_tok_fc2_w, L0_tok_fc2_b, L0_tok_norm_w, L0_tok_norm_b, L0_attn_conv_w, L0_attn_conv_b, L0_attn_q_w, L0_attn_mem_w1, L0_attn_mem_w2, L0_attn_eta_w1, L0_attn_eta_w2, L0_attn_alpha_w1, L0_attn_alpha_w2, L0_ffn_gate_w, L0_ffn_w1, L0_ffn_b1, L0_ffn_w2, L0_ffn_b2, L0_ffn_sw1, L0_ffn_sb1, L0_ffn_sw2, L0_ffn_sb2):
    import jax
    import jax.numpy as jnp

    def _L0_tok_ref(x, conv_w, conv_b, cls_token, pos_embed, ln1_w, ln1_b, qkv_w, qkv_b, proj_w, proj_b, ln2_w, ln2_b, fc1_w, fc1_b, fc2_w, fc2_b, norm_w, norm_b):
        import jax, jax.numpy as jnp
        import numpy as np
        DEPTH = 4
        HEADS = 8
        DIM = 128
        HID = 256
        P = 16
        IMG = 224
        GRID = IMG // P
        NPATCH = GRID * GRID
        NTOK = NPATCH + 1
        BATCH = 64
        EPS = 1e-05

        def layernorm(x, w, b):
            mu = jnp.mean(x, axis=-1, keepdims=True)
            var = jnp.mean(jnp.square(x - mu), axis=-1, keepdims=True)
            return (x - mu) * jax.lax.rsqrt(var + EPS) * w + b
        B = x.shape[0]
        hd = DIM // HEADS
        scale = hd ** (-0.5)
        patches = x.reshape(B, 3, GRID, P, GRID, P)
        patches = patches.transpose(0, 2, 4, 1, 3, 5).reshape(B, NPATCH, 3 * P * P)
        tok = patches @ conv_w + conv_b
        cls = jnp.broadcast_to(cls_token, (B, 1, DIM))
        h = jnp.concatenate([cls, tok], axis=1) + pos_embed
        for i in range(DEPTH):
            y = layernorm(h, ln1_w[i], ln1_b[i])
            qkv = (y @ qkv_w[i] + qkv_b[i]).reshape(B, NTOK, 3, HEADS, hd)
            qkv = qkv.transpose(2, 0, 3, 1, 4)
            q, k, v = (qkv[0], qkv[1], qkv[2])
            attn = jax.nn.softmax(jnp.einsum('bhnd,bhmd->bhnm', q, k) * scale, axis=-1)
            o = jnp.einsum('bhnm,bhmd->bhnd', attn, v)
            o = o.transpose(0, 2, 1, 3).reshape(B, NTOK, DIM)
            h = h + (o @ proj_w[i] + proj_b[i])
            y = layernorm(h, ln2_w[i], ln2_b[i])
            y = jax.nn.gelu(y @ fc1_w[i] + fc1_b[i], approximate=False)
            h = h + (y @ fc2_w[i] + fc2_b[i])
        return layernorm(h, norm_w, norm_b)

    def _L0_attn_ref(x, conv_w, conv_b, q_w, mem_w1, mem_w2, eta_w1, eta_w2, alpha_w1, alpha_w2):
        import jax, jax.numpy as jnp
        import numpy as np
        from jax import lax
        B, L, D = (8, 512, 128)

        def _mlp(x, w1, w2):
            return x + jax.nn.gelu(x @ w1, approximate=False) @ w2

        def _l2norm(t):
            n = jnp.linalg.norm(t, axis=-1, keepdims=True)
            return t / jnp.maximum(n, 1e-12)

        def _forward(x, conv_w, conv_b, q_w, mem_w1, mem_w2, eta_w1, eta_w2, alpha_w1, alpha_w2):
            xc = lax.conv_general_dilated(jnp.transpose(x, (0, 2, 1)), conv_w, window_strides=(1,), padding=[(3, 0)], feature_group_count=D, dimension_numbers=('NCH', 'OIH', 'NCH')) + conv_b[None, :, None]
            xc = jnp.transpose(xc, (0, 2, 1))
            q = _l2norm(xc @ q_w.T)
            eta_mean = jax.nn.sigmoid(_mlp(xc, eta_w1, eta_w2)).mean(axis=(0, 2))
            alpha_mean = jax.nn.sigmoid(_mlp(xc, alpha_w1, alpha_w2)).mean(axis=(0, 2))

            def step(carry, inp):
                w1, w2 = carry
                q_t, a_t, e_t = inp
                o_t = _mlp(q_t, w1, w2)
                new_w1 = w1 * a_t - e_t * 0.01
                new_w2 = w2 * a_t - e_t * 0.01
                return ((new_w1, new_w2), o_t)
            qs = jnp.transpose(q, (1, 0, 2))
            (_, _), outs = lax.scan(step, (mem_w1, mem_w2), (qs, alpha_mean, eta_mean))
            return jnp.transpose(outs, (1, 0, 2))
        return _forward(x, conv_w, conv_b, q_w, mem_w1, mem_w2, eta_w1, eta_w2, alpha_w1, alpha_w2)

    def _L0_ffn_ref(x, gate_w, w1, b1, w2, b2, sw1, sb1, sw2, sb2):
        import jax, jax.numpy as jnp
        import numpy as np
        D, H, E, B, S = (128, 512, 16, 8, 2048)
        MAX_GROUP_SIZE = 1024
        MIN_CAPACITY = 8
        CAPACITY_FACTOR = 1.0

        def _group_dims(num_tokens, num_experts):
            num_groups = -(-num_tokens // MAX_GROUP_SIZE)
            while num_tokens % num_groups != 0 or num_groups % num_experts != 0:
                num_groups += 1
            return (num_tokens // num_groups, num_groups)
        Bn, Sn, Dn = x.shape
        En = gate_w.shape[1]
        T = Bn * Sn
        group_size, num_groups = _group_dims(T, En)
        cap = max(int(round(CAPACITY_FACTOR * group_size * num_groups / En)), MIN_CAPACITY)
        xg = x.reshape(num_groups, group_size, Dn)
        logits = jnp.einsum('gsd,de->gse', xg, gate_w)
        probs = jax.nn.softmax(logits, axis=-1)
        flat_probs = probs.transpose(2, 0, 1).reshape(En, T)
        scores, tok_idx = jax.lax.top_k(flat_probs, cap)
        xf = x.reshape(T, Dn)
        toks = xf[tok_idx]
        h = jax.nn.gelu(jnp.einsum('ecd,edh->ech', toks, w1) + b1[:, None, :])
        y = jnp.einsum('ech,ehd->ecd', h, w2) + b2[:, None, :]
        y = y * scores[..., None]
        routed = jnp.zeros_like(xf).at[tok_idx.reshape(-1)].add(y.reshape(-1, Dn))
        shared = jax.nn.gelu(xf @ sw1 + sb1) @ sw2 + sb2
        out = (routed + shared).reshape(Bn, Sn, Dn)
        return out
    h = _L0_tok_ref(x, L0_tok_conv_w, L0_tok_conv_b, L0_tok_cls_token, L0_tok_pos_embed, L0_tok_ln1_w, L0_tok_ln1_b, L0_tok_qkv_w, L0_tok_qkv_b, L0_tok_proj_w, L0_tok_proj_b, L0_tok_ln2_w, L0_tok_ln2_b, L0_tok_fc1_w, L0_tok_fc1_b, L0_tok_fc2_w, L0_tok_fc2_b, L0_tok_norm_w, L0_tok_norm_b)
    h = jnp.concatenate([h, txt], axis=1)
    h = h + _L0_attn_ref(_layernorm(h, axis=-1), L0_attn_conv_w, L0_attn_conv_b, L0_attn_q_w, L0_attn_mem_w1, L0_attn_mem_w2, L0_attn_eta_w1, L0_attn_eta_w2, L0_attn_alpha_w1, L0_attn_alpha_w2)
    h = h + _L0_ffn_ref(_layernorm(h, axis=-1), L0_ffn_gate_w, L0_ffn_w1, L0_ffn_b1, L0_ffn_w2, L0_ffn_b2, L0_ffn_sw1, L0_ffn_sb1, L0_ffn_sw2, L0_ffn_sb2)
    return h

_drawn_inputs = setup_inputs


def setup_inputs(seed=0):
    import zlib

    import numpy as np

    out = dict(_drawn_inputs(seed))
    spreads = {'L0_tok_conv_b': (0.0, 0.1),
     'L0_tok_ln1_w': (1.0, 0.6),
     'L0_tok_ln1_b': (0.0, 0.524),
     'L0_tok_qkv_b': (0.0, 0.1),
     'L0_tok_proj_b': (0.0, 0.1),
     'L0_tok_ln2_w': (1.0, 0.6),
     'L0_tok_ln2_b': (0.0, 0.724),
     'L0_tok_fc1_b': (0.0, 0.1),
     'L0_tok_fc2_b': (0.0, 0.1),
     'L0_tok_norm_w': (1.0, 0.2),
     'L0_tok_norm_b': (0.0, 0.1),
     'L0_ffn_b1': (0.0, 0.8),
     'L0_ffn_b2': (0.0, 0.8),
     'L0_ffn_sb1': (0.0, 0.367),
     'L0_ffn_sb2': (0.0, 0.1)}
    factors = {'L0_tok_cls_token': 24.262,
     'L0_attn_mem_w1': 35.831,
     'L0_attn_mem_w2': 39.837,
     'L0_attn_eta_w1': 200.0,
     'L0_attn_eta_w2': 200.0,
     'L0_attn_alpha_w1': 200.0,
     'L0_attn_alpha_w2': 200.0,
     'L0_ffn_gate_w': 5.728,
     'L0_ffn_w1': 8.0,
     'L0_ffn_w2': 8.0}
    for name, (base, spread) in spreads.items():
        noise = np.random.default_rng([zlib.crc32(name.encode()), seed]).standard_normal(out[name].shape)
        drawn = base * np.exp(spread * noise) if base else spread * noise
        out[name] = jnp.asarray(drawn.astype(out[name].dtype))
    for name, factor in factors.items():
        out[name] = (out[name] * factor).astype(out[name].dtype)
    return out
```

```python
from contextlib import ExitStack

import concourse.bass as bass
from concourse import mybir

F32 = mybir.dt.float32
BF16 = mybir.dt.bfloat16
I32 = mybir.dt.int32
U32 = mybir.dt.uint32
ALU = mybir.AluOpType
ACT = mybir.ActivationFunctionType
AX = mybir.AxisListType

B, D, HEADS, HD = 64, 128, 8, 16
DEPTH, HID = 4, 256
NTOK = 197
TC = 99
TB = 2 * TC
PAIRS = B // 2
PW = 2 * TB
KC = 3 * 16 * 16 // 128
TXT = 32
L = NTOK + TXT
T = B * L
EPS = 1e-5
SPLIT = 6 * HD


def below(value, total):
    return min(value, total) if isinstance(value, int) else value


def wait(eng, sem, value):
    if isinstance(value, int) and value <= 0:
        return
    eng.wait_ge(sem, value)


def wait_alone(eng, sem, value):
    if not isinstance(value, int):
        with eng.register() as count:
            eng.reg_mov(count, value)
            eng.wait_ge(sem, 1)
            eng.wait_ge(sem, count)
    else:
        wait(eng, sem, value)


class Sems:

    def __init__(self, nc, ctx, names):
        self.nc, self.all = nc, {}
        for n in names.split():
            self.all[n] = ctx.enter_context(nc.semaphore(n))

    def __getitem__(self, name):
        return self.all[name]

    def clear(self):
        for s in self.all.values():
            self.nc.gpsimd.sem_clear(s)
        self.nc.all_engine_barrier()


class Core:
    pass


def load_constants(nc, g, A):
    with ExitStack() as ctx:
        s = Sems(nc, ctx, "c_load c_set")
        with nc.Block() as block:
            @block.sync
            def _(sp):
                sp.dma_start(g.ident[:], A["ident"]).then_inc(s["c_load"], 16)
                sp.wait_ge(s["c_load"], 16)

            @block.gpsimd
            def _(pool):
                nc.gpsimd.memset(g.neg_half[:], -0.5).then_inc(s["c_set"], 1)
        s.clear()


def patch_phase(nc, g, A):
    NB = 4
    with ExitStack() as ctx:
        s = Sems(nc, ctx, "p_const p_add " + " ".join(f"p_x{u} p_mm{u} p_h{u}" for u in range(NB)))
        xb = ctx.enter_context(nc.sbuf_tensor("xpatch", [128, NB, KC, TB], F32))
        wc = ctx.enter_context(nc.sbuf_tensor("conv_w", [128, KC, D], F32))
        posb = ctx.enter_context(nc.sbuf_tensor("pos", [TC, 2, D], F32))
        rowb = ctx.enter_context(nc.sbuf_tensor("rowb", [TC, 2, D], F32))
        ps = [ctx.enter_context(nc.psum_tensor(f"p_ps{i}", [128, 512], F32)) for i in range(NB)]
        x_loaded, x_used, sum_read = ([s[f"{n}{u}"] for u in range(NB)] for n in ("p_x", "p_mm", "p_h"))
        with nc.Block() as block:
            @block.sync
            def _(sp):
                sp.dma_start(wc[:], A["conv_w"]).then_inc(s["p_const"], 16)
                sp.dma_start(posb[:], A["pos"]).then_inc(s["p_const"], 16)
                sp.dma_start(rowb[:], A["row_bias"]).then_inc(s["p_const"], 16)
                with sp.Fori(0, B // NB) as j:
                    for u in range(NB):
                        sp.wait_ge(x_used[u], j)
                        sp.dma_start(xb[:, u], A["x"][bass.ds(j * NB + u, 1)]
                                     .rearrange("o p k t -> p (o k) t")).then_inc(x_loaded[u], 16)

            @block.tensor
            def _(pe):
                pe.wait_ge(s["p_const"], 48)
                with pe.Fori(0, B // NB) as j:
                    for u in range(NB):
                        pe.wait_ge(x_loaded[u], j * 16 + 16)
                        pe.wait_ge(sum_read[u], j)
                        for c in range(2):
                            for k in range(KC):
                                mm = nc.tensor.matmul(ps[u][0:TC, c * D:(c + 1) * D],
                                                      xb[:, u, k, c * TC:(c + 1) * TC], wc[:, k, :],
                                                      start=(k == 0), stop=(k == KC - 1))
                        mm.then_inc(x_used[u], 1)

            @block.vector
            def _(dve):
                dve.wait_ge(s["p_const"], 48)
                nc.vector.tensor_tensor(posb[:], posb[:], rowb[:], ALU.add).then_inc(s["p_add"], 1)
                dve.wait_ge(s["p_add"], 1)
                with dve.Fori(0, B // NB) as j:
                    for u in range(NB):
                        dve.wait_ge(x_used[u], j + 1)
                        nc.vector.tensor_tensor(
                            g.h[0:TC, bass.ds(j * (2 * NB) + 2 * u, 2), :],
                            ps[u][0:TC, 0:2 * D].rearrange("p (c d) -> p c d", c=2),
                            posb[:], ALU.add).then_inc(sum_read[u], 1)
        s.clear()


def load_layer(nc, g, A, layer):
    one = bass.ds(layer, 1)
    with ExitStack() as ctx:
        s = Sems(nc, ctx, "w_load w_scale")
        with nc.Block() as block:
            @block.sync
            def _(sp):
                sp.dma_start(g.w[:], A["weights"][one].rearrange("o p n -> p (o n)")).then_inc(s["w_load"], 16)
                sp.dma_start(g.cols[:], A["cols"][one].rearrange("o p n -> p (o n)")).then_inc(s["w_load"], 16)
                sp.dma_start(g.rows[:], A["rows"][one].rearrange("o p n -> p (o n)")).then_inc(s["w_load"], 16)
                sp.wait_ge(s["w_load"], 48)

            @block.vector
            def _(dve):
                dve.wait_ge(s["w_load"], 48)
                nc.vector.tensor_scalar(g.wq, g.wq, HD ** -0.5, None, ALU.mult).then_inc(s["w_scale"], 1)
                nc.vector.tensor_scalar(g.bq, g.bq, HD ** -0.5, None, ALU.mult).then_inc(s["w_scale"], 1)
                dve.wait_ge(s["w_scale"], 2)
        s.clear()


def attention_phase(nc, g):
    with ExitStack() as ctx:
        s = Sems(nc, ctx, "stats aggr var_eps rstd xn turned yT q_k v hi res mid lo v_aug "
                 "part_wr stack_rd max_rd scores row_max max_turned max_parts scores_t probs pv "
                 "o_copied o_turned recip o_norm oT_turned oT proj h_bias h_done ones")

        def sb(name, shape, dt=F32):
            return ctx.enter_context(nc.sbuf_tensor("a_" + name, shape, dt))

        stats, mv, ve, rstd = sb("stats", [TC, 4, 6]), sb("mv", [TC, 4, 2]), sb("ve", [TC, 4]), sb("rstd", [TC, 4])
        xn, yT = sb("xn", [TC, 4, D]), sb("yT", [D, PW])
        parts = sb("parts", [D, 3, 2, PW], BF16)
        res = sb("res", [D, 2, PW])
        q_st = [sb(f"q_st{p}", [SPLIT + 3, HEADS, PW], BF16) for p in range(2)]
        k_st = [sb(f"k_st{p}", [SPLIT + 3, HEADS, PW], BF16) for p in range(2)]
        v_aug = [sb(f"v_aug{p}", [TC, 4, HEADS, 32]) for p in range(2)]
        neg_max = sb("neg_max", [TC, 32])
        max_res, max_parts = sb("max_res", [32, TC]), sb("max_parts", [32, 3, TC], BF16)
        probs = sb("probs", [TC, 4, 4 * TB])
        o_sb, rec, o_n, oT = sb("o_sb", [D, 2 * TB]), sb("rec", [TC, 16]), sb("o_n", [TC, 2, D]), sb("oT", [D, PW])
        S = ctx.enter_context(nc.psum_tensor("a_S", [128, 2, 512], F32))
        St = ctx.enter_context(nc.psum_tensor("a_St", [128, 2, 512], F32))
        O, M0, M1, M2 = (ctx.enter_context(nc.psum_tensor(n, [128, 512], F32)) for n in ("a_O", "a_M0", "a_M1", "a_M2"))
        spill = [[nc.dram_tensor(f"spill_{n}{p}", [HEADS, 3 * HD, PW], BF16).ap() for p in range(2)] for n in "qk"]

        def steps(body):
            def run(eng):
                for i in (-2, -1):
                    body(i, i % 2, True, i + 1 >= 0, False)
                with eng.Fori(0, PAIRS // 2 - 1) as j:
                    for p in range(2):
                        body(j * 2 + p, p, True, True, True)
                for i in (PAIRS - 2, PAIRS - 1):
                    body(i, i % 2, False, i + 1 < PAIRS, True)
            return run

        def upto(n, value):
            return below(value, n * PAIRS)

        with nc.Block() as block:
            @block.sync
            def _(sp):
                def body(i, p, front, maxima, back):
                    if front:
                        for part, ready, n in ((0, s["hi"], 2), (1, s["mid"], 1), (2, s["lo"], 1)):
                            wait(sp, ready, n * (i + 3))
                            for qk in range(2):
                                to = 2 - part if qk == 0 else part
                                sp.dma_start(spill[qk][p][:, to * HD:(to + 1) * HD, :],
                                             parts[:, part, qk, :]).then_inc(s["part_wr"], 16)
                        wait_alone(sp, s["part_wr"], 96 * (i + 3))
                        wait(sp, s["scores_t"], 8 * (i + 1))
                        for qk, st in ((1, k_st[p]), (0, q_st[p])):
                            for to, n in ((0, 3), (3, 2), (5, 1)):
                                at = 0 if qk == 1 else 3 - n
                                sp.dma_start(st[to * HD:(to + n) * HD, :, :],
                                             spill[qk][p][:, at * HD:(at + n) * HD, :]
                                             .rearrange("h r t -> r h t")).then_inc(s["stack_rd"], 16)
                    if maxima:
                        wait(sp, s["max_parts"], 4 * (i + 2))
                        for part in range(3):
                            sp.dma_start(q_st[1 - p][SPLIT + part:SPLIT + part + 1, :, :]
                                         .rearrange("o h (x t) -> o (h x) t", t=TC),
                                         max_parts[:, part, :]).then_inc(s["max_rd"], 16)
                steps(body)(sp)
                sp.wait_ge(s["part_wr"], 96 * PAIRS)

            @block.tensor
            def _(pe):
                def scores(i, p, u):
                    b, half, c = u // 4, u // 2 % 2, u % 2
                    if u == 0:
                        wait(pe, s["stack_rd"], 96 * (i + 1))
                    wait(pe, s["row_max"], 8 * i + u)
                    for j in range(4):
                        head = half * 4 + j
                        mm = nc.tensor.matmul(S[0:TC, j // 2, j % 2 * TB:j % 2 * TB + NTOK],
                                              q_st[p][0:SPLIT, head, b * TB + c * TC:b * TB + (c + 1) * TC],
                                              k_st[p][0:SPLIT, head, b * TB:b * TB + NTOK], start=True, stop=True)
                    mm.then_inc(s["scores"], 1)

                def scores_t(i, p, u):
                    b, half, c = u // 4, u // 2 % 2, u % 2
                    keys = TC - c
                    if u == 0:
                        wait(pe, s["max_rd"], 48 * (i + 1))
                    wait(pe, s["probs"], 8 * i + u)
                    for j in range(4):
                        head = half * 4 + j
                        at = b * TB + c * TC
                        mm = nc.tensor.matmul(St[0:keys, j // 2, j % 2 * TB:(j % 2 + 1) * TB],
                                              k_st[p][:, head, at:at + keys],
                                              q_st[p][:, head, b * TB:(b + 1) * TB], start=True, stop=True)
                    mm.then_inc(s["scores_t"], 1)

                def pv(i, p, b, half):
                    if b == 0 and half == 0:
                        wait(pe, s["v_aug"], i + 1)
                    if half == 0:
                        wait(pe, s["o_copied"], 2 * i + b)
                    wait(pe, s["probs"], 8 * i + 4 * b + 2 * half + 2)
                    for j in range(4):
                        for c in range(2):
                            keys = TC - c
                            mm = nc.tensor.matmul(O[32 * j:32 * j + 32, half * TB:(half + 1) * TB],
                                                  v_aug[p][0:keys, 2 * b + c, half * 4 + j, :],
                                                  probs[0:keys, 2 * half + c, j * TB:(j + 1) * TB],
                                                  start=(c == 0), stop=(c == 1))
                    mm.then_inc(s["pv"], 1)

                def o_turn(i, b):
                    wait(pe, s["o_copied"], 2 * i + b + 1)
                    for c in range(2):
                        for half in range(2):
                            x = 2 * c + half
                            mm = nc.tensor.transpose(M1[0:TC, x * D:(x + 1) * D],
                                                     o_sb[:, half * TB + c * TC:half * TB + (c + 1) * TC],
                                                     g.ident[:])
                    mm.then_inc(s["o_turned"], 1)

                def oT_turn(i, b):
                    wait(pe, s["o_norm"], 2 * i + b + 1)
                    wait(pe, s["oT"], 2 * i + b)
                    for c in range(2):
                        at = b * TB + c * TC
                        mm = nc.tensor.transpose(M2[:, at:at + TC], o_n[:, c, :], g.ident[0:TC, 0:TC])
                    mm.then_inc(s["oT_turned"], 1)

                pe.sem_inc(s["pv"], 1)
                pe.wait_ge(s["ones"], 4)

                def body(i, p, front, maxima, back):
                    q = 1 - p
                    if back:
                        scores_t(i, p, 0)
                        scores_t(i, p, 1)
                        pv(i, p, 0, 0)
                    if front:
                        wait(pe, s["xn"], i + 3)
                        wait(pe, s["v_aug"], i + 2)
                        for t in range(4):
                            mm = nc.tensor.transpose(M0[:, t * TC:(t + 1) * TC], xn[:, t, :], g.ident[0:TC, 0:TC])
                        mm.then_inc(s["turned"], 1)
                    if maxima:
                        scores(i + 1, q, 0)
                    if back:
                        scores_t(i, p, 2)
                    if maxima:
                        scores(i + 1, q, 1)
                    if front:
                        wait(pe, s["yT"], i + 3)
                        wait(pe, s["h_done"], i)
                        nc.tensor.matmul(M1[:, 0:PW], g.wq, yT[:], start=True, stop=True).then_inc(s["q_k"], 1)
                        wait(pe, s["oT"], 2 * i)
                        nc.tensor.matmul(M2[:, 0:PW], g.wk, yT[:], start=True, stop=True).then_inc(s["q_k"], 1)
                    if back:
                        scores_t(i, p, 3)
                    if maxima:
                        scores(i + 1, q, 2)
                    if back:
                        pv(i, p, 0, 1)
                        scores_t(i, p, 4)
                    if maxima:
                        scores(i + 1, q, 3)
                    if back:
                        wait(pe, s["res"], upto(2, 2 * (i + 3)))
                        wait(pe, s["h_done"], i)
                        o_turn(i, 0)
                        scores_t(i, p, 5)
                    if maxima:
                        scores(i + 1, q, 4)
                    if back:
                        pv(i, p, 1, 0)
                        oT_turn(i, 0)
                        scores_t(i, p, 6)
                    if maxima:
                        scores(i + 1, q, 5)
                    if back:
                        scores_t(i, p, 7)
                    if maxima:
                        scores(i + 1, q, 6)
                        scores(i + 1, q, 7)
                    if back:
                        pv(i, p, 1, 1)
                    if maxima:
                        wait(pe, s["row_max"], 8 * (i + 2))
                        wait(pe, s["yT"], upto(1, i + 3))
                        nc.tensor.transpose(M0[0:32, 0:TC], neg_max[:], g.ident[0:TC, 0:TC]).then_inc(s["max_turned"], 1)
                    if back:
                        o_turn(i, 1)
                        oT_turn(i, 1)
                    if front:
                        wait(pe, s["max_parts"], 4 * (i + 2))
                        for t in range(4):
                            mm = nc.tensor.matmul(M0[0:TC, t * D:(t + 1) * D], yT[:, t * TC:(t + 1) * TC], g.wv,
                                                  start=True, stop=True)
                        mm.then_inc(s["v"], 1)
                    if back:
                        wait(pe, s["oT"], 2 * i + 2)
                        for t in range(4):
                            mm = nc.tensor.matmul(M1[0:TC, t * D:(t + 1) * D], oT[:, t * TC:(t + 1) * TC], g.wp,
                                                  start=True, stop=True)
                        mm.then_inc(s["proj"], 1)
                steps(body)(pe)

            @block.scalar
            def _(act):
                def exp(i, u):
                    keys = TC - u % 2
                    wait(act, s["scores_t"], 8 * i + u + 1)
                    wait(act, s["pv"], 4 * i + u // 2)
                    nc.scalar.activation(probs[0:keys, u % 4, :].rearrange("p (x t) -> p x t", x=2),
                                         St[0:keys, :, 0:2 * TB], ACT.Exp).then_inc(s["probs"], 1)

                def o_copy(i, b):
                    wait(act, s["pv"], 4 * i + 2 * b + 3)
                    wait(act, s["o_turned"], 2 * i + b)
                    nc.scalar.activation(o_sb[:], O[:, 0:2 * TB], ACT.Copy).then_inc(s["o_copied"], 1)

                def oT_copy(i, b):
                    wait(act, s["oT_turned"], 2 * i + b + 1)
                    wait(act, s["proj"], i)
                    nc.scalar.activation(oT[:, b * TB:(b + 1) * TB], M2[:, b * TB:(b + 1) * TB],
                                         ACT.Copy).then_inc(s["oT"], 1)

                def body(i, p, front, maxima, back):
                    if back:
                        exp(i, 0)
                        exp(i, 1)
                    if front:
                        wait(act, s["turned"], i + 3)
                        wait(act, s["v"], i + 2)
                        nc.scalar.activation(yT[:], M0[:, 0:PW], ACT.Identity, bias=g.ln1_b,
                                             scale=g.ln1_w).then_inc(s["yT"], 1)
                    if back:
                        exp(i, 2)
                    if front:
                        for qk, (m, bias) in enumerate(((M1, g.bq), (M2, g.bk))):
                            wait(act, s["q_k"], 2 * (i + 2) + qk + 1)
                            wait(act, s["part_wr"], 96 * (i + 2))
                            nc.scalar.activation(parts[:, 0, qk, :], m[:, 0:PW], ACT.Identity,
                                                 bias=bias).then_inc(s["hi"], 1)
                    if back:
                        exp(i, 3)
                    if front:
                        wait(act, s["res"], 2 * (i + 3))
                        nc.scalar.activation(parts[:, 1, :, :], res[:], ACT.Copy).then_inc(s["mid"], 1)
                    if back:
                        o_copy(i, 0)
                        exp(i, 4)
                        exp(i, 5)
                        oT_copy(i, 0)
                        exp(i, 6)
                        exp(i, 7)
                        o_copy(i, 1)
                        oT_copy(i, 1)
                steps(body)(act)

            @block.gpsimd
            def _(pool):
                def body(i, p, front, maxima, back):
                    if not front:
                        return
                    wait_alone(pool, s["aggr"], i + 3)
                    nc.gpsimd.tensor_scalar(ve[:], mv[:, :, 1], EPS, None, ALU.add).then_inc(s["var_eps"], 1)
                    wait(pool, s["var_eps"], i + 3)
                    wait(pool, s["xn"], i + 2)
                    nc.gpsimd.tensor_tensor(rstd[:], ve[:], g.neg_half[0:TC, 0:1].to_broadcast([TC, 4]),
                                            ALU.pow).then_inc(s["rstd"], 1)
                    wait(pool, s["xn"], i + 3)
                    hp = g.h[0:TC, bass.ds((i + 2) * 4, 4), :]
                    nc.gpsimd.tensor_tensor(hp, hp, g.bp.unsqueeze(1).to_broadcast([TC, 4, D]),
                                            ALU.add).then_inc(s["h_bias"], 1)
                    wait(pool, s["mid"], i + 3)
                    nc.gpsimd.tensor_tensor(parts[:, 2, :, :], res[:], parts[:, 1, :, :],
                                            ALU.subtract).then_inc(s["lo"], 1)
                steps(body)(pool)

            @block.vector
            def _(dve):
                for p in range(2):
                    nc.vector.memset(v_aug[p][:], 1.0).then_inc(s["ones"], 1)
                    nc.vector.memset(k_st[p][SPLIT:SPLIT + 3, :, :], 1.0).then_inc(s["ones"], 1)

                def row_max(i, u):
                    b, half, c = u // 4, u // 2 % 2, u % 2
                    wait(dve, s["scores"], 8 * i + u + 1)
                    if u == 0:
                        wait(dve, s["max_turned"], i)
                    out = neg_max[:].rearrange("p (h b c) -> p h b c", b=2, c=2)[:, half * 4:half * 4 + 4, b, c]
                    nc.vector.tensor_reduce(out.rearrange("p (x y) -> p x y", x=2),
                                            S[0:TC, :, 0:2 * TB].rearrange("p x (y t) -> p x y t", y=2)[:, :, :, 0:NTOK],
                                            AX.X, ALU.max, negate=True).then_inc(s["row_max"], 1)

                def o_norm(i, b):
                    wait(dve, s["o_turned"], 2 * i + b + 1)
                    o = M1[0:TC, :].rearrange("p (h e) -> p h e", e=32)
                    nc.vector.reciprocal(rec[:], o[:, :, HD]).then_inc(s["recip"], 1)
                    wait(dve, s["recip"], 2 * i + b + 1)
                    wait(dve, s["oT_turned"], 2 * i + b)
                    nc.vector.tensor_tensor(o_n[:].rearrange("p c (h e) -> p (c h) e", e=HD), o[:, :, 0:HD],
                                            rec[:].unsqueeze(2).to_broadcast([TC, 16, HD]),
                                            ALU.mult).then_inc(s["o_norm"], 1)

                def body(i, p, front, maxima, back):
                    if front:
                        hp = g.h[0:TC, bass.ds((i + 2) * 4, 4), :]
                        for t in range(4):
                            bn = nc.vector.bn_stats(stats[:, t, :], g.h[0:TC, bass.ds((i + 2) * 4 + t, 1), :]
                                                    .rearrange("p o d -> p (o d)"))
                        bn.then_inc(s["stats"], 1)
                        wait_alone(dve, s["stats"], i + 3)
                        wait(dve, s["var_eps"], i + 2)
                        for t in range(4):
                            bn = nc.vector.bn_aggr(mv[:, t, :], stats[:, t, :])
                        bn.then_inc(s["aggr"], 1)
                        wait(dve, s["aggr"], i + 3)
                        wait(dve, s["rstd"], i + 3)
                        wait(dve, s["turned"], i + 2)
                        for t in range(4):
                            x = nc.vector.tensor_scalar(xn[:, t, :], g.h[0:TC, bass.ds((i + 2) * 4 + t, 1), :]
                                                        .rearrange("p o d -> p (o d)"), mv[:, t, 0:1],
                                                        rstd[:, t:t + 1], ALU.subtract, ALU.mult)
                        x.then_inc(s["xn"], 1)
                    if maxima:
                        row_max(i + 1, 0)
                        row_max(i + 1, 1)
                    if front:
                        for qk, (m, bias) in enumerate(((M1, g.bq), (M2, g.bk))):
                            wait(dve, s["hi"], 2 * (i + 2) + qk + 1)
                            wait(dve, s["lo"], i + 2)
                            nc.vector.scalar_tensor_tensor(out=res[:, qk, :], in0=m[:, 0:PW], scalar=bias,
                                                           in1=parts[:, 0, qk, :], op0=ALU.add,
                                                           op1=ALU.subtract).then_inc(s["res"], 1)
                    if maxima:
                        row_max(i + 1, 2)
                        row_max(i + 1, 3)
                    if back:
                        o_norm(i, 0)
                    if maxima:
                        for u in range(4, 8):
                            row_max(i + 1, u)
                        n = 4 * (i + 1)
                        wait(dve, s["max_turned"], i + 2)
                        wait(dve, s["max_rd"], 48 * (i + 1))
                        m = M0[0:32, 0:TC]
                        nc.vector.tensor_copy(max_parts[:, 0, :], m).then_inc(s["max_parts"], 1)
                        wait(dve, s["max_parts"], n + 1)
                        nc.vector.tensor_tensor(max_res[:], m, max_parts[:, 0, :], ALU.subtract).then_inc(s["max_parts"], 1)
                        wait(dve, s["max_parts"], n + 2)
                        nc.vector.tensor_copy(max_parts[:, 1, :], max_res[:]).then_inc(s["max_parts"], 1)
                        wait(dve, s["max_parts"], n + 3)
                        nc.vector.tensor_tensor(max_parts[:, 2, :], max_res[:], max_parts[:, 1, :],
                                                ALU.subtract).then_inc(s["max_parts"], 1)
                    if back:
                        o_norm(i, 1)
                    if front:
                        wait(dve, s["v"], i + 3)
                        wait(dve, s["pv"], 4 * (i + 1) + 1)
                        wait(dve, s["ones"], 4)
                        nc.vector.tensor_tensor(v_aug[p][:, :, :, 0:HD],
                                                M0[0:TC, :].rearrange("p (t h e) -> p t h e", t=4, e=HD),
                                                g.bv.rearrange("p (h e) -> p h e", e=HD).unsqueeze(1)
                                                .to_broadcast([TC, 4, HEADS, HD]), ALU.add).then_inc(s["v_aug"], 1)
                    if back:
                        wait(dve, s["proj"], i + 1)
                        wait(dve, s["h_bias"], i + 1)
                        hp = g.h[0:TC, bass.ds(i * 4, 4), :]
                        nc.vector.tensor_tensor(hp, M1[0:TC, :].rearrange("p (t d) -> p t d", t=4), hp,
                                                ALU.add).then_inc(s["h_done"], 1)
                steps(body)(dve)
        s.clear()


def mlp_phase(nc, g):
    with ExitStack() as ctx:
        s = Sems(nc, ctx, "m_stats m_aggr m_ve m_rstd m_xn m_turned m_yT m_fc1 m_gelu m_fc2 m_bias m_h")

        def sb(name, shape, dt=F32):
            return ctx.enter_context(nc.sbuf_tensor("m_" + name, shape, dt))

        stats, mv, ve, rstd = sb("stats", [TC, 4, 6]), sb("mv", [TC, 4, 2]), sb("ve", [TC, 4]), sb("rstd", [TC, 4])
        xn = [sb(f"xn{p}", [TC, 4, D]) for p in range(2)]
        yT = [sb(f"yT{p}", [D, PW]) for p in range(2)]
        gl = [sb(f"gelu{p}", [128, 2, PW]) for p in range(2)]
        Y = [ctx.enter_context(nc.psum_tensor(f"m_Y{p}", [128, 512], F32)) for p in range(2)]
        H = [[ctx.enter_context(nc.psum_tensor(f"m_H{p}{k}", [128, 512], F32)) for k in range(2)] for p in range(2)]
        Z = [ctx.enter_context(nc.psum_tensor(f"m_Z{p}", [128, 512], F32)) for p in range(2)]

        def steps(eng, body):
            for i in (-2, -1):
                body(i, i % 2, True, i + 1 >= 0, False)
            with eng.Fori(0, PAIRS // 2 - 1) as j:
                for p in range(2):
                    body(j * 2 + p, p, True, True, True)
            for i in (PAIRS - 2, PAIRS - 1):
                body(i, i % 2, False, i + 1 < PAIRS, True)

        with nc.Block() as block:
            @block.tensor
            def _(pe):
                def body(i, p, front, middle, back):
                    q = 1 - p
                    if middle:
                        wait(pe, s["m_yT"], i + 2)
                        wait(pe, s["m_gelu"], 2 * i)
                        for k in range(2):
                            nc.tensor.matmul(H[q][k][:, 0:PW], g.w1[:, k * 128:(k + 1) * 128], yT[q][:],
                                             start=True, stop=True).then_inc(s["m_fc1"], 1)
                    if back:
                        wait(pe, s["m_gelu"], 2 * (i + 1))
                        wait(pe, s["m_h"], i)
                        for t in range(4):
                            for k in range(2):
                                mm = nc.tensor.matmul(Z[p][0:TC, t * D:(t + 1) * D], gl[p][:, k, t * TC:(t + 1) * TC],
                                                      g.w2[:, k * D:(k + 1) * D], start=(k == 0), stop=(k == 1))
                        mm.then_inc(s["m_fc2"], 1)
                    if front:
                        wait(pe, s["m_xn"], i + 3)
                        wait(pe, s["m_yT"], i + 1)
                        for t in range(4):
                            mm = nc.tensor.transpose(Y[p][:, t * TC:(t + 1) * TC], xn[p][:, t, :], g.ident[0:TC, 0:TC])
                        mm.then_inc(s["m_turned"], 1)
                steps(pe, body)

            @block.scalar
            def _(act):
                def body(i, p, front, middle, back):
                    q = 1 - p
                    if middle:
                        for k in range(2):
                            wait(act, s["m_fc1"], 2 * (i + 1) + k + 1)
                            wait(act, s["m_fc2"], i)
                            nc.scalar.activation(gl[q][:, k, :], H[q][k][:, 0:PW], ACT.Gelu,
                                                 bias=g.b1[:, k:k + 1]).then_inc(s["m_gelu"], 1)
                    if front:
                        wait(act, s["m_turned"], i + 3)
                        wait(act, s["m_fc1"], 2 * (i + 1))
                        nc.scalar.activation(yT[p][:], Y[p][:, 0:PW], ACT.Identity, bias=g.ln2_b,
                                             scale=g.ln2_w).then_inc(s["m_yT"], 1)
                steps(act, body)

            @block.gpsimd
            def _(pool):
                def body(i, p, front, middle, back):
                    if not front:
                        return
                    wait_alone(pool, s["m_aggr"], i + 3)
                    nc.gpsimd.tensor_scalar(ve[:], mv[:, :, 1], EPS, None, ALU.add).then_inc(s["m_ve"], 1)
                    wait(pool, s["m_ve"], i + 3)
                    wait(pool, s["m_xn"], i + 2)
                    nc.gpsimd.tensor_tensor(rstd[:], ve[:], g.neg_half[0:TC, 0:1].to_broadcast([TC, 4]),
                                            ALU.pow).then_inc(s["m_rstd"], 1)
                    wait(pool, s["m_xn"], i + 3)
                    hp = g.h[0:TC, bass.ds((i + 2) * 4, 4), :]
                    nc.gpsimd.tensor_tensor(hp, hp, g.b2.unsqueeze(1).to_broadcast([TC, 4, D]),
                                            ALU.add).then_inc(s["m_bias"], 1)
                steps(pool, body)

            @block.vector
            def _(dve):
                def body(i, p, front, middle, back):
                    if front:
                        for t in range(4):
                            bn = nc.vector.bn_stats(stats[:, t, :], g.h[0:TC, bass.ds((i + 2) * 4 + t, 1), :]
                                                    .rearrange("p o d -> p (o d)"))
                        bn.then_inc(s["m_stats"], 1)
                        wait_alone(dve, s["m_stats"], i + 3)
                        wait(dve, s["m_ve"], i + 2)
                        for t in range(4):
                            bn = nc.vector.bn_aggr(mv[:, t, :], stats[:, t, :])
                        bn.then_inc(s["m_aggr"], 1)
                    if back:
                        wait(dve, s["m_fc2"], i + 1)
                        wait(dve, s["m_bias"], i + 1)
                        hp = g.h[0:TC, bass.ds(i * 4, 4), :]
                        nc.vector.tensor_tensor(hp, Z[p][0:TC, :].rearrange("p (t d) -> p t d", t=4), hp,
                                                ALU.add).then_inc(s["m_h"], 1)
                    if front:
                        wait(dve, s["m_aggr"], i + 3)
                        wait(dve, s["m_rstd"], i + 3)
                        wait(dve, s["m_turned"], i + 1)
                        for t in range(4):
                            x = nc.vector.tensor_scalar(xn[p][:, t, :], g.h[0:TC, bass.ds((i + 2) * 4 + t, 1), :]
                                                        .rearrange("p o d -> p (o d)"), mv[:, t, 0:1],
                                                        rstd[:, t:t + 1], ALU.subtract, ALU.mult)
                        x.then_inc(s["m_xn"], 1)
                steps(dve, body)
        s.clear()


def vit(nc, g, A, ctx):
    g.ident = ctx.enter_context(nc.sbuf_tensor("ident", [128, 128], F32))
    g.neg_half = ctx.enter_context(nc.sbuf_tensor("neg_half", [128, 1], F32))
    g.h = ctx.enter_context(nc.sbuf_tensor("h", [128, 2 * B, D], F32))
    load_constants(nc, g, A)
    patch_phase(nc, g, A)
    with ExitStack() as vctx:
        g.w = vctx.enter_context(nc.sbuf_tensor("layer_w", [128, 8 * D], F32))
        g.cols = vctx.enter_context(nc.sbuf_tensor("layer_cols", [128, 8], F32))
        g.rows = vctx.enter_context(nc.sbuf_tensor("layer_rows", [TC, 3 * D], F32))
        g.wq, g.wk, g.wv, g.wp = (g.w[:, n * D:(n + 1) * D] for n in range(4))
        g.w1, g.w2 = g.w[:, 4 * D:6 * D], g.w[:, 6 * D:8 * D]
        g.ln1_w, g.ln1_b, g.bq, g.bk, g.ln2_w, g.ln2_b = (g.cols[:, n:n + 1] for n in range(6))
        g.b1 = g.cols[:, 6:8]
        g.bv, g.bp, g.b2 = (g.rows[:, n * D:(n + 1) * D] for n in range(3))
        with nc.Fori(0, DEPTH) as layer:
            load_layer(nc, g, A, layer)
            attention_phase(nc, g)
            mlp_phase(nc, g)


def lay_out(np, x, p):
    f = {k: np.asarray(v) for k, v in p.items()}
    xp = np.asarray(x).reshape(B, 3, 14, 16, 14, 16).transpose(0, 1, 3, 5, 2, 4).reshape(B, KC, 128, 196)
    X = np.zeros((B, 128, KC, TB), np.float32)
    X[:, :, :, 1:NTOK] = xp.transpose(0, 2, 1, 3)

    def chunks(rows):
        out = np.zeros((TB, D), np.float32)
        out[0:NTOK] = rows
        return np.ascontiguousarray(out.reshape(2, TC, D).transpose(1, 0, 2))

    rows = np.concatenate([f["cls_token"].reshape(1, D), np.repeat(f["conv_b"][None], NTOK - 1, 0)])
    w2 = f["fc2_w"].reshape(DEPTH, 2, 128, D).transpose(0, 2, 1, 3).reshape(DEPTH, 128, 2 * D)
    cols = [f["ln1_w"], f["ln1_b"], f["qkv_b"][:, 0:D], f["qkv_b"][:, D:2 * D], f["ln2_w"], f["ln2_b"],
            f["fc1_b"][:, 0:128], f["fc1_b"][:, 128:256]]
    rws = np.concatenate([f["qkv_b"][:, 2 * D:], f["proj_b"], f["fc2_b"]], 1)
    return {
        "x": X,
        "conv_w": np.ascontiguousarray(f["conv_w"].reshape(KC, 128, D).transpose(1, 0, 2)),
        "pos": chunks(f["pos_embed"][0]), "row_bias": chunks(rows),
        "weights": np.ascontiguousarray(np.concatenate([f["qkv_w"], f["proj_w"], f["fc1_w"], w2], 2)),
        "cols": np.ascontiguousarray(np.stack(cols, 2)),
        "rows": np.ascontiguousarray(np.repeat(rws[:, None, :], TC, 1)),
        "norm": np.repeat(np.stack([f["norm_w"], f["norm_b"]])[None], TC, 0),
        "ident": np.eye(128, dtype=np.float32),
    }


TL = 115
WL = 2 * L


def run_pairs(eng, body, depth):
    def step(i):
        body(i, i % 2, lambda k: 0 <= i + k < PAIRS)

    loops = (PAIRS - depth) // 2
    for i in range(-depth, 0):
        step(i)
    with eng.Fori(0, loops) as j:
        for p in range(2):
            body(j * 2 + p, p, lambda k: True)
    for i in range(2 * loops, PAIRS):
        step(i)


def fuse_phase(nc, g, A):
    with ExitStack() as ctx:
        s = Sems(nc, ctx, "f_load f_set f_diag f_txt0 f_txt1 f_stats f_aggr f_ve f_rstd f_xn f_xw f_y f_out0 f_out1 "
                 "f_stats2 f_aggr2 f_ve2 f_rstd2 f_z f_turned f_zT f_conv f_xc f_up f_gelu f_down f_tanh f_sum")

        def sb(name, shape, dt=F32):
            return ctx.enter_context(nc.sbuf_tensor("f_" + name, shape, dt))

        taps, gate_w = sb("taps", [D, 5]), sb("gate_w", [D, 4, D])
        diag, norm = sb("diag", [D, 4, D]), sb("norm", [TC, 2, D])
        stats, mv, ve, rstd = sb("stats", [TC, 4, 6]), sb("mv", [TC, 4, 2]), sb("ve", [TC, 4]), sb("rstd", [TC, 4])
        stats2, mv2, ve2, rstd2 = sb("stats2", [TC, 5, 6]), sb("mv2", [TC, 5, 2]), sb("ve2", [TC, 5]), sb("rstd2", [TC, 5])
        y = [sb(f"y{p}", [TC, 5, D]) for p in range(2)]
        z = [sb(f"z{p}", [TC, 5, D]) for p in range(2)]
        zT = [sb(f"zT{p}", [D, 2, L + 3]) for p in range(2)]
        gel = [sb(f"gel{n}", [D, WL]) for n in range(2)]
        tan = [sb(f"tan{n}", [D, WL]) for n in range(2)]
        Tp, Cp = (ctx.enter_context(nc.psum_tensor(n, [128, 512], F32)) for n in ("f_T", "f_C"))
        Up = [ctx.enter_context(nc.psum_tensor(f"f_U{n}", [128, 512], F32)) for n in range(2)]
        Zp = [ctx.enter_context(nc.psum_tensor(f"f_Z{n}", [128, 512], F32)) for n in range(2)]
        txt_in, sent = [s["f_txt0"], s["f_txt1"]], [s["f_out0"], s["f_out1"]]

        with nc.Block() as block:
            @block.sync
            def _(sp):
                for dst, src in ((taps, "taps"), (gate_w, "gate_w"), (norm, "norm")):
                    sp.dma_start(dst[:], A[src]).then_inc(s["f_load"], 16)
                sp.dma_start(g.hcat[0:T, :].rearrange("(b l) d -> b l d", l=L)[:, NTOK:L, :],
                             A["txt"].rearrange("(b l) d -> b l d", l=TXT)).then_inc(s["f_load"], 16)

                sp.wait_ge(s["f_set"], 8)

                def body(i, p, live):
                    if live(3):
                        wait(sp, s["f_z"], i + 2)
                        sp.dma_start(y[1 - p][0:2 * TXT, 4, :],
                                     A["txt"][bass.ds((i + 3) * (2 * TXT), 2 * TXT), :]).then_inc(txt_in[1 - p], 16)
                        wait(sp, s["f_y"], i + 4)
                        for t in range(4):
                            n, row = TC - t % 2, (t // 2) * L + (t % 2) * TC
                            sp.dma_start(g.hcat[bass.ds((i + 3) * WL + row, n), :],
                                         y[1 - p][0:n, t, :]).then_inc(sent[1 - p], 16)
                run_pairs(sp, body, 3)
                for p in range(2):
                    sp.wait_ge(sent[p], 32 * PAIRS)
                sp.wait_ge(s["f_load"], 64)

            @block.tensor
            def _(pe):
                pe.wait_ge(s["f_load"], 64)
                pe.wait_ge(s["f_diag"], 4)

                def body(i, p, live):
                    q = 1 - p
                    if live(0):
                        for n in range(2):
                            if n == 0:
                                wait(pe, s["f_xc"], i + 1)
                            wait(pe, s["f_gelu"], 2 * i + n)
                            nc.tensor.matmul(Up[n][:, 0:WL], gate_w[:, 2 * n, :], g.xT[:, bass.ds(i * WL, WL)],
                                             start=True, stop=True).then_inc(s["f_up"], 1)
                    if live(2):
                        wait(pe, s["f_z"], i + 3)
                        wait(pe, s["f_zT"], i + 2)
                        for b in range(2):
                            at = b * NTOK
                            nc.tensor.transpose(Tp[:, at:at + TC], z[p][:, 2 * b, :], g.ident[0:TC, 0:TC])
                            nc.tensor.transpose(Tp[:, at + TC:at + NTOK], z[p][0:TC - 1, 2 * b + 1, :],
                                                g.ident[0:TC - 1, 0:TC - 1])
                        mm = nc.tensor.transpose(Tp[:, 2 * NTOK:WL], z[p][0:2 * TXT, 4, :], g.ident[0:2 * TXT, 0:2 * TXT])
                        mm.then_inc(s["f_turned"], 1)
                    if live(0):
                        wait(pe, s["f_gelu"], 2 * i + 1)
                        wait(pe, s["f_tanh"], 2 * i)
                        nc.tensor.matmul(Zp[0][:, 0:WL], gate_w[:, 1, :], gel[0][:], start=True, stop=False)
                        nc.tensor.matmul(Zp[0][:, 0:WL], g.ident[:], g.xT[:, bass.ds(i * WL, WL)],
                                         start=False, stop=True).then_inc(s["f_down"], 1)
                    if live(1):
                        wait(pe, s["f_zT"], i + 2)
                        wait(pe, s["f_xc"], i + 1)
                        for k in range(4):
                            mm = nc.tensor.matmul(Cp[:, 0:WL].rearrange("p (b l) -> p b l", b=2), diag[:, k, :],
                                                  zT[q][:, :, k:k + L], start=(k == 0), stop=(k == 3))
                        mm.then_inc(s["f_conv"], 1)
                    if live(0):
                        wait(pe, s["f_gelu"], 2 * i + 2)
                        wait(pe, s["f_tanh"], 2 * i + 1)
                        nc.tensor.matmul(Zp[1][:, 0:WL], gate_w[:, 3, :], gel[1][:], start=True, stop=False)
                        nc.tensor.matmul(Zp[1][:, 0:WL], g.ident[:], g.xT[:, bass.ds(i * WL, WL)],
                                         start=False, stop=True).then_inc(s["f_down"], 1)
                run_pairs(pe, body, 3)

            @block.scalar
            def _(act):
                act.wait_ge(s["f_load"], 64)
                act.wait_ge(s["f_set"], 8)

                def body(i, p, live):
                    q = 1 - p
                    if live(0):
                        for n in range(2):
                            wait(act, s["f_up"], 2 * i + n + 1)
                            wait(act, s["f_down"], 2 * i)
                            nc.scalar.activation(gel[n][:], Up[n][:, 0:WL], ACT.Gelu).then_inc(s["f_gelu"], 1)
                    if live(2):
                        wait(act, s["f_turned"], i + 3)
                        wait(act, s["f_conv"], i + 1)
                        nc.scalar.activation(zT[p][:, :, 3:3 + NTOK],
                                             Tp[:, 0:2 * NTOK].rearrange("p (b l) -> p b l", b=2), ACT.Copy)
                        nc.scalar.activation(zT[p][:, :, 3 + NTOK:],
                                             Tp[:, 2 * NTOK:WL].rearrange("p (b l) -> p b l", b=2),
                                             ACT.Copy).then_inc(s["f_zT"], 1)
                    if live(1):
                        wait_alone(act, s["f_conv"], i + 2)
                        nc.scalar.activation(g.xT[:, bass.ds((i + 1) * WL, WL)], Cp[:, 0:WL], ACT.Identity,
                                             bias=taps[:, 4:5]).then_inc(s["f_xc"], 1)
                    if live(0):
                        for n in range(2):
                            wait(act, s["f_down"], 2 * i + n + 1)
                            wait(act, s["f_sum"], 2 * i)
                            nc.scalar.activation(tan[n][:], Zp[n][:, 0:WL], ACT.Tanh, scale=0.5)\
                                .then_inc(s["f_tanh"], 1)
                run_pairs(act, body, 3)

            @block.gpsimd
            def _(pool):
                pool.wait_ge(s["f_load"], 64)
                pool.wait_ge(s["f_set"], 8)

                def body(i, p, live):
                    q = 1 - p
                    if live(3):
                        wait_alone(pool, s["f_aggr"], i + 4)
                        nc.gpsimd.tensor_scalar(ve[:], mv[:, :, 1], EPS, None, ALU.add).then_inc(s["f_ve"], 1)
                        wait(pool, s["f_ve"], i + 4)
                        wait(pool, s["f_xn"], i + 3)
                        nc.gpsimd.tensor_tensor(rstd[:], ve[:], g.neg_half[0:TC, 0:1].to_broadcast([TC, 4]),
                                                ALU.pow).then_inc(s["f_rstd"], 1)
                    if live(2):
                        wait_alone(pool, s["f_aggr2"], i + 3)
                        nc.gpsimd.tensor_scalar(ve2[:], mv2[:, :, 1], EPS, None, ALU.add).then_inc(s["f_ve2"], 1)
                        wait(pool, s["f_ve2"], i + 3)
                        wait(pool, s["f_z"], i + 2)
                        nc.gpsimd.tensor_tensor(rstd2[:], ve2[:], g.neg_half[0:TC, 0:1].to_broadcast([TC, 5]),
                                                ALU.pow).then_inc(s["f_rstd2"], 1)
                    if live(0):
                        wait(pool, s["f_sum"], 2 * i)
                        for n in range(2):
                            wait(pool, s["f_tanh"], 2 * i + n + 1)
                            nc.gpsimd.tensor_tensor(g.gate_sum[:, n, :], g.gate_sum[:, n, :], tan[n][:],
                                                    ALU.add).then_inc(s["f_sum"], 1)
                    if live(3):
                        wait(pool, s["f_xw"], i + 4)
                        nc.gpsimd.tensor_tensor(y[q][:, 0:4, :], y[q][:, 0:4, :],
                                                norm[:, 1, :].unsqueeze(1).to_broadcast([TC, 4, D]),
                                                ALU.add).then_inc(s["f_y"], 1)
                run_pairs(pool, body, 3)

            @block.vector
            def _(dve):
                nc.vector.memset(g.gate_sum[:], 0.0).then_inc(s["f_set"], 1)
                nc.vector.memset(mv2[:], 1.0).then_inc(s["f_set"], 1)
                for p in range(2):
                    nc.vector.memset(y[p][:, 4, :], 0.0).then_inc(s["f_set"], 1)
                    nc.vector.memset(z[p][:], 0.0).then_inc(s["f_set"], 1)
                    nc.vector.memset(zT[p][:, :, 0:3], 0.0).then_inc(s["f_set"], 1)
                dve.wait_ge(s["f_load"], 64)
                for k in range(4):
                    nc.vector.tensor_scalar(diag[:, k, :], g.ident[:], taps[:, k:k + 1], None,
                                            ALU.mult).then_inc(s["f_diag"], 1)
                dve.wait_ge(s["f_set"], 8)
                rows = [TC, TC - 1, TC, TC - 1, 2 * TXT]

                def body(i, p, live):
                    q = 1 - p
                    if live(3):
                        for t in range(4):
                            bn = nc.vector.bn_stats(stats[:, t, :], g.h[0:TC, bass.ds((i + 3) * 4 + t, 1), :]
                                                    .rearrange("p o d -> p (o d)"))
                        bn.then_inc(s["f_stats"], 1)
                        wait_alone(dve, s["f_stats"], i + 4)
                        wait(dve, s["f_ve"], i + 3)
                        for t in range(4):
                            bn = nc.vector.bn_aggr(mv[:, t, :], stats[:, t, :])
                        bn.then_inc(s["f_aggr"], 1)
                    if live(2):
                        wait(dve, s["f_y"], i + 3)
                        wait(dve, txt_in[p], (i + 2 - p) * 8 + 16)
                        for t, n in enumerate(rows):
                            bn = nc.vector.bn_stats(stats2[0:n, t, :], y[p][0:n, t, :])
                        bn.then_inc(s["f_stats2"], 1)
                        wait_alone(dve, s["f_stats2"], i + 3)
                        wait(dve, s["f_ve2"], i + 2)
                        for t, n in enumerate(rows):
                            bn = nc.vector.bn_aggr(mv2[0:n, t, :], stats2[0:n, t, :])
                        bn.then_inc(s["f_aggr2"], 1)
                    if live(3):
                        wait(dve, s["f_aggr"], i + 4)
                        wait(dve, s["f_rstd"], i + 4)
                        wait(dve, sent[q], 32 * (i + 1 - q) + 64)
                        for t in range(4):
                            x = nc.vector.tensor_scalar(y[q][:, t, :], g.h[0:TC, bass.ds((i + 3) * 4 + t, 1), :]
                                                        .rearrange("p o d -> p (o d)"), mv[:, t, 0:1],
                                                        rstd[:, t:t + 1], ALU.subtract, ALU.mult)
                        x.then_inc(s["f_xn"], 1)
                        wait(dve, s["f_xn"], i + 4)
                        nc.vector.tensor_tensor(y[q][:, 0:4, :], y[q][:, 0:4, :],
                                                norm[:, 0, :].unsqueeze(1).to_broadcast([TC, 4, D]),
                                                ALU.mult).then_inc(s["f_xw"], 1)
                    if live(2):
                        wait(dve, s["f_aggr2"], i + 3)
                        wait(dve, s["f_rstd2"], i + 3)
                        wait(dve, s["f_turned"], i + 1)
                        for t, n in enumerate(rows):
                            x = nc.vector.tensor_scalar(z[p][0:n, t, :], y[p][0:n, t, :], mv2[0:n, t, 0:1],
                                                        rstd2[0:n, t:t + 1], ALU.subtract, ALU.mult)
                        x.then_inc(s["f_z"], 1)
                run_pairs(dve, body, 3)
        s.clear()


def gate_phase(nc, g):
    with ExitStack() as ctx:
        s = Sems(nc, ctx, "g_sum g_set g_mean g_scan g_pair")

        def sb(name, shape, dt=F32):
            return ctx.enter_context(nc.sbuf_tensor("g_" + name, shape, dt))

        mean, zero, one_step = sb("mean", [128, 2, L]), sb("zero", [128, L]), sb("one", [128, 2, L])
        ones = sb("ones", [128, 128])
        Mp = [ctx.enter_context(nc.psum_tensor(f"g_M{n}", [128, 512], F32)) for n in range(2)]
        with nc.Block() as block:
            @block.tensor
            def _(pe):
                pe.wait_ge(s["g_set"], 5)
                for n in range(2):
                    for b in range(2):
                        mm = nc.tensor.matmul(Mp[n][:, 0:L], ones[:], g.gate_sum[:, n, b * L:(b + 1) * L],
                                              start=(b == 0), stop=(b == 1))
                    mm.then_inc(s["g_sum"], 1)

            @block.vector
            def _(dve):
                nc.vector.memset(ones[:], 1.0).then_inc(s["g_set"], 1)
                nc.vector.memset(zero[:], 0.0).then_inc(s["g_set"], 1)
                nc.vector.memset(g.minus[:], -1.0).then_inc(s["g_set"], 1)
                nc.vector.memset(g.decay[:, :, 0:1], 1.0).then_inc(s["g_set"], 1)
                nc.vector.memset(g.drift[:, :, 0:1], 0.0).then_inc(s["g_set"], 1)
                for n in range(2):
                    dve.wait_ge(s["g_sum"], n + 1)
                    nc.vector.tensor_scalar(mean[:, n, :], Mp[n][:, 0:L], 0.5 / (B * D), 0.5, ALU.mult,
                                            ALU.add).then_inc(s["g_mean"], 1)
                dve.wait_ge(s["g_mean"], 2)
                nc.vector.tensor_scalar(one_step[:, 0, :], mean[:, 0, :], 0.01, None, ALU.mult).then_inc(s["g_mean"], 1)
                dve.wait_ge(s["g_mean"], 3)
                nc.vector.tensor_tensor_scan(g.decay[:, 0, 1:L], mean[:, 1, 0:L - 1], zero[:, 0:L - 1], 1.0,
                                             ALU.mult, ALU.add).then_inc(s["g_scan"], 1)
                nc.vector.tensor_tensor_scan(g.drift[:, 0, 1:L], mean[:, 1, 0:L - 1], one_step[:, 0, 0:L - 1], 0.0,
                                             ALU.mult, ALU.add).then_inc(s["g_scan"], 1)
                dve.wait_ge(s["g_scan"], 2)
                for k in (g.decay, g.drift):
                    nc.vector.tensor_copy(k[:, 1, 1:L], k[:, 0, 1:L]).then_inc(s["g_pair"], 1)
                dve.wait_ge(s["g_pair"], 2)
        s.clear()


def memory_phase(nc, g, A):
    with ExitStack() as ctx:
        s = Sems(nc, ctx, "y_load y_set y_xc y_q y_sq y_max y_rinv y_qn y_qT y_q2 y_up y_gelu y_g2 y_down y_hc0 y_hc1 "
                 "y_pre y_h2 y_stats y_aggr y_ve y_rstd y_zn y_zout0 y_zout1 y_turned y_zs y_zst y_logit y_lg")

        def sb(name, shape, dt=F32):
            return ctx.enter_context(nc.sbuf_tensor("y_" + name, shape, dt))

        w = sb("w", [D, 3, D])
        router = sb("router", [D, 16])
        xc = [sb(f"xc{p}", [D, WL + 1]) for p in range(2)]
        junk, ss, rinv = sb("junk", [TL, 4, D]), sb("ss", [TL, 4]), sb("rinv", [TL, 4])
        ssm = sb("ssm", [TL, 4])
        qn = [sb(f"qn{p}", [TL, 4, D]) for p in range(2)]
        q_decay, q_drift = sb("q_decay", [D, WL]), sb("q_drift", [D, WL])
        gel = sb("gel", [D, WL])
        g_decay, g_drift = ([sb(f"{n}{p}", [D, WL + 1]) for p in range(2)] for n in ("g_decay", "g_drift"))
        hc = [sb(f"hc{p}", [TL, 4, D]) for p in range(2)]
        stats, mv, ve, rstd = sb("stats", [TL, 4, 6]), sb("mv", [TL, 4, 2]), sb("ve", [TL, 4]), sb("rstd", [TL, 4])
        zn = [sb(f"zn{p}", [TL, 4, D]) for p in range(2)]
        zs = [sb(f"zs{p}", [D, WL + 1]) for p in range(2)]
        Qp, QTp, Up, Op, ZTp, Lp = (ctx.enter_context(nc.psum_tensor("y_" + n, [128, 512], F32))
                                    for n in ("Q", "QT", "U", "O", "ZT", "L"))
        hc_in, sent = [s["y_hc0"], s["y_hc1"]], [s["y_zout0"], s["y_zout1"]]
        decay = g.decay[:].rearrange("p b l -> p (b l)")
        drift = g.drift[:].rearrange("p b l -> p (b l)")
        rows = [TL, TL - 1, TL, TL - 1]
        cols = [(t // 2) * L + (t % 2) * TL for t in range(4)]

        with nc.Block() as block:
            @block.sync
            def _(sp):
                sp.dma_start(w[:], A["memory_w"]).then_inc(s["y_load"], 16)
                sp.dma_start(router[:], A["router_w"]).then_inc(s["y_load"], 16)
                sp.wait_ge(s["y_set"], 12)

                def body(i, p, live):
                    q = 1 - p
                    if live(1):
                        wait(sp, s["y_h2"], i)
                        for t in range(4):
                            sp.dma_start(hc[q][0:rows[t], t, :], g.hcat[bass.ds((i + 1) * WL + cols[t], rows[t]), :])\
                                .then_inc(hc_in[q], 16)
                        wait(sp, s["y_zn"], i + 2)
                        for t in range(4):
                            sp.dma_start(g.table[bass.ds((i + 1) * WL + cols[t], rows[t]), 0:D],
                                         zn[q][0:rows[t], t, :]).then_inc(sent[q], 16)
                run_pairs(sp, body, 3)
                for p in range(2):
                    sp.wait_ge(sent[p], 32 * PAIRS)

            @block.tensor
            def _(pe):
                pe.wait_ge(s["y_load"], 32)

                def body(i, p, live):
                    q = 1 - p
                    if live(1):
                        wait(pe, s["y_g2"], 2 * (i + 2))
                        wait(pe, s["y_h2"], i + 1)
                        for t in range(4):
                            nc.tensor.matmul(Op[0:TL, t * D:(t + 1) * D], g_decay[q][:, cols[t]:cols[t] + TL],
                                             w[:, 2, :], start=True, stop=False)
                            mm = nc.tensor.matmul(Op[0:TL, t * D:(t + 1) * D], g_drift[q][:, cols[t]:cols[t] + TL],
                                                  g.minus[:], start=False, stop=True)
                        mm.then_inc(s["y_down"], 1)
                    if live(2):
                        wait(pe, s["y_qn"], i + 3)
                        wait(pe, s["y_q2"], 2 * (i + 2))
                        for t in range(4):
                            mm = nc.tensor.transpose(QTp[:, cols[t]:cols[t] + rows[t]], qn[p][0:rows[t], t, :],
                                                     g.ident[0:rows[t], 0:rows[t]])
                        mm.then_inc(s["y_qT"], 1)
                    if live(3):
                        wait(pe, s["y_xc"], i + 4)
                        wait(pe, s["y_qn"], i + 3)
                        for t in range(4):
                            mm = nc.tensor.matmul(Qp[0:TL, t * D:(t + 1) * D], xc[q][:, cols[t]:cols[t] + TL],
                                                  w[:, 0, :], start=True, stop=True)
                        mm.then_inc(s["y_q"], 1)
                    if live(0):
                        wait(pe, s["y_zs"], i + 1)
                        wait(pe, s["y_lg"], i)
                        for t in range(4):
                            mm = nc.tensor.matmul(Lp[0:TL, t * 16:(t + 1) * 16], zs[p][:, cols[t]:cols[t] + TL],
                                                  router[:], start=True, stop=True)
                        mm.then_inc(s["y_logit"], 1)
                    if live(2):
                        wait(pe, s["y_q2"], 2 * (i + 3))
                        wait(pe, s["y_gelu"], i + 2)
                        nc.tensor.matmul(Up[:, 0:WL], w[:, 1, :], q_decay[:], start=True, stop=False)
                        nc.tensor.matmul(Up[:, 0:WL], g.minus[:], q_drift[:], start=False,
                                         stop=True).then_inc(s["y_up"], 1)
                    if live(1):
                        wait(pe, s["y_zn"], i + 2)
                        wait(pe, s["y_zs"], i + 1)
                        for t in range(4):
                            mm = nc.tensor.transpose(ZTp[:, cols[t]:cols[t] + rows[t]], zn[q][0:rows[t], t, :],
                                                     g.ident[0:rows[t], 0:rows[t]])
                        mm.then_inc(s["y_turned"], 1)
                run_pairs(pe, body, 3)

            @block.scalar
            def _(act):
                act.wait_ge(s["y_set"], 12)

                def body(i, p, live):
                    q = 1 - p
                    if live(3):
                        wait(act, s["y_q"], i + 4)
                        wait(act, s["y_max"], i + 3)
                        for t in range(4):
                            a = nc.scalar.activation(junk[:, t, :], Qp[0:TL, t * D:(t + 1) * D], ACT.Square,
                                                     accum_out=ss[:, t:t + 1])
                        a.then_inc(s["y_sq"], 1)
                    if live(2):
                        wait(act, s["y_up"], i + 3)
                        wait(act, s["y_g2"], 2 * (i + 2))
                        nc.scalar.activation(gel[:], Up[:, 0:WL], ACT.Gelu).then_inc(s["y_gelu"], 1)
                    if live(1):
                        wait(act, s["y_turned"], i + 2)
                        wait(act, s["y_logit"], i)
                        wait(act, s["y_zst"], i)
                        nc.scalar.activation(zs[q][:, 0:WL], ZTp[:, 0:WL], ACT.Copy).then_inc(s["y_zs"], 1)
                run_pairs(act, body, 3)

            @block.gpsimd
            def _(pool):
                pool.wait_ge(s["y_set"], 12)

                def body(i, p, live):
                    q = 1 - p
                    if live(3):
                        wait(pool, s["y_q"], i + 2)
                        nc.gpsimd.tensor_copy(xc[q][:, 0:WL], g.xT[:, bass.ds((i + 3) * WL, WL)])\
                            .then_inc(s["y_xc"], 1)
                    if live(1):
                        wait(pool, hc_in[q], (i + 1 - q) * 32 + 64)
                        nc.gpsimd.tensor_tensor(hc[q][:], hc[q][:], qn[q][:], ALU.add).then_inc(s["y_pre"], 1)
                    if live(3):
                        wait_alone(pool, s["y_sq"], i + 4)
                        nc.gpsimd.tensor_scalar(ssm[:], ss[:], 1e-24, None, ALU.max).then_inc(s["y_max"], 1)
                        wait(pool, s["y_max"], i + 4)
                        wait(pool, s["y_qn"], i + 3)
                        nc.gpsimd.tensor_tensor(rinv[:], ssm[:], g.neg_half[0:TL, 0:1].to_broadcast([TL, 4]),
                                                ALU.pow).then_inc(s["y_rinv"], 1)
                    if live(1):
                        wait_alone(pool, s["y_aggr"], i + 2)
                        nc.gpsimd.tensor_scalar(ve[:], mv[:, :, 1], EPS, None, ALU.add).then_inc(s["y_ve"], 1)
                        wait(pool, s["y_ve"], i + 2)
                        wait(pool, s["y_zn"], i + 1)
                        nc.gpsimd.tensor_tensor(rstd[:], ve[:], g.neg_half[0:TL, 0:1].to_broadcast([TL, 4]),
                                                ALU.pow).then_inc(s["y_rstd"], 1)
                    if live(2):
                        wait(pool, s["y_gelu"], i + 3)
                        wait(pool, s["y_down"], i + 1)
                        nc.gpsimd.tensor_tensor(g_drift[p][:, 0:WL], gel[:], drift, ALU.mult).then_inc(s["y_g2"], 1)
                    if live(1):
                        wait(pool, s["y_zs"], i + 2)
                        nc.gpsimd.tensor_copy(g.xT[:, bass.ds((i + 1) * WL, WL)], zs[q][:, 0:WL])\
                            .then_inc(s["y_zst"], 1)
                run_pairs(pool, body, 3)

            @block.vector
            def _(dve):
                for p in range(2):
                    for t in (xc[p], g_decay[p], g_drift[p], zs[p]):
                        nc.vector.memset(t[:, WL:WL + 1], 0.0).then_inc(s["y_set"], 1)
                    nc.vector.memset(hc[p][:], 0.0).then_inc(s["y_set"], 1)
                    nc.vector.memset(zn[p][:], 0.0).then_inc(s["y_set"], 1)

                def body(i, p, live):
                    q = 1 - p
                    if live(1):
                        wait(dve, s["y_down"], i + 2)
                        wait(dve, s["y_pre"], i + 2)
                        h2 = g.h[0:TL, bass.ds((i + 1) * 4, 4), :]
                        nc.vector.tensor_tensor(h2, Op[0:TL, :].rearrange("p (t d) -> p t d", t=4), hc[q][:],
                                                ALU.add).then_inc(s["y_h2"], 1)
                        wait_alone(dve, s["y_h2"], i + 2)
                        for t in range(4):
                            bn = nc.vector.bn_stats(stats[:, t, :], g.h[0:TL, bass.ds((i + 1) * 4 + t, 1), :]
                                                    .rearrange("p o d -> p (o d)"))
                        bn.then_inc(s["y_stats"], 1)
                        wait_alone(dve, s["y_stats"], i + 2)
                        wait(dve, s["y_ve"], i + 1)
                        for t in range(4):
                            bn = nc.vector.bn_aggr(mv[:, t, :], stats[:, t, :])
                        bn.then_inc(s["y_aggr"], 1)
                    if live(2):
                        for k, (dst, c) in enumerate(((q_decay, decay), (q_drift, drift))):
                            if k == 0:
                                wait(dve, s["y_qT"], i + 3)
                                wait(dve, s["y_up"], i + 2)
                            nc.vector.tensor_tensor(dst[:], QTp[:, 0:WL], c, ALU.mult).then_inc(s["y_q2"], 1)
                    if live(1):
                        wait(dve, s["y_aggr"], i + 2)
                        wait(dve, s["y_rstd"], i + 2)
                        wait(dve, s["y_turned"], i)
                        wait(dve, sent[q], 32 * (i + 1 - q))
                        for t in range(4):
                            x = nc.vector.tensor_scalar(zn[q][:, t, :], g.h[0:TL, bass.ds((i + 1) * 4 + t, 1), :]
                                                        .rearrange("p o d -> p (o d)"), mv[:, t, 0:1],
                                                        rstd[:, t:t + 1], ALU.subtract, ALU.mult)
                        x.then_inc(s["y_zn"], 1)
                    if live(3):
                        wait(dve, s["y_rinv"], i + 4)
                        wait(dve, s["y_qT"], i + 2)
                        wait(dve, s["y_pre"], i + 2)
                        nc.vector.tensor_tensor(qn[q][:], Qp[0:TL, :].rearrange("p (t d) -> p t d", t=4),
                                                rinv[:].unsqueeze(2).to_broadcast([TL, 4, D]),
                                                ALU.mult).then_inc(s["y_qn"], 1)
                    if live(2):
                        wait(dve, s["y_gelu"], i + 3)
                        wait(dve, s["y_down"], i + 1)
                        nc.vector.tensor_tensor(g_decay[p][:, 0:WL], gel[:], decay, ALU.mult).then_inc(s["y_g2"], 1)
                    if live(0):
                        wait(dve, s["y_logit"], i + 1)
                        nc.vector.tensor_copy(g.logits[:, :, bass.ds(i * 2, 2), :],
                                              Lp[0:TL, 0:64].rearrange("p (b c e) -> p c b e", b=2, c=2)).then_inc(s["y_lg"], 1)
                run_pairs(dve, body, 3)
        s.clear()


E = 16
CAP = T // E
EH = 512
BLK = L
NBLK = T // BLK
TILES = 8
SLOTS = [min(TL, CAP - k * TL) for k in range(TILES)]
ROW = D + E


def router_phase(nc, g):
    QUADS = B // 4
    with ExitStack() as ctx:
        s = Sems(nc, ctx, "r_max r_sub r_exp r_sum r_inv r_prob r_turn r_copy r_out")

        def sb(name, shape, dt=F32):
            return ctx.enter_context(nc.sbuf_tensor("r_" + name, shape, dt))

        mx, total = sb("max", [TL, 2 * B]), sb("total", [TL, 2 * B])
        pT = sb("pT", [4 * E, QUADS, L])
        P = [ctx.enter_context(nc.psum_tensor(f"r_P{n}", [128, 512], F32)) for n in range(4)]
        by_chunk = g.logits
        lg = by_chunk[:].rearrange("p c b e -> p (c b) e")

        def wide(a):
            return a[:].unsqueeze(2).to_broadcast([TL, 2 * B, E])

        with nc.Block() as block:
            @block.sync
            def _(sp):
                sp.wait_ge(s["r_prob"], 1)
                for c in range(2):
                    n = TL - c
                    sp.dma_start(g.table[:, D:ROW].rearrange("(b l) e -> l b e", l=L)[c * TL:c * TL + n],
                                 by_chunk[0:n, c]).then_inc(s["r_out"], 16)
                sp.wait_ge(s["r_copy"], QUADS)
                for b in range(4):
                    sp.dma_start(g.by_expert.rearrange("e (q b l) -> b e q l", b=4, l=L)[b],
                                 pT[b * E:(b + 1) * E, :, :]).then_inc(s["r_out"], 16)
                sp.wait_ge(s["r_out"], 96)

            @block.vector
            def _(dve):
                nc.vector.tensor_reduce(mx[:], lg, AX.X, ALU.max).then_inc(s["r_max"], 1)
                dve.wait_ge(s["r_max"], 1)
                nc.vector.tensor_tensor(lg, lg, wide(mx), ALU.subtract).then_inc(s["r_sub"], 1)
                dve.wait_ge(s["r_exp"], 1)
                nc.vector.tensor_reduce(total[:], lg, AX.X, ALU.add).then_inc(s["r_sum"], 1)
                dve.wait_ge(s["r_sum"], 1)
                nc.vector.reciprocal(mx[:], total[:]).then_inc(s["r_inv"], 1)
                dve.wait_ge(s["r_inv"], 1)
                nc.vector.tensor_tensor(lg, lg, wide(mx), ALU.mult).then_inc(s["r_prob"], 1)
                for q in range(QUADS):
                    dve.wait_ge(s["r_turn"], q + 1)
                    nc.vector.tensor_copy(pT[:, q, :], P[q % 4][0:4 * E, 0:L]).then_inc(s["r_copy"], 1)

            @block.scalar
            def _(act):
                act.wait_ge(s["r_sub"], 1)
                nc.scalar.activation(lg, lg, ACT.Exp).then_inc(s["r_exp"], 1)

            @block.tensor
            def _(pe):
                pe.wait_ge(s["r_prob"], 1)
                for q in range(QUADS):
                    if q >= 4:
                        pe.wait_ge(s["r_copy"], q - 3)
                    for c in range(2):
                        n = TL - c
                        mm = nc.tensor.transpose(P[q % 4][0:4 * E, c * TL:c * TL + n],
                                                 by_chunk[0:n, c, 4 * q:4 * q + 4, :].rearrange("p b e -> p (b e)"), g.ident[0:n, 0:n])
                    mm.then_inc(s["r_turn"], 1)
        s.clear()


def choice_phase(nc, g, A):
    with ExitStack() as ctx:
        s = Sems(nc, ctx, "t_load t_set t_cand t_count t_total t_step t_thr t_bit t_gt t_tie t_pref t_off t_need "
                 "t_sel t_run t_runoff t_final t_save t_spread t_cmp t_blk t_row t_fetch0 t_fetch1 t_in0 t_in1 t_now t_idx")
        W = T // 8

        def sb(name, shape, dt=F32):
            return ctx.enter_context(nc.sbuf_tensor("t_" + name, shape, dt))

        prob, gt, tie, run, zero = (sb(n, [128, W]) for n in ("prob", "gt", "tie", "run", "zero"))
        same, ahead = sb("same", [128, 128]), sb("ahead", [128, 128])
        thr, bit, cand, step = (sb(n, [128, 1], I32) for n in ("thr", "bit", "cand", "step"))
        cnt, n_gt, n_tie, need, ends = sb("cnt", [128, 1]), sb("n_gt", [128, 1]), sb("n_tie", [128, 1]), sb("need", [128, 1]), sb("ends", [128, 8])
        slot, first_row = sb("slot", [TL, TILES]), sb("first_row", [TL, E])
        spread, cmp = sb("spread", [TL, E * NBLK]), sb("cmp", [TL, E * NBLK])
        blk, row = sb("blk", [TL, TILES, E]), sb("row", [TL, TILES, E], I32)
        fetched = [sb(f"fetched{p}", [TL, TILES, BLK]) for p in range(2)]
        inside = sb("inside", [TL, E * TILES])
        junk = sb("junk", [TL, 2, TILES, BLK])
        Tp = ctx.enter_context(nc.psum_tensor("t_T", [128, 4], F32))
        fetch, read = [s["t_fetch0"], s["t_fetch1"]], [s["t_in0"], s["t_in1"]]
        now = [sb(f"now{p}", [TL, TILES], I32) for p in range(2)]
        BITS = 30

        with nc.Block() as block:
            @block.sync
            def _(sp):
                sp.dma_start(prob[:], g.by_expert.rearrange("e (k n) -> (e k) n", k=8)).then_inc(s["t_load"], 16)
                for dst, src in ((same, "same_expert"), (ahead, "ahead"), (slot, "slot"), (first_row, "first_row")):
                    sp.dma_start(dst[:], A[src]).then_inc(s["t_load"], 16)
                sp.wait_ge(s["t_final"], 2)
                sp.dma_start(g.counts.rearrange("(p x) n -> p (x n)", x=8), run[:]).then_inc(s["t_save"], 16)
                sp.dma_start(g.ends.rearrange("o (p x) -> (o p) x", x=8), ends[:]).then_inc(s["t_save"], 16)
                sp.wait_ge(s["t_save"], 32)
                sp.dma_start(spread[:], g.ends.to_broadcast([TL, E * NBLK])).then_inc(s["t_spread"], 16)

            @block.tensor
            def _(pe):
                pe.wait_ge(s["t_load"], 80)
                with pe.Fori(0, BITS) as i:
                    pe.wait_ge(s["t_count"], i + 1)
                    pe.wait_ge(s["t_step"], i)
                    nc.tensor.matmul(Tp[:, 0:1], same[:], cnt[:], start=True, stop=True).then_inc(s["t_total"], 1)
                pe.wait_ge(s["t_step"], BITS)
                pe.wait_ge(s["t_pref"], 1)
                nc.tensor.matmul(Tp[:, 0:1], same[:], n_gt[:], start=True, stop=False)
                nc.tensor.matmul(Tp[:, 0:1], ahead[:], run[:, W - 1:W], start=False, stop=True).then_inc(s["t_off"], 1)
                pe.wait_ge(s["t_run"], 1)
                nc.tensor.matmul(Tp[:, 1:2], ahead[:], run[:, W - 1:W], start=True, stop=True).then_inc(s["t_runoff"], 1)

            @block.vector
            def _(dve):
                nc.vector.memset(thr[:], 0).then_inc(s["t_set"], 1)
                nc.vector.memset(bit[:], 1 << (BITS - 1)).then_inc(s["t_set"], 1)
                nc.vector.memset(zero[:], 0.0).then_inc(s["t_set"], 1)
                nc.vector.memset(g.token[:], 0).then_inc(s["t_set"], 1)
                dve.wait_ge(s["t_set"], 4)
                dve.wait_ge(s["t_load"], 80)
                with dve.Fori(0, BITS) as i:
                    dve.wait_ge(s["t_thr"], i)
                    dve.wait_ge(s["t_bit"], i)
                    nc.vector.tensor_tensor(cand[:], thr[:], bit[:], ALU.bitwise_or).then_inc(s["t_cand"], 1)
                    dve.wait_ge(s["t_cand"], i + 1)
                    dve.wait_ge(s["t_total"], i)
                    nc.vector.tensor_scalar(gt[:], prob[:], cand[:].bitcast(F32), None, ALU.is_ge, ALU.add,
                                            accum_out=cnt[:]).then_inc(s["t_count"], 1)
                    dve.wait_ge(s["t_total"], i + 1)
                    nc.vector.scalar_tensor_tensor(out=step[:], in0=Tp[:, 0:1], scalar=float(CAP), in1=bit[:],
                                                   op0=ALU.is_ge, op1=ALU.mult).then_inc(s["t_step"], 1)
                    dve.wait_ge(s["t_step"], i + 1)
                    nc.vector.tensor_tensor(thr[:], thr[:], step[:], ALU.bitwise_or).then_inc(s["t_thr"], 1)
                    nc.vector.tensor_single_scalar(bit[:], bit[:], 1, ALU.logical_shift_right).then_inc(s["t_bit"], 1)
                dve.wait_ge(s["t_thr"], BITS)
                at = thr[:].bitcast(F32)
                nc.vector.tensor_scalar(gt[:], prob[:], at, None, ALU.is_gt, ALU.add,
                                        accum_out=n_gt[:]).then_inc(s["t_gt"], 1)
                nc.vector.tensor_scalar(tie[:], prob[:], at, None, ALU.is_equal).then_inc(s["t_tie"], 1)
                dve.wait_ge(s["t_gt"], 1)
                dve.wait_ge(s["t_tie"], 1)
                nc.vector.tensor_tensor_scan(run[:], tie[:], zero[:], 0.0, ALU.add, ALU.add).then_inc(s["t_pref"], 1)
                dve.wait_ge(s["t_off"], 1)
                nc.vector.tensor_scalar(need[:], Tp[:, 0:1], -1.0, float(CAP), ALU.mult, ALU.add).then_inc(s["t_need"], 1)
                dve.wait_ge(s["t_need"], 1)
                dve.wait_ge(s["t_pref"], 1)
                nc.vector.scalar_tensor_tensor(out=tie[:], in0=run[:], scalar=need[:], in1=tie[:], op0=ALU.is_le,
                                               op1=ALU.mult).then_inc(s["t_sel"], 1)
                dve.wait_ge(s["t_sel"], 1)
                nc.vector.tensor_tensor_scan(run[:], gt[:], tie[:], 0.0, ALU.add, ALU.add).then_inc(s["t_run"], 1)
                dve.wait_ge(s["t_runoff"], 1)
                dve.wait_ge(s["t_run"], 1)
                nc.vector.tensor_copy(cnt[:], Tp[:, 1:2]).then_inc(s["t_sel"], 1)
                dve.wait_ge(s["t_sel"], 2)
                nc.vector.tensor_scalar(run[:], run[:], cnt[:], None, ALU.add).then_inc(s["t_final"], 1)
                dve.wait_ge(s["t_final"], 1)
                nc.vector.tensor_copy(ends[:], run[:, BLK - 1::BLK]).then_inc(s["t_final"], 1)
                dve.wait_ge(s["t_spread"], 16)
                for k in range(TILES):
                    if k:
                        dve.wait_ge(s["t_blk"], k)
                    nc.vector.tensor_scalar(cmp[:], spread[:], slot[:, k:k + 1], None, ALU.is_le).then_inc(s["t_cmp"], 1)
                    dve.wait_ge(s["t_cmp"], k + 1)
                    nc.vector.tensor_reduce(blk[:, k, :], cmp[:].rearrange("p (e n) -> p e n", e=E), AX.X,
                                            ALU.add).then_inc(s["t_blk"], 1)
                dve.wait_ge(s["t_blk"], TILES)
                nc.vector.tensor_tensor(row[:], blk[:], first_row[:].unsqueeze(1).to_broadcast([TL, TILES, E]),
                                        ALU.add).then_inc(s["t_row"], 1)
                with dve.Fori(0, E // 2) as j:
                    for p in range(2):
                        dve.wait_ge(fetch[p], (j + 1) * (16 * TILES))
                        for k, n in enumerate(SLOTS):
                            a = nc.vector.tensor_scalar(junk[0:n, p, k, :], fetched[p][0:n, k, :], slot[0:n, k:k + 1], None,
                                                        ALU.is_le, ALU.add,
                                                        accum_out=inside[0:n, bass.ds(j * (2 * TILES) + p * TILES + k, 1)])
                        a.then_inc(read[p], 1)
                for p in range(2):
                    dve.wait_ge(read[p], E // 2)
                for k, n in enumerate(SLOTS):
                    nc.vector.scalar_tensor_tensor(out=g.token[0:n, k, :], in0=blk[0:n, k, :], scalar=float(BLK),
                                                   in1=inside[0:n, k::TILES], op0=ALU.mult, op1=ALU.add)\
                        .then_inc(s["t_idx"], 1)

            @block.gpsimd
            def _(pool):
                pool.wait_ge(s["t_save"], 32)
                pool.wait_ge(s["t_row"], 1)
                with pool.Fori(0, E // 2) as j:
                    for p in range(2):
                        pool.wait_ge(read[p], j)
                        nc.gpsimd.tensor_copy(now[p][:], row[:, :, bass.ds(j * 2 + p, 1)]
                                              .rearrange("p k o -> p (k o)")).then_inc(s["t_now"], 1)
                        wait_alone(pool, s["t_now"], j * 2 + p + 1)
                        for k, n in enumerate(SLOTS):
                            nc.gpsimd.indirect_dma_start(
                                out=fetched[p][0:n, k, :], out_offset=None, in_=g.counts[:, :],
                                in_offset=bass.IndirectOffsetOnAxis(now[p][0:n, k:k + 1].bitcast(U32), 0))\
                                .then_inc(fetch[p], 16)
        s.clear()


def shared_phase(nc, g, A, out):
    with ExitStack() as ctx:
        s = Sems(nc, ctx, "h_load h_set h_up h_gelu h_down0 h_down1 h_bias h_sum0 h_sum1 h_out0 h_out1")

        def sb(name, shape, dt=F32):
            return ctx.enter_context(nc.sbuf_tensor("h_" + name, shape, dt))

        w1, w2, b1, b2 = sb("w1", [D, EH]), sb("w2", [128, 4, D]), sb("b1", [128, 4]), sb("b2", [TL, D])
        gel = [sb(f"gel{p}", [128, 4, WL + 1]) for p in range(2)]
        y = [sb(f"y{p}", [TL, 4, D]) for p in range(2)]
        Up = [ctx.enter_context(nc.psum_tensor(f"h_U{n}", [128, 512], F32)) for n in range(4)]
        Op = [ctx.enter_context(nc.psum_tensor(f"h_O{p}", [128, 512], F32)) for p in range(2)]
        rows = [TL, TL - 1, TL, TL - 1]
        cols = [(t // 2) * L + (t % 2) * TL for t in range(4)]
        summed, sent = [s["h_sum0"], s["h_sum1"]], [s["h_out0"], s["h_out1"]]
        down = [s["h_down0"], s["h_down1"]]

        with nc.Block() as block:
            @block.sync
            def _(sp):
                for dst, src in ((w1, "sw1"), (w2, "sw2"), (b1, "sb1"), (b2, "sb2")):
                    sp.dma_start(dst[:], A[src]).then_inc(s["h_load"], 16)
                with sp.Fori(0, PAIRS // 2) as j:
                    for p in range(2):
                        sp.wait_ge(summed[p], j + 1)
                        for t in range(4):
                            sp.dma_start(out[bass.ds(j * (2 * WL) + p * WL + cols[t], rows[t]), :],
                                         y[p][0:rows[t], t, :]).then_inc(sent[p], 16)
                for p in range(2):
                    sp.wait_ge(sent[p], 32 * PAIRS)

            @block.tensor
            def _(pe):
                pe.wait_ge(s["h_load"], 64)
                pe.wait_ge(s["h_set"], 2)

                def body(i, p, j, first, second):
                    if first:
                        for k in range(4):
                            wait(pe, s["h_gelu"], 4 * i + k + 1)
                            nc.tensor.matmul(Up[k][:, 0:WL], w1[:, k * 128:(k + 1) * 128],
                                             g.xT[:, bass.ds((i + 1) * WL, WL)], start=True,
                                             stop=True).then_inc(s["h_up"], 1)
                    if second:
                        wait(pe, s["h_gelu"], 4 * (i + 1))
                        wait(pe, summed[p], j)
                        for t in range(4):
                            for k in range(4):
                                mm = nc.tensor.matmul(Op[p][0:TL, t * D:(t + 1) * D], gel[p][:, k, cols[t]:cols[t] + TL],
                                                      w2[:, k, :], start=(k == 0), stop=(k == 3))
                        mm.then_inc(down[p], 1)
                body(-1, 1, 0, True, False)
                with pe.Fori(0, PAIRS // 2 - 1) as j:
                    for p in range(2):
                        body(j * 2 + p, p, j, True, True)
                body(PAIRS - 2, 0, PAIRS // 2 - 1, True, True)
                body(PAIRS - 1, 1, PAIRS // 2 - 1, False, True)

            @block.scalar
            def _(act):
                act.wait_ge(s["h_load"], 64)
                with act.Fori(0, PAIRS // 2) as j:
                    for p in range(2):
                        i = j * 2 + p
                        for k in range(4):
                            act.wait_ge(s["h_up"], 4 * i + k + 1)
                            act.wait_ge(down[p], j)
                            nc.scalar.activation(gel[p][:, k, 0:WL], Up[k][:, 0:WL], ACT.Gelu_apprx_tanh,
                                                 bias=b1[:, k:k + 1]).then_inc(s["h_gelu"], 1)

            @block.gpsimd
            def _(pool):
                pool.wait_ge(s["h_load"], 64)
                with pool.Fori(0, PAIRS) as i:
                    h2 = g.h[0:TL, bass.ds(i * 4, 4), :]
                    nc.gpsimd.tensor_tensor(h2, h2, b2[:].unsqueeze(1).to_broadcast([TL, 4, D]),
                                            ALU.add).then_inc(s["h_bias"], 1)

            @block.vector
            def _(dve):
                for p in range(2):
                    nc.vector.memset(gel[p][:, :, WL:WL + 1], 0.0).then_inc(s["h_set"], 1)
                with dve.Fori(0, PAIRS // 2) as j:
                    for p in range(2):
                        i = j * 2 + p
                        dve.wait_ge(down[p], j + 1)
                        dve.wait_ge(s["h_bias"], i + 1)
                        dve.wait_ge(sent[p], j * 64)
                        nc.vector.tensor_tensor(y[p][:], Op[p][0:TL, :].rearrange("p (t d) -> p t d", t=4),
                                                g.h[0:TL, bass.ds(i * 4, 4), :], ALU.add).then_inc(summed[p], 1)
        s.clear()


def expert_phase(nc, g, A, out):
    with ExitStack() as ctx:
        s = Sems(nc, ctx, "e_load e_set e_w0 e_w1 e_in0 e_in1 e_turned e_xT e_up e_gelu e_down e_biased e_y e_now e_done0 e_done1")

        def sb(name, shape, dt=F32):
            return ctx.enter_context(nc.sbuf_tensor("e_" + name, shape, dt))

        w1 = [sb(f"w1{p}", [D, EH]) for p in range(2)]
        w2 = [sb(f"w2{p}", [128, 4, D]) for p in range(2)]
        b1, b2 = sb("b1", [128, E, 4]), sb("b2", [TL, E, D])
        x = [sb(f"x{p}", [TL, TILES, ROW]) for p in range(2)]
        xT = sb("xT", [D, TILES * TL])
        gel = sb("gel", [128, 4, TILES * TL])
        y = [sb(f"y{p}", [TL, TILES, D]) for p in range(2)]
        Xp = [ctx.enter_context(nc.psum_tensor(f"e_X{n}", [128, 512], F32)) for n in range(2)]
        Up = [ctx.enter_context(nc.psum_tensor(f"e_U{n}", [128, 512], F32)) for n in range(4)]
        Op = [ctx.enter_context(nc.psum_tensor(f"e_O{n}", [128, 512], F32)) for n in range(2)]
        w_in, x_in = [s["e_w0"], s["e_w1"]], [s["e_in0"], s["e_in1"]]
        HALF = CAP // 2
        done, now = [s["e_done0"], s["e_done1"]], [sb(f"now{p}", [TL, TILES], I32) for p in range(2)]

        with nc.Block() as block:
            @block.sync
            def _(sp):
                sp.dma_start(b1[:], A["eb1"]).then_inc(s["e_load"], 16)
                sp.dma_start(b2[:], A["eb2"]).then_inc(s["e_load"], 16)
                with sp.Fori(0, E // 2) as j:
                    for p in range(2):
                        sp.wait_ge(s["e_down"], 4 * j)
                        e = bass.ds(j * 2 + p, 1)
                        sp.dma_start(w1[p][:], A["ew1"][e].rearrange("o p n -> p (o n)")).then_inc(w_in[p], 16)
                        sp.dma_start(w2[p][:], A["ew2"][e].rearrange("o p k n -> p (o k) n")).then_inc(w_in[p], 16)

            @block.gpsimd
            def _(pool):
                pool.wait_ge(s["e_set"], 5)

                def gather(e, p):
                    wait(pool, s["e_y"], 2 * (e - 1))
                    wait(pool, done[p], (e - p) * (8 * TILES))
                    nc.gpsimd.tensor_copy(now[p][:], g.token[:, :, bass.ds(e, 1)].rearrange("p k o -> p (k o)"))\
                        .then_inc(s["e_now"], 1)
                    wait_alone(pool, s["e_now"], e + 1)
                    for k, n in enumerate(SLOTS):
                        nc.gpsimd.indirect_dma_start(
                            out=x[p][0:n, k, :], out_offset=None, in_=g.table[:, :],
                            in_offset=bass.IndirectOffsetOnAxis(now[p][0:n, k:k + 1].bitcast(U32), 0))\
                            .then_inc(x_in[p], 16)

                def scatter(e, p):
                    wait_alone(pool, s["e_y"], 2 * (e + 1))
                    wait(pool, done[1 - p], (e + p) * (8 * TILES))
                    for k, n in enumerate(SLOTS):
                        nc.gpsimd.indirect_dma_start(
                            out=out[:, :], out_offset=bass.IndirectOffsetOnAxis(now[p][0:n, k:k + 1].bitcast(U32), 0),
                            in_=y[p][0:n, k, :], in_offset=None, compute_op=ALU.add).then_inc(done[p], 16)

                gather(0, 0)
                with pool.Fori(0, E // 2 - 1) as j:
                    for p in range(2):
                        gather(j * 2 + p + 1, 1 - p)
                        scatter(j * 2 + p, p)
                gather(E - 1, 1)
                scatter(E - 2, 0)
                scatter(E - 1, 1)
                for p in range(2):
                    pool.wait_ge(done[p], E * 8 * TILES)

            @block.tensor
            def _(pe):
                pe.wait_ge(s["e_set"], 5)
                with pe.Fori(0, E // 2) as j:
                    for p in range(2):
                        e = j * 2 + p
                        pe.wait_ge(x_in[p], (j + 1) * (16 * TILES))
                        pe.wait_ge(s["e_xT"], 2 * e)
                        for k, n in enumerate(SLOTS):
                            mm = nc.tensor.transpose(Xp[k // 4][:, k % 4 * TL:k % 4 * TL + n], x[p][0:n, k, 0:D],
                                                     g.ident[0:n, 0:n])
                            if k % 4 == 3:
                                mm.then_inc(s["e_turned"], 1)
                        pe.wait_ge(s["e_xT"], 2 * e + 2)
                        pe.wait_ge(w_in[p], j * 32 + 32)
                        for k in range(4):
                            for m in range(2):
                                x8 = 2 * k + m
                                if x8 >= 4:
                                    pe.wait_ge(s["e_gelu"], 8 * e + x8 - 3)
                                else:
                                    pe.wait_ge(s["e_gelu"], 8 * e)
                                nc.tensor.matmul(Up[x8 % 4][:, 0:HALF], w1[p][:, k * 128:(k + 1) * 128],
                                                 xT[:, m * HALF:(m + 1) * HALF], start=True,
                                                 stop=True).then_inc(s["e_up"], 1)
                        pe.wait_ge(s["e_gelu"], 8 * e + 8)
                        for t in range(TILES):
                            if t % 4 == 0:
                                pe.wait_ge(s["e_biased"], 2 * e)
                            for k in range(4):
                                mm = nc.tensor.matmul(Op[t // 4][0:TL, t % 4 * D:(t % 4 + 1) * D],
                                                      gel[:, k, t * TL:(t + 1) * TL], w2[p][:, k, :],
                                                      start=(k == 0), stop=(k == 3))
                            if t % 4 == 3:
                                mm.then_inc(s["e_down"], 1)

            @block.scalar
            def _(act):
                act.wait_ge(s["e_load"], 32)
                act.wait_ge(s["e_set"], 5)
                with act.Fori(0, E // 2) as j:
                    for p in range(2):
                        e = j * 2 + p
                        for h in range(2):
                            act.wait_ge(s["e_turned"], 2 * e + h + 1)
                            act.wait_ge(s["e_up"], 8 * e)
                            n = 4 * TL if h == 0 else CAP - 4 * TL
                            nc.scalar.activation(xT[:, h * 4 * TL:h * 4 * TL + n], Xp[h][:, 0:n],
                                                 ACT.Copy).then_inc(s["e_xT"], 1)
                        for k in range(4):
                            for m in range(2):
                                x8 = 2 * k + m
                                wait_alone(act, s["e_up"], 8 * e + x8 + 1)
                                wait(act, s["e_down"], 2 * e)
                                nc.scalar.activation(gel[:, k, m * HALF:(m + 1) * HALF], Up[x8 % 4][:, 0:HALF],
                                                     ACT.Gelu_apprx_tanh, bias=b1[:, bass.ds(e, 1), k:k + 1]
                                                     .rearrange("p o k -> p (o k)")).then_inc(s["e_gelu"], 1)

            @block.vector
            def _(dve):
                for p in range(2):
                    nc.vector.memset(x[p][:, TILES - 1, :], 0.0).then_inc(s["e_set"], 1)
                    nc.vector.memset(y[p][:, TILES - 1, :], 0.0).then_inc(s["e_set"], 1)
                nc.vector.memset(gel[:, :, CAP:], 0.0).then_inc(s["e_set"], 1)
                dve.wait_ge(s["e_load"], 32)
                with dve.Fori(0, E // 2) as j:
                    for p in range(2):
                        e = j * 2 + p
                        dve.wait_ge(x_in[p], (j + 1) * (16 * TILES))
                        dve.wait_ge(done[p], j * (16 * TILES))
                        for h in range(2):
                            dve.wait_ge(s["e_down"], 2 * e + h + 1)
                            part = y[p][:, 4 * h:4 * h + 4, :]
                            nc.vector.tensor_tensor(part, Op[h][0:TL, :].rearrange("p (t d) -> p t d", t=4),
                                                    b2[:, bass.ds(e, 1), :].to_broadcast([TL, 4, D]),
                                                    ALU.add).then_inc(s["e_biased"], 1)
                            dve.wait_ge(s["e_biased"], 2 * e + h + 1)
                            nc.vector.tensor_tensor(part, part, x[p][:, 4 * h:4 * h + 4, bass.ds(e + D, 1)]
                                                    .to_broadcast([TL, 4, D]), ALU.mult).then_inc(s["e_y"], 1)
        s.clear()


def constants(np):
    p = np.arange(128)
    same = (p[:, None] // 8 == p[None, :] // 8).astype(np.float32)
    return {
        "same_expert": same, "ahead": same * (p[:, None] < p[None, :]).astype(np.float32),
        "slot": (np.arange(TILES)[None, :] * TL + np.arange(TL)[:, None]).astype(np.float32),
        "first_row": np.repeat((np.arange(E) * NBLK)[None].astype(np.float32), TL, 0),
    }


def lay_out_rest(np, txt, attn, ffn):
    a, f = ({k: np.asarray(v) for k, v in d.items()} for d in (attn, ffn))
    return {
        "txt": np.asarray(txt).reshape(B * TXT, D),
        "taps": np.ascontiguousarray(np.concatenate([a["conv_w"][:, 0, :], a["conv_b"][:, None]], 1)),
        "gate_w": np.ascontiguousarray(np.stack([a["eta_w1"], a["eta_w2"], a["alpha_w1"], a["alpha_w2"]], 1)),
        "memory_w": np.ascontiguousarray(np.stack([a["q_w"].T, a["mem_w1"], a["mem_w2"]], 1)),
        "router_w": f["gate_w"],
        "sw1": f["sw1"], "sw2": np.ascontiguousarray(f["sw2"].reshape(4, 128, D).transpose(1, 0, 2)),
        "sb1": np.ascontiguousarray(f["sb1"].reshape(4, 128).T), "sb2": np.repeat(f["sb2"][None], TL, 0),
        "ew1": f["w1"], "ew2": np.ascontiguousarray(f["w2"].reshape(E, 4, 128, D).transpose(0, 2, 1, 3)),
        "eb1": np.ascontiguousarray(f["b1"].reshape(E, 4, 128).transpose(2, 0, 1)),
        "eb2": np.ascontiguousarray(np.repeat(f["b2"][None], TL, 0)),
    }


def build(nc, A, out):
    with ExitStack() as ctx:
        g = Core()
        vit(nc, g, A, ctx)
        g.xT = ctx.enter_context(nc.sbuf_tensor("xT", [D, T], F32))
        g.logits = ctx.enter_context(nc.sbuf_tensor("logits", [TL, 2, B, E], F32))
        g.token = ctx.enter_context(nc.sbuf_tensor("token", [TL, TILES, E], I32))
        g.hcat = nc.dram_tensor("hcat", [T, D], F32).ap()
        g.table = nc.dram_tensor("table", [T, ROW], F32).ap()
        g.by_expert = nc.dram_tensor("by_expert", [E, T], F32).ap()
        g.counts = nc.dram_tensor("counts", [E * NBLK, BLK], F32).ap()
        g.ends = nc.dram_tensor("ends", [1, E * NBLK], F32).ap()
        with ExitStack() as mctx:
            g.gate_sum = mctx.enter_context(nc.sbuf_tensor("gate_sum", [D, 2, WL], F32))
            g.decay = mctx.enter_context(nc.sbuf_tensor("decay", [D, 2, L], F32))
            g.drift = mctx.enter_context(nc.sbuf_tensor("drift", [D, 2, L], F32))
            g.minus = mctx.enter_context(nc.sbuf_tensor("minus", [D, D], F32))
            fuse_phase(nc, g, A)
            gate_phase(nc, g)
            memory_phase(nc, g, A)
        router_phase(nc, g)
        choice_phase(nc, g, A)
        shared_phase(nc, g, A, out)
        expert_phase(nc, g, A, out)


def kernel(x, txt, **params):
    import numpy as np
    from concourse import bacc
    from concourse.bass_utils import run_bass_kernel_spmd

    def part(prefix):
        return {k.removeprefix(prefix): v for k, v in params.items() if k.startswith(prefix)}

    arrays = {**lay_out(np, x, part("L0_tok_")), **lay_out_rest(np, txt, part("L0_attn_"), part("L0_ffn_")),
              **constants(np)}
    nc = bacc.Bacc("TRN2", target_bir_lowering=False, num_devices=1)
    A = {k: nc.dram_tensor(f"in_{k}", v.shape, mybir.dt.from_np(v.dtype), kind="ExternalInput").ap()
         for k, v in arrays.items()}
    out = nc.dram_tensor("out", [T, D], F32, kind="ExternalOutput").ap()
    build(nc, A, out)
    r = run_bass_kernel_spmd(nc, [{f"in_{k}": v for k, v in arrays.items()}], core_ids=[0])
    return r.results[0]["out"].reshape(B, L, D)
```

```python
from contextlib import ExitStack

import concourse.bass as bass
from concourse import mybir

F32 = mybir.dt.float32
BF16 = mybir.dt.bfloat16
I32 = mybir.dt.int32
U32 = mybir.dt.uint32
ALU = mybir.AluOpType
ACT = mybir.ActivationFunctionType
AX = mybir.AxisListType

B, D, HEADS, HD = 64, 128, 8, 16
DEPTH, HID = 4, 256
NTOK = 197
TC = 99
TB = 2 * TC
PAIRS = B // 2
PW = 2 * TB
KC = 3 * 16 * 16 // 128
TXT = 32
L = NTOK + TXT
T = B * L
EPS = 1e-5
SPLIT = 6 * HD


def below(value, total):
    return min(value, total) if isinstance(value, int) else value


def wait(eng, sem, value):
    if isinstance(value, int) and value <= 0:
        return
    eng.wait_ge(sem, value)


def wait_alone(eng, sem, value):
    if not isinstance(value, int):
        with eng.register() as count:
            eng.reg_mov(count, value)
            eng.wait_ge(sem, 1)
            eng.wait_ge(sem, count)
    else:
        wait(eng, sem, value)


def loop(eng, n, step):
    step(0)
    with eng.Fori(1, n) as j:
        step(j)


def run_pairs(eng, body, depth):
    def step(i):
        body(i, i % 2, lambda k: 0 <= i + k < PAIRS)

    loops = (PAIRS - depth) // 2
    for i in range(-depth, 2):
        step(i)
    with eng.Fori(1, loops) as j:
        for p in range(2):
            body(j * 2 + p, p, lambda k: True)
    for i in range(2 * loops, PAIRS):
        step(i)


class Sems:

    def __init__(self, nc, ctx, names):
        self.nc, self.all = nc, {}
        for n in names.split():
            self.all[n] = ctx.enter_context(nc.semaphore(n))

    def __getitem__(self, name):
        return self.all[name]

    def clear(self):
        for s in self.all.values():
            self.nc.gpsimd.sem_clear(s)
        self.nc.all_engine_barrier()


class Core:
    pass


def load_constants(nc, g, A):
    with ExitStack() as ctx:
        s = Sems(nc, ctx, "c_load c_set")
        with nc.Block() as block:
            @block.sync
            def _(sp):
                sp.dma_start(g.ident[:], A["ident"]).then_inc(s["c_load"], 16)
                sp.wait_ge(s["c_load"], 16)

            @block.gpsimd
            def _(pool):
                nc.gpsimd.memset(g.neg_half[:], -0.5).then_inc(s["c_set"], 1)
                nc.gpsimd.memset(g.eps[:], EPS).then_inc(s["c_set"], 1)
        s.clear()


def patch_phase(nc, g, A):
    NB = 4
    with ExitStack() as ctx:
        s = Sems(nc, ctx, "p_const p_add " + " ".join(f"p_x{u} p_mm{u} p_h{u}" for u in range(NB)))
        xb = ctx.enter_context(nc.sbuf_tensor("xpatch", [128, NB, KC, TB], F32))
        wc = ctx.enter_context(nc.sbuf_tensor("conv_w", [128, KC, D], F32))
        posb = ctx.enter_context(nc.sbuf_tensor("pos", [TC, 2, D], F32))
        rowb = ctx.enter_context(nc.sbuf_tensor("rowb", [TC, 2, D], F32))
        ps = [ctx.enter_context(nc.psum_tensor(f"p_ps{i}", [128, 512], F32)) for i in range(NB)]
        x_loaded, x_used, sum_read = ([s[f"{n}{u}"] for u in range(NB)] for n in ("p_x", "p_mm", "p_h"))
        with nc.Block() as block:
            @block.sync
            def _(sp):
                sp.dma_start(wc[:], A["conv_w"]).then_inc(s["p_const"], 16)
                sp.dma_start(posb[:], A["pos"]).then_inc(s["p_const"], 16)
                sp.dma_start(rowb[:], A["row_bias"]).then_inc(s["p_const"], 16)
                def turn(j):
                    for u in range(NB):
                        wait(sp, x_used[u], j)
                        sp.dma_start(xb[:, u], A["x"][bass.ds(j * NB + u, 1)]
                                     .rearrange("o p k t -> p (o k) t")).then_inc(x_loaded[u], 16)
                loop(sp, B // NB, turn)

            @block.tensor
            def _(pe):
                pe.wait_ge(s["p_const"], 48)
                def turn(j):
                    for u in range(NB):
                        wait(pe, x_loaded[u], j * 16 + 16)
                        wait(pe, sum_read[u], j)
                        for c in range(2):
                            for k in range(KC):
                                mm = nc.tensor.matmul(ps[u][0:TC, c * D:(c + 1) * D],
                                                      xb[:, u, k, c * TC:(c + 1) * TC], wc[:, k, :],
                                                      start=(k == 0), stop=(k == KC - 1))
                        mm.then_inc(x_used[u], 1)
                loop(pe, B // NB, turn)

            @block.vector
            def _(dve):
                dve.wait_ge(s["p_const"], 48)
                nc.vector.tensor_tensor(posb[:], posb[:], rowb[:], ALU.add).then_inc(s["p_add"], 1)
                dve.wait_ge(s["p_add"], 1)
                def turn(j):
                    for u in range(NB):
                        wait(dve, x_used[u], j + 1)
                        nc.vector.tensor_tensor(
                            g.h[0:TC, bass.ds(j * (2 * NB) + 2 * u, 2), :],
                            ps[u][0:TC, 0:2 * D].rearrange("p (c d) -> p c d", c=2),
                            posb[:], ALU.add).then_inc(sum_read[u], 1)
                loop(dve, B // NB, turn)
        s.clear()


def load_layer(nc, g, A, layer):
    one = bass.ds(layer, 1)
    with ExitStack() as ctx:
        s = Sems(nc, ctx, "w_load w_scale")
        with nc.Block() as block:
            @block.sync
            def _(sp):
                sp.dma_start(g.w[:], A["weights"][one].rearrange("o p n -> p (o n)")).then_inc(s["w_load"], 16)
                sp.dma_start(g.cols[:], A["cols"][one].rearrange("o p n -> p (o n)")).then_inc(s["w_load"], 16)
                sp.dma_start(g.rows[:], A["rows"][one].rearrange("o p n -> p (o n)")).then_inc(s["w_load"], 16)
                sp.wait_ge(s["w_load"], 48)

            @block.vector
            def _(dve):
                dve.wait_ge(s["w_load"], 48)
                nc.vector.tensor_scalar(g.wq, g.wq, HD ** -0.5, None, ALU.mult).then_inc(s["w_scale"], 1)
                nc.vector.tensor_scalar(g.bq, g.bq, HD ** -0.5, None, ALU.mult).then_inc(s["w_scale"], 1)
                dve.wait_ge(s["w_scale"], 2)
        s.clear()


def attention_phase(nc, g):
    with ExitStack() as ctx:
        s = Sems(nc, ctx, "stats aggr var_eps rstd xn turned yT q_k v hi res mid lo v_aug "
                 "part_wr stack_rd max_rd scores row_max max_turned max_parts scores_t probs pv "
                 "o_copied o_turned recip o_norm oT_turned oT proj h_bias h_done ones")

        def sb(name, shape, dt=F32):
            return ctx.enter_context(nc.sbuf_tensor("a_" + name, shape, dt))

        stats, mv, ve, rstd = sb("stats", [TC, 4, 6]), sb("mv", [TC, 4, 2]), sb("ve", [TC, 4]), sb("rstd", [TC, 4])
        xn, yT = sb("xn", [TC, 4, D]), sb("yT", [D, PW])
        parts = sb("parts", [D, 3, 2, PW], BF16)
        res = sb("res", [D, 2, PW])
        q_st = [sb(f"q_st{p}", [SPLIT + 3, HEADS, PW], BF16) for p in range(4)]
        k_st = [sb(f"k_st{p}", [SPLIT + 3, HEADS, PW], BF16) for p in range(4)]
        v_aug = [sb(f"v_aug{p}", [TC, 4, HEADS, 32]) for p in range(4)]
        neg_max = sb("neg_max", [TC, 32])
        max_res, max_parts = sb("max_res", [32, TC]), sb("max_parts", [32, 3, TC], BF16)
        probs = sb("probs", [TC, 4, 4 * TB])
        o_sb, rec, o_n, oT = sb("o_sb", [D, 2 * TB]), sb("rec", [TC, 16]), sb("o_n", [TC, 2, D]), sb("oT", [D, PW])
        S = ctx.enter_context(nc.psum_tensor("a_S", [128, 2, 512], F32))
        St = ctx.enter_context(nc.psum_tensor("a_St", [128, 2, 512], F32))
        O, M0, M1, M2 = (ctx.enter_context(nc.psum_tensor(n, [128, 512], F32)) for n in ("a_O", "a_M0", "a_M1", "a_M2"))
        spill = [[nc.dram_tensor(f"spill_{n}{p}", [HEADS, 3 * HD, PW], BF16).ap() for p in range(2)] for n in "qk"]

        def steps(body):
            def step(i):
                body(i, i % 4, lambda k: 0 <= i + k < PAIRS)

            def run(eng):
                for i in range(-4, 4):
                    step(i)
                with eng.Fori(1, PAIRS // 4 - 1) as j:
                    for p in range(4):
                        body(j * 4 + p, p, lambda k: True)
                for i in range(PAIRS - 4, PAIRS + 1):
                    step(i)
            return run

        def upto(n, value):
            return below(value, n * PAIRS)

        with nc.Block() as block:
            @block.sync
            def _(sp):
                def body(i, p, live):
                    if live(1):
                        wait(sp, s["max_parts"], 4 * (i + 2))
                        for part in range(3):
                            sp.dma_start(q_st[(p + 1) % 4][SPLIT + part:SPLIT + part + 1, :, :]
                                         .rearrange("o h (x t) -> o (h x) t", t=TC),
                                         max_parts[:, part, :]).then_inc(s["max_rd"], 16)
                    if live(3):
                        for part, ready, n in ((0, s["hi"], 2), (1, s["mid"], 1), (2, s["lo"], 1)):
                            wait(sp, ready, n * (i + 4))
                            for qk in range(2):
                                to = 2 - part if qk == 0 else part
                                sp.dma_start(spill[qk][p % 2][:, to * HD:(to + 1) * HD, :],
                                             parts[:, part, qk, :]).then_inc(s["part_wr"], 16)
                        wait_alone(sp, s["part_wr"], 96 * (i + 4))
                        wait(sp, s["scores_t"], 8 * i)
                        for qk, st in ((1, k_st[(p + 3) % 4]), (0, q_st[(p + 3) % 4])):
                            for to, n in ((0, 3), (3, 2), (5, 1)):
                                at = 0 if qk == 1 else 3 - n
                                sp.dma_start(st[to * HD:(to + n) * HD, :, :],
                                             spill[qk][p % 2][:, at * HD:(at + n) * HD, :]
                                             .rearrange("h r t -> r h t")).then_inc(s["stack_rd"], 16)
                steps(body)(sp)
                sp.wait_ge(s["part_wr"], 96 * PAIRS)

            @block.tensor
            def _(pe):
                def scores(i, p, u):
                    b, half, c = u // 4, u // 2 % 2, u % 2
                    if u == 0:
                        wait(pe, s["stack_rd"], 96 * (i + 1))
                    wait(pe, s["row_max"], 8 * i + u)
                    for j in range(4):
                        head = half * 4 + j
                        mm = nc.tensor.matmul(S[0:TC, j // 2, j % 2 * TB:j % 2 * TB + NTOK],
                                              q_st[p][0:SPLIT, head, b * TB + c * TC:b * TB + (c + 1) * TC],
                                              k_st[p][0:SPLIT, head, b * TB:b * TB + NTOK], start=True, stop=True)
                    mm.then_inc(s["scores"], 1)

                def scores_t(i, p, u):
                    b, half, c = u // 4, u // 2 % 2, u % 2
                    keys = TC - c
                    if u == 0:
                        wait(pe, s["max_rd"], 48 * (i + 1))
                    wait(pe, s["probs"], 8 * i + u)
                    for j in range(4):
                        head = half * 4 + j
                        at = b * TB + c * TC
                        mm = nc.tensor.matmul(St[0:keys, j // 2, j % 2 * TB:(j % 2 + 1) * TB],
                                              k_st[p][:, head, at:at + keys],
                                              q_st[p][:, head, b * TB:(b + 1) * TB], start=True, stop=True)
                    mm.then_inc(s["scores_t"], 1)

                def pv(i, p, b, half):
                    if b == 0 and half == 0:
                        wait(pe, s["v_aug"], i + 1)
                    if half == 0:
                        wait(pe, s["o_copied"], 2 * i + b)
                    wait(pe, s["probs"], 8 * i + 4 * b + 2 * half + 2)
                    for j in range(4):
                        for c in range(2):
                            keys = TC - c
                            mm = nc.tensor.matmul(O[32 * j:32 * j + 32, half * TB:(half + 1) * TB],
                                                  v_aug[p][0:keys, 2 * b + c, half * 4 + j, :],
                                                  probs[0:keys, 2 * half + c, j * TB:(j + 1) * TB],
                                                  start=(c == 0), stop=(c == 1))
                    mm.then_inc(s["pv"], 1)

                def o_turn(i, b):
                    wait(pe, s["o_copied"], 2 * i + b + 1)
                    for c in range(2):
                        for half in range(2):
                            x = 2 * c + half
                            mm = nc.tensor.transpose(M1[0:TC, x * D:(x + 1) * D],
                                                     o_sb[:, half * TB + c * TC:half * TB + (c + 1) * TC],
                                                     g.ident[:])
                    mm.then_inc(s["o_turned"], 1)

                def oT_turn(i, b):
                    wait(pe, s["o_norm"], 2 * i + b + 1)
                    wait(pe, s["oT"], 2 * i + b)
                    for c in range(2):
                        at = b * TB + c * TC
                        mm = nc.tensor.transpose(M2[:, at:at + TC], o_n[:, c, :], g.ident[0:TC, 0:TC])
                    mm.then_inc(s["oT_turned"], 1)

                pe.sem_inc(s["pv"], 1)
                pe.wait_ge(s["ones"], 8)

                def body(i, p, live):
                    now, nxt, then, front, last = live(0), live(1), live(2), live(3), live(-1)
                    if now:
                        scores_t(i, p, 0)
                    if nxt:
                        scores(i + 1, (p + 1) % 4, 4)
                    if last:
                        pv(i - 1, (p - 1) % 4, 1, 1)
                    if front:
                        wait(pe, s["xn"], i + 4)
                        wait(pe, s["max_parts"], 4 * (i + 1))
                        for t in range(4):
                            mm = nc.tensor.transpose(M0[:, t * TC:(t + 1) * TC], xn[:, t, :], g.ident[0:TC, 0:TC])
                        mm.then_inc(s["turned"], 1)
                    if now:
                        scores_t(i, p, 1)
                    if nxt:
                        scores(i + 1, (p + 1) % 4, 5)
                    if last:
                        o_turn(i - 1, 1)
                    if now:
                        scores_t(i, p, 2)
                    if nxt:
                        scores(i + 1, (p + 1) % 4, 6)
                    if last:
                        oT_turn(i - 1, 1)
                    if now:
                        pv(i, p, 0, 0)
                    if front:
                        wait(pe, s["yT"], i + 4)
                        for t in range(4):
                            mm = nc.tensor.matmul(M0[0:TC, t * D:(t + 1) * D], yT[:, t * TC:(t + 1) * TC], g.wv,
                                                  start=True, stop=True)
                        mm.then_inc(s["v"], 1)
                    if now:
                        scores_t(i, p, 3)
                    if nxt:
                        scores(i + 1, (p + 1) % 4, 7)
                    if last:
                        wait(pe, s["oT"], 2 * i)
                        for t in range(4):
                            mm = nc.tensor.matmul(M1[0:TC, t * D:(t + 1) * D], oT[:, t * TC:(t + 1) * TC], g.wp,
                                                  start=True, stop=True)
                        mm.then_inc(s["proj"], 1)
                    if now:
                        scores_t(i, p, 4)
                    if nxt:
                        wait(pe, s["row_max"], 8 * (i + 2))
                        wait(pe, s["v_aug"], upto(1, i + 4))
                        nc.tensor.transpose(M0[0:32, 0:TC], neg_max[:], g.ident[0:TC, 0:TC]).then_inc(s["max_turned"], 1)
                    if then:
                        scores(i + 2, (p + 2) % 4, 0)
                    if now:
                        pv(i, p, 0, 1)
                        scores_t(i, p, 5)
                    if then:
                        scores(i + 2, (p + 2) % 4, 1)
                    if front:
                        wait(pe, s["h_done"], i)
                        nc.tensor.matmul(M1[:, 0:PW], g.wq, yT[:], start=True, stop=True).then_inc(s["q_k"], 1)
                        wait(pe, s["oT"], 2 * i)
                        nc.tensor.matmul(M2[:, 0:PW], g.wk, yT[:], start=True, stop=True).then_inc(s["q_k"], 1)
                    if now:
                        scores_t(i, p, 6)
                    if then:
                        scores(i + 2, (p + 2) % 4, 2)
                    if now:
                        pv(i, p, 1, 0)
                        wait(pe, s["res"], upto(2, 2 * (i + 4)))
                        wait(pe, s["h_done"], i)
                        o_turn(i, 0)
                        scores_t(i, p, 7)
                    if then:
                        scores(i + 2, (p + 2) % 4, 3)
                    if now:
                        oT_turn(i, 0)
                steps(body)(pe)

            @block.scalar
            def _(act):
                def exp(i, u):
                    keys = TC - u % 2
                    wait(act, s["scores_t"], 8 * i + u + 1)
                    wait(act, s["pv"], 4 * i + u // 2)
                    nc.scalar.activation(probs[0:keys, u % 4, :].rearrange("p (x t) -> p x t", x=2),
                                         St[0:keys, :, 0:2 * TB], ACT.Exp).then_inc(s["probs"], 1)

                def o_copy(i, b):
                    wait(act, s["pv"], 4 * i + 2 * b + 3)
                    wait(act, s["o_turned"], 2 * i + b)
                    nc.scalar.activation(o_sb[:], O[:, 0:2 * TB], ACT.Copy).then_inc(s["o_copied"], 1)

                def oT_copy(i, b):
                    wait(act, s["oT_turned"], 2 * i + b + 1)
                    wait(act, s["proj"], i)
                    nc.scalar.activation(oT[:, b * TB:(b + 1) * TB], M2[:, b * TB:(b + 1) * TB],
                                         ACT.Copy).then_inc(s["oT"], 1)

                def body(i, p, live):
                    now, front, last = live(0), live(3), live(-1)
                    if now:
                        exp(i, 0)
                    if last:
                        o_copy(i - 1, 1)
                    if front:
                        wait(act, s["turned"], i + 4)
                        wait(act, s["q_k"], 2 * (i + 3))
                        nc.scalar.activation(yT[:], M0[:, 0:PW], ACT.Identity, bias=g.ln1_b,
                                             scale=g.ln1_w).then_inc(s["yT"], 1)
                    if now:
                        exp(i, 1)
                        exp(i, 2)
                    if last:
                        oT_copy(i - 1, 1)
                    if now:
                        exp(i, 3)
                        exp(i, 4)
                        o_copy(i, 0)
                        exp(i, 5)
                    if front:
                        for qk, (m, bias) in enumerate(((M1, g.bq), (M2, g.bk))):
                            wait(act, s["q_k"], 2 * (i + 3) + qk + 1)
                            wait(act, s["part_wr"], 96 * (i + 3))
                            nc.scalar.activation(parts[:, 0, qk, :], m[:, 0:PW], ACT.Identity,
                                                 bias=bias).then_inc(s["hi"], 1)
                    if now:
                        exp(i, 6)
                    if front:
                        wait(act, s["res"], 2 * (i + 4))
                        nc.scalar.activation(parts[:, 1, :, :], res[:], ACT.Copy).then_inc(s["mid"], 1)
                    if now:
                        exp(i, 7)
                        oT_copy(i, 0)
                steps(body)(act)

            @block.gpsimd
            def _(pool):
                def body(i, p, live):
                    if live(4):
                        wait(pool, s["aggr"], i + 5)
                        nc.gpsimd.tensor_tensor(ve[:], mv[:, :, 1], g.eps[0:TC, 0:1].to_broadcast([TC, 4]),
                                                ALU.add).then_inc(s["var_eps"], 1)
                        wait(pool, s["var_eps"], i + 5)
                        wait(pool, s["xn"], i + 4)
                        nc.gpsimd.tensor_tensor(rstd[:], ve[:], g.neg_half[0:TC, 0:1].to_broadcast([TC, 4]),
                                                ALU.pow).then_inc(s["rstd"], 1)
                    if live(3):
                        wait(pool, s["mid"], i + 4)
                        nc.gpsimd.tensor_tensor(parts[:, 2, :, :], res[:], parts[:, 1, :, :],
                                                ALU.subtract).then_inc(s["lo"], 1)
                    if live(4):
                        wait(pool, s["xn"], i + 5)
                        hp = g.h[0:TC, bass.ds((i + 4) * 4, 4), :]
                        nc.gpsimd.tensor_tensor(hp, hp, g.bp.unsqueeze(1).to_broadcast([TC, 4, D]),
                                                ALU.add).then_inc(s["h_bias"], 1)
                steps(body)(pool)

            @block.vector
            def _(dve):
                for p in range(4):
                    nc.vector.memset(v_aug[p][:], 1.0).then_inc(s["ones"], 1)
                    nc.vector.memset(k_st[p][SPLIT:SPLIT + 3, :, :], 1.0).then_inc(s["ones"], 1)

                def row_max(i, u):
                    b, half, c = u // 4, u // 2 % 2, u % 2
                    wait(dve, s["scores"], 8 * i + u + 1)
                    if u == 0:
                        wait(dve, s["max_turned"], i)
                    out = neg_max[:].rearrange("p (h b c) -> p h b c", b=2, c=2)[:, half * 4:half * 4 + 4, b, c]
                    nc.vector.tensor_reduce(out.rearrange("p (x y) -> p x y", x=2),
                                            S[0:TC, :, 0:2 * TB].rearrange("p x (y t) -> p x y t", y=2)[:, :, :, 0:NTOK],
                                            AX.X, ALU.max, negate=True).then_inc(s["row_max"], 1)

                def o_norm(i, b):
                    wait(dve, s["o_turned"], 2 * i + b + 1)
                    o = M1[0:TC, :].rearrange("p (h e) -> p h e", e=32)
                    nc.vector.reciprocal(rec[:], o[:, :, HD]).then_inc(s["recip"], 1)
                    wait(dve, s["recip"], 2 * i + b + 1)
                    wait(dve, s["oT_turned"], 2 * i + b)
                    nc.vector.tensor_tensor(o_n[:].rearrange("p c (h e) -> p (c h) e", e=HD), o[:, :, 0:HD],
                                            rec[:].unsqueeze(2).to_broadcast([TC, 16, HD]),
                                            ALU.mult).then_inc(s["o_norm"], 1)

                def body(i, p, live):
                    now, nxt, then, front, last = live(0), live(1), live(2), live(3), live(-1)
                    if nxt:
                        row_max(i + 1, 4)
                        row_max(i + 1, 5)
                    if last:
                        o_norm(i - 1, 1)
                    if nxt:
                        row_max(i + 1, 6)
                    if front:
                        wait(dve, s["v"], i + 4)
                        wait(dve, s["ones"], 8)
                        nc.vector.tensor_tensor(v_aug[(p + 3) % 4][:, :, :, 0:HD],
                                                M0[0:TC, :].rearrange("p (t h e) -> p t h e", t=4, e=HD),
                                                g.bv.rearrange("p (h e) -> p h e", e=HD).unsqueeze(1)
                                                .to_broadcast([TC, 4, HEADS, HD]), ALU.add).then_inc(s["v_aug"], 1)
                    if nxt:
                        row_max(i + 1, 7)
                        n = 4 * (i + 1)
                        wait(dve, s["max_turned"], i + 2)
                        wait(dve, s["max_rd"], 48 * (i + 1))
                        m = M0[0:32, 0:TC]
                        nc.vector.tensor_copy(max_parts[:, 0, :], m).then_inc(s["max_parts"], 1)
                        wait(dve, s["max_parts"], n + 1)
                        nc.vector.tensor_tensor(max_res[:], m, max_parts[:, 0, :], ALU.subtract).then_inc(s["max_parts"], 1)
                        wait(dve, s["max_parts"], n + 2)
                        nc.vector.tensor_copy(max_parts[:, 1, :], max_res[:]).then_inc(s["max_parts"], 1)
                        wait(dve, s["max_parts"], n + 3)
                        nc.vector.tensor_tensor(max_parts[:, 2, :], max_res[:], max_parts[:, 1, :],
                                                ALU.subtract).then_inc(s["max_parts"], 1)
                    if last:
                        wait(dve, s["proj"], i)
                        wait(dve, s["h_bias"], i)
                        hp = g.h[0:TC, bass.ds((i - 1) * 4, 4), :]
                        nc.vector.tensor_tensor(hp, M1[0:TC, :].rearrange("p (t d) -> p t d", t=4), hp,
                                                ALU.add).then_inc(s["h_done"], 1)
                    if then:
                        row_max(i + 2, 0)
                    if live(4):
                        for t in range(4):
                            bn = nc.vector.bn_stats(stats[:, t, :], g.h[0:TC, bass.ds((i + 4) * 4 + t, 1), :]
                                                    .rearrange("p o d -> p (o d)"))
                        bn.then_inc(s["stats"], 1)
                        wait_alone(dve, s["stats"], i + 5)
                        wait(dve, s["var_eps"], i + 4)
                        for t in range(4):
                            bn = nc.vector.bn_aggr(mv[:, t, :], stats[:, t, :])
                        bn.then_inc(s["aggr"], 1)
                    if then:
                        row_max(i + 2, 1)
                    if front:
                        for qk, (m, bias) in enumerate(((M1, g.bq), (M2, g.bk))):
                            wait(dve, s["hi"], 2 * (i + 3) + qk + 1)
                            wait(dve, s["lo"], i + 3)
                            nc.vector.scalar_tensor_tensor(out=res[:, qk, :], in0=m[:, 0:PW], scalar=bias,
                                                           in1=parts[:, 0, qk, :], op0=ALU.add,
                                                           op1=ALU.subtract).then_inc(s["res"], 1)
                    if then:
                        row_max(i + 2, 2)
                    if now:
                        o_norm(i, 0)
                    if live(4):
                        wait(dve, s["aggr"], i + 5)
                        wait(dve, s["rstd"], i + 5)
                        wait(dve, s["turned"], i + 4)
                        for t in range(4):
                            x = nc.vector.tensor_scalar(xn[:, t, :], g.h[0:TC, bass.ds((i + 4) * 4 + t, 1), :]
                                                        .rearrange("p o d -> p (o d)"), mv[:, t, 0:1],
                                                        rstd[:, t:t + 1], ALU.subtract, ALU.mult)
                        x.then_inc(s["xn"], 1)
                    if then:
                        row_max(i + 2, 3)
                steps(body)(dve)
        s.clear()


def mlp_phase(nc, g):
    with ExitStack() as ctx:
        s = Sems(nc, ctx, "m_stats m_aggr m_ve m_rstd m_xn m_turned m_yT m_fc1 m_gelu m_fc2 m_bias m_h")

        def sb(name, shape, dt=F32):
            return ctx.enter_context(nc.sbuf_tensor("m_" + name, shape, dt))

        stats, mv, ve, rstd = ([sb(f"{n}{p}", [TC, 4, w]) for p in range(2)]
                               for n, w in (("stats", 6), ("mv", 2), ("ve", 1), ("rstd", 1)))
        xn = [sb(f"xn{p}", [TC, 4, D]) for p in range(2)]
        yT = [sb(f"yT{p}", [D, PW]) for p in range(2)]
        gl = [sb(f"gelu{p}", [128, 2, PW]) for p in range(2)]
        Y = [ctx.enter_context(nc.psum_tensor(f"m_Y{p}", [128, 512], F32)) for p in range(2)]
        H = [[ctx.enter_context(nc.psum_tensor(f"m_H{p}{k}", [128, 512], F32)) for k in range(2)] for p in range(2)]
        Z = [ctx.enter_context(nc.psum_tensor(f"m_Z{p}", [128, 512], F32)) for p in range(2)]

        with nc.Block() as block:
            @block.tensor
            def _(pe):
                def body(i, p, live):
                    q = 1 - p
                    if live(1):
                        wait(pe, s["m_yT"], i + 2)
                        wait(pe, s["m_gelu"], 2 * i)
                        for k in range(2):
                            nc.tensor.matmul(H[q][k][:, 0:PW], g.w1[:, k * 128:(k + 1) * 128], yT[q][:],
                                             start=True, stop=True).then_inc(s["m_fc1"], 1)
                    if live(0):
                        wait(pe, s["m_gelu"], 2 * (i + 1))
                        wait(pe, s["m_h"], i - 1)
                        for t in range(4):
                            for k in range(2):
                                mm = nc.tensor.matmul(Z[p][0:TC, t * D:(t + 1) * D], gl[p][:, k, t * TC:(t + 1) * TC],
                                                      g.w2[:, k * D:(k + 1) * D], start=(k == 0), stop=(k == 1))
                        mm.then_inc(s["m_fc2"], 1)
                    if live(2):
                        wait(pe, s["m_xn"], i + 3)
                        wait(pe, s["m_yT"], i + 1)
                        for t in range(4):
                            mm = nc.tensor.transpose(Y[p][:, t * TC:(t + 1) * TC], xn[p][:, t, :], g.ident[0:TC, 0:TC])
                        mm.then_inc(s["m_turned"], 1)
                run_pairs(pe, body, 3)

            @block.scalar
            def _(act):
                def body(i, p, live):
                    q = 1 - p
                    if live(1):
                        for k in range(2):
                            wait(act, s["m_fc1"], 2 * (i + 1) + k + 1)
                            wait(act, s["m_fc2"], i)
                            nc.scalar.activation(gl[q][:, k, :], H[q][k][:, 0:PW], ACT.Gelu,
                                                 bias=g.b1[:, k:k + 1]).then_inc(s["m_gelu"], 1)
                    if live(2):
                        wait(act, s["m_turned"], i + 3)
                        wait(act, s["m_fc1"], 2 * (i + 1))
                        nc.scalar.activation(yT[p][:], Y[p][:, 0:PW], ACT.Identity, bias=g.ln2_b,
                                             scale=g.ln2_w).then_inc(s["m_yT"], 1)
                run_pairs(act, body, 3)

            @block.gpsimd
            def _(pool):
                def body(i, p, live):
                    q = 1 - p
                    if live(2):
                        wait(pool, s["m_xn"], i + 3)
                        hp = g.h[0:TC, bass.ds((i + 2) * 4, 4), :]
                        nc.gpsimd.tensor_tensor(hp, hp, g.b2.unsqueeze(1).to_broadcast([TC, 4, D]),
                                                ALU.add).then_inc(s["m_bias"], 1)
                    if live(3):
                        wait(pool, s["m_aggr"], i + 4)
                        nc.gpsimd.tensor_tensor(ve[q][:], mv[q][:, :, 1:2],
                                                g.eps[0:TC, 0:1].unsqueeze(1).to_broadcast([TC, 4, 1]),
                                                ALU.add).then_inc(s["m_ve"], 1)
                        wait(pool, s["m_ve"], i + 4)
                        nc.gpsimd.tensor_tensor(rstd[q][:], ve[q][:],
                                                g.neg_half[0:TC, 0:1].unsqueeze(1).to_broadcast([TC, 4, 1]),
                                                ALU.pow).then_inc(s["m_rstd"], 1)
                run_pairs(pool, body, 3)

            @block.vector
            def _(dve):
                def body(i, p, live):
                    q = 1 - p
                    if live(3):
                        for t in range(4):
                            bn = nc.vector.bn_stats(stats[q][:, t, :], g.h[0:TC, bass.ds((i + 3) * 4 + t, 1), :]
                                                    .rearrange("p o d -> p (o d)"))
                        bn.then_inc(s["m_stats"], 1)
                    if live(2):
                        wait(dve, s["m_rstd"], i + 3)
                        wait(dve, s["m_turned"], i + 1)
                        for t in range(4):
                            x = nc.vector.tensor_scalar(xn[p][:, t, :], g.h[0:TC, bass.ds((i + 2) * 4 + t, 1), :]
                                                        .rearrange("p o d -> p (o d)"), mv[p][:, t, 0:1],
                                                        rstd[p][:, t, :], ALU.subtract, ALU.mult)
                        x.then_inc(s["m_xn"], 1)
                    if live(3):
                        wait_alone(dve, s["m_stats"], i + 4)
                        wait(dve, s["m_ve"], i + 2)
                        for t in range(4):
                            bn = nc.vector.bn_aggr(mv[q][:, t, :], stats[q][:, t, :])
                        bn.then_inc(s["m_aggr"], 1)
                    if live(0):
                        wait(dve, s["m_fc2"], i + 1)
                        wait(dve, s["m_bias"], i + 1)
                        hp = g.h[0:TC, bass.ds(i * 4, 4), :]
                        nc.vector.tensor_tensor(hp, Z[p][0:TC, :].rearrange("p (t d) -> p t d", t=4), hp,
                                                ALU.add).then_inc(s["m_h"], 1)
                run_pairs(dve, body, 3)
        s.clear()


def vit(nc, g, A, ctx):
    g.ident = ctx.enter_context(nc.sbuf_tensor("ident", [128, 128], F32))
    g.neg_half = ctx.enter_context(nc.sbuf_tensor("neg_half", [128, 1], F32))
    g.eps = ctx.enter_context(nc.sbuf_tensor("eps", [128, 1], F32))
    g.h = ctx.enter_context(nc.sbuf_tensor("h", [128, 2 * B, D], F32))
    load_constants(nc, g, A)
    patch_phase(nc, g, A)
    with ExitStack() as vctx:
        g.w = vctx.enter_context(nc.sbuf_tensor("layer_w", [128, 8 * D], F32))
        g.cols = vctx.enter_context(nc.sbuf_tensor("layer_cols", [128, 8], F32))
        g.rows = vctx.enter_context(nc.sbuf_tensor("layer_rows", [TC, 3 * D], F32))
        g.wq, g.wk, g.wv, g.wp = (g.w[:, n * D:(n + 1) * D] for n in range(4))
        g.w1, g.w2 = g.w[:, 4 * D:6 * D], g.w[:, 6 * D:8 * D]
        g.ln1_w, g.ln1_b, g.bq, g.bk, g.ln2_w, g.ln2_b = (g.cols[:, n:n + 1] for n in range(6))
        g.b1 = g.cols[:, 6:8]
        g.bv, g.bp, g.b2 = (g.rows[:, n * D:(n + 1) * D] for n in range(3))
        with nc.Fori(0, DEPTH) as layer:
            load_layer(nc, g, A, layer)
            attention_phase(nc, g)
            mlp_phase(nc, g)


def lay_out(np, x, p):
    f = {k: np.asarray(v) for k, v in p.items()}
    xp = np.asarray(x).reshape(B, 3, 14, 16, 14, 16).transpose(0, 1, 3, 5, 2, 4).reshape(B, KC, 128, 196)
    X = np.zeros((B, 128, KC, TB), np.float32)
    X[:, :, :, 1:NTOK] = xp.transpose(0, 2, 1, 3)

    def chunks(rows):
        out = np.zeros((TB, D), np.float32)
        out[0:NTOK] = rows
        return np.ascontiguousarray(out.reshape(2, TC, D).transpose(1, 0, 2))

    rows = np.concatenate([f["cls_token"].reshape(1, D), np.repeat(f["conv_b"][None], NTOK - 1, 0)])
    w2 = f["fc2_w"].reshape(DEPTH, 2, 128, D).transpose(0, 2, 1, 3).reshape(DEPTH, 128, 2 * D)
    cols = [f["ln1_w"], f["ln1_b"], f["qkv_b"][:, 0:D], f["qkv_b"][:, D:2 * D], f["ln2_w"], f["ln2_b"],
            f["fc1_b"][:, 0:128], f["fc1_b"][:, 128:256]]
    rws = np.concatenate([f["qkv_b"][:, 2 * D:], f["proj_b"], f["fc2_b"]], 1)
    return {
        "x": X,
        "conv_w": np.ascontiguousarray(f["conv_w"].reshape(KC, 128, D).transpose(1, 0, 2)),
        "pos": chunks(f["pos_embed"][0]), "row_bias": chunks(rows),
        "weights": np.ascontiguousarray(np.concatenate([f["qkv_w"], f["proj_w"], f["fc1_w"], w2], 2)),
        "cols": np.ascontiguousarray(np.stack(cols, 2)),
        "rows": np.ascontiguousarray(np.repeat(rws[:, None, :], TC, 1)),
        "norm": np.repeat(np.stack([f["norm_w"], f["norm_b"]])[None], TC, 0),
        "ident": np.eye(128, dtype=np.float32),
    }


TL = 115
WL = 2 * L


def fuse_phase(nc, g, A):
    with ExitStack() as ctx:
        s = Sems(nc, ctx, "f_load f_set f_diag f_txt0 f_txt1 f_stats f_aggr f_ve f_rstd f_xn f_xw f_y f_out0 f_out1 "
                 "f_stats2 f_aggr2 f_ve2 f_rstd2 f_z f_turned f_zT f_conv f_xc f_up f_gelu f_down f_tanh f_sum")

        def sb(name, shape, dt=F32):
            return ctx.enter_context(nc.sbuf_tensor("f_" + name, shape, dt))

        taps, gate_w = sb("taps", [D, 5]), sb("gate_w", [D, 4, D])
        diag, norm = sb("diag", [D, 4, D]), sb("norm", [TC, 2, D])
        stats, mv, ve, rstd = sb("stats", [TC, 4, 6]), sb("mv", [TC, 4, 2]), sb("ve", [TC, 4]), sb("rstd", [TC, 4])
        stats2, mv2, ve2, rstd2 = sb("stats2", [TC, 5, 6]), sb("mv2", [TC, 5, 2]), sb("ve2", [TC, 5]), sb("rstd2", [TC, 5])
        y = [sb(f"y{p}", [TC, 5, D]) for p in range(2)]
        z = [sb(f"z{p}", [TC, 5, D]) for p in range(2)]
        zT = [sb(f"zT{p}", [D, 2, L + 3]) for p in range(2)]
        gel = [sb(f"gel{n}", [D, WL]) for n in range(2)]
        tan = [sb(f"tan{n}", [D, WL]) for n in range(2)]
        Tp, Cp = (ctx.enter_context(nc.psum_tensor(n, [128, 512], F32)) for n in ("f_T", "f_C"))
        Up = [ctx.enter_context(nc.psum_tensor(f"f_U{n}", [128, 512], F32)) for n in range(2)]
        Zp = [ctx.enter_context(nc.psum_tensor(f"f_Z{n}", [128, 512], F32)) for n in range(2)]
        txt_in, sent = [s["f_txt0"], s["f_txt1"]], [s["f_out0"], s["f_out1"]]

        with nc.Block() as block:
            @block.sync
            def _(sp):
                for dst, src in ((taps, "taps"), (gate_w, "gate_w"), (norm, "norm")):
                    sp.dma_start(dst[:], A[src]).then_inc(s["f_load"], 16)
                sp.dma_start(g.hcat[0:T, :].rearrange("(b l) d -> b l d", l=L)[:, NTOK:L, :],
                             A["txt"].rearrange("(b l) d -> b l d", l=TXT)).then_inc(s["f_load"], 16)

                sp.wait_ge(s["f_set"], 8)

                def body(i, p, live):
                    if live(3):
                        wait(sp, s["f_z"], i + 2)
                        sp.dma_start(y[1 - p][0:2 * TXT, 4, :],
                                     A["txt"][bass.ds((i + 3) * (2 * TXT), 2 * TXT), :]).then_inc(txt_in[1 - p], 16)
                        wait(sp, s["f_y"], i + 4)
                        for t in range(4):
                            n, row = TC - t % 2, (t // 2) * L + (t % 2) * TC
                            sp.dma_start(g.hcat[bass.ds((i + 3) * WL + row, n), :],
                                         y[1 - p][0:n, t, :]).then_inc(sent[1 - p], 16)
                run_pairs(sp, body, 3)
                for p in range(2):
                    sp.wait_ge(sent[p], 32 * PAIRS)
                sp.wait_ge(s["f_load"], 64)

            @block.tensor
            def _(pe):
                pe.wait_ge(s["f_load"], 64)
                pe.wait_ge(s["f_diag"], 4)

                def body(i, p, live):
                    q = 1 - p
                    if live(0):
                        for n in range(2):
                            if n == 0:
                                wait(pe, s["f_xc"], i + 1)
                            wait(pe, s["f_gelu"], 2 * i + n)
                            nc.tensor.matmul(Up[n][:, 0:WL], gate_w[:, 2 * n, :], g.xT[:, bass.ds(i * WL, WL)],
                                             start=True, stop=True).then_inc(s["f_up"], 1)
                    if live(1):
                        wait(pe, s["f_zT"], i + 2)
                        wait(pe, s["f_xc"], i + 1)
                        for k in range(4):
                            mm = nc.tensor.matmul(Cp[:, 0:WL].rearrange("p (b l) -> p b l", b=2), diag[:, k, :],
                                                  zT[q][:, :, k:k + L], start=(k == 0), stop=(k == 3))
                        mm.then_inc(s["f_conv"], 1)
                    if live(0):
                        wait(pe, s["f_gelu"], 2 * i + 1)
                        wait(pe, s["f_tanh"], 2 * i)
                        nc.tensor.matmul(Zp[0][:, 0:WL], gate_w[:, 1, :], gel[0][:], start=True, stop=False)
                        nc.tensor.matmul(Zp[0][:, 0:WL], g.ident[:], g.xT[:, bass.ds(i * WL, WL)],
                                         start=False, stop=True).then_inc(s["f_down"], 1)
                    if live(0):
                        wait(pe, s["f_gelu"], 2 * i + 2)
                        wait(pe, s["f_tanh"], 2 * i + 1)
                        nc.tensor.matmul(Zp[1][:, 0:WL], gate_w[:, 3, :], gel[1][:], start=True, stop=False)
                        nc.tensor.matmul(Zp[1][:, 0:WL], g.ident[:], g.xT[:, bass.ds(i * WL, WL)],
                                         start=False, stop=True).then_inc(s["f_down"], 1)
                    if live(2):
                        wait(pe, s["f_z"], i + 3)
                        wait(pe, s["f_zT"], i + 2)
                        for b in range(2):
                            at = b * NTOK
                            nc.tensor.transpose(Tp[:, at:at + TC], z[p][:, 2 * b, :], g.ident[0:TC, 0:TC])
                            nc.tensor.transpose(Tp[:, at + TC:at + NTOK], z[p][0:TC - 1, 2 * b + 1, :],
                                                g.ident[0:TC - 1, 0:TC - 1])
                        mm = nc.tensor.transpose(Tp[:, 2 * NTOK:WL], z[p][0:2 * TXT, 4, :], g.ident[0:2 * TXT, 0:2 * TXT])
                        mm.then_inc(s["f_turned"], 1)
                run_pairs(pe, body, 3)

            @block.scalar
            def _(act):
                act.wait_ge(s["f_load"], 64)
                act.wait_ge(s["f_set"], 8)

                def body(i, p, live):
                    q = 1 - p
                    if live(0):
                        for n in range(2):
                            wait(act, s["f_up"], 2 * i + n + 1)
                            wait(act, s["f_down"], 2 * i)
                            nc.scalar.activation(gel[n][:], Up[n][:, 0:WL], ACT.Gelu).then_inc(s["f_gelu"], 1)
                    if live(1):
                        wait_alone(act, s["f_conv"], i + 2)
                        nc.scalar.activation(g.xT[:, bass.ds((i + 1) * WL, WL)], Cp[:, 0:WL], ACT.Identity,
                                             bias=taps[:, 4:5]).then_inc(s["f_xc"], 1)
                    if live(0):
                        for n in range(2):
                            wait(act, s["f_down"], 2 * i + n + 1)
                            wait(act, s["f_sum"], 2 * i)
                            nc.scalar.activation(tan[n][:], Zp[n][:, 0:WL], ACT.Tanh, scale=0.5)\
                                .then_inc(s["f_tanh"], 1)
                    if live(2):
                        wait(act, s["f_turned"], i + 3)
                        wait(act, s["f_conv"], i + 1)
                        nc.scalar.activation(zT[p][:, :, 3:3 + NTOK],
                                             Tp[:, 0:2 * NTOK].rearrange("p (b l) -> p b l", b=2), ACT.Copy)
                        nc.scalar.activation(zT[p][:, :, 3 + NTOK:],
                                             Tp[:, 2 * NTOK:WL].rearrange("p (b l) -> p b l", b=2),
                                             ACT.Copy).then_inc(s["f_zT"], 1)
                run_pairs(act, body, 3)

            @block.gpsimd
            def _(pool):
                pool.wait_ge(s["f_load"], 64)
                pool.wait_ge(s["f_set"], 8)

                def sums(i):
                    wait(pool, s["f_sum"], 2 * i)
                    for n in range(2):
                        wait(pool, s["f_tanh"], 2 * i + n + 1)
                        nc.gpsimd.tensor_tensor(g.gate_sum[:, n, :], g.gate_sum[:, n, :], tan[n][:],
                                                ALU.add).then_inc(s["f_sum"], 1)

                def body(i, p, live):
                    q = 1 - p
                    if live(2):
                        wait(pool, s["f_aggr2"], i + 3)
                        nc.gpsimd.tensor_tensor(ve2[:], mv2[:, :, 1], g.eps[0:TC, 0:1].to_broadcast([TC, 5]),
                                                ALU.add).then_inc(s["f_ve2"], 1)
                        wait(pool, s["f_ve2"], i + 3)
                        wait(pool, s["f_z"], i + 2)
                        nc.gpsimd.tensor_tensor(rstd2[:], ve2[:], g.neg_half[0:TC, 0:1].to_broadcast([TC, 5]),
                                                ALU.pow).then_inc(s["f_rstd2"], 1)
                    if live(3):
                        wait(pool, s["f_aggr"], i + 4)
                        nc.gpsimd.tensor_tensor(ve[:], mv[:, :, 1], g.eps[0:TC, 0:1].to_broadcast([TC, 4]),
                                                ALU.add).then_inc(s["f_ve"], 1)
                        wait(pool, s["f_ve"], i + 4)
                        wait(pool, s["f_xn"], i + 3)
                        nc.gpsimd.tensor_tensor(rstd[:], ve[:], g.neg_half[0:TC, 0:1].to_broadcast([TC, 4]),
                                                ALU.pow).then_inc(s["f_rstd"], 1)
                    if live(-1):
                        sums(i - 1)
                    if live(3):
                        wait(pool, s["f_xw"], i + 4)
                        nc.gpsimd.tensor_tensor(y[q][:, 0:4, :], y[q][:, 0:4, :],
                                                norm[:, 1, :].unsqueeze(1).to_broadcast([TC, 4, D]),
                                                ALU.add).then_inc(s["f_y"], 1)
                run_pairs(pool, body, 3)
                sums(PAIRS - 1)

            @block.vector
            def _(dve):
                nc.vector.memset(g.gate_sum[:], 0.0).then_inc(s["f_set"], 1)
                nc.vector.memset(mv2[:], 1.0).then_inc(s["f_set"], 1)
                for p in range(2):
                    nc.vector.memset(y[p][:, 4, :], 0.0).then_inc(s["f_set"], 1)
                    nc.vector.memset(z[p][:], 0.0).then_inc(s["f_set"], 1)
                    nc.vector.memset(zT[p][:, :, 0:3], 0.0).then_inc(s["f_set"], 1)
                dve.wait_ge(s["f_load"], 64)
                for k in range(4):
                    nc.vector.tensor_scalar(diag[:, k, :], g.ident[:], taps[:, k:k + 1], None,
                                            ALU.mult).then_inc(s["f_diag"], 1)
                dve.wait_ge(s["f_set"], 8)
                rows = [TC, TC - 1, TC, TC - 1, 2 * TXT]

                def body(i, p, live):
                    q = 1 - p
                    if live(2):
                        wait(dve, s["f_y"], i + 3)
                        wait(dve, txt_in[p], (i + 2 - p) * 8 + 16)
                        for t, n in enumerate(rows):
                            bn = nc.vector.bn_stats(stats2[0:n, t, :], y[p][0:n, t, :])
                        bn.then_inc(s["f_stats2"], 1)
                        wait_alone(dve, s["f_stats2"], i + 3)
                        wait(dve, s["f_ve2"], i + 2)
                        for t, n in enumerate(rows):
                            bn = nc.vector.bn_aggr(mv2[0:n, t, :], stats2[0:n, t, :])
                        bn.then_inc(s["f_aggr2"], 1)
                    if live(3):
                        for t in range(4):
                            bn = nc.vector.bn_stats(stats[:, t, :], g.h[0:TC, bass.ds((i + 3) * 4 + t, 1), :]
                                                    .rearrange("p o d -> p (o d)"))
                        bn.then_inc(s["f_stats"], 1)
                        wait_alone(dve, s["f_stats"], i + 4)
                        wait(dve, s["f_ve"], i + 3)
                        for t in range(4):
                            bn = nc.vector.bn_aggr(mv[:, t, :], stats[:, t, :])
                        bn.then_inc(s["f_aggr"], 1)
                    if live(2):
                        wait(dve, s["f_aggr2"], i + 3)
                        wait(dve, s["f_rstd2"], i + 3)
                        wait(dve, s["f_turned"], i + 1)
                        for t, n in enumerate(rows):
                            x = nc.vector.tensor_scalar(z[p][0:n, t, :], y[p][0:n, t, :], mv2[0:n, t, 0:1],
                                                        rstd2[0:n, t:t + 1], ALU.subtract, ALU.mult)
                        x.then_inc(s["f_z"], 1)
                    if live(3):
                        wait(dve, s["f_aggr"], i + 4)
                        wait(dve, s["f_rstd"], i + 4)
                        wait(dve, sent[q], 32 * (i + 1 - q) + 64)
                        for t in range(4):
                            x = nc.vector.tensor_scalar(y[q][:, t, :], g.h[0:TC, bass.ds((i + 3) * 4 + t, 1), :]
                                                        .rearrange("p o d -> p (o d)"), mv[:, t, 0:1],
                                                        rstd[:, t:t + 1], ALU.subtract, ALU.mult)
                        x.then_inc(s["f_xn"], 1)
                        wait(dve, s["f_xn"], i + 4)
                        nc.vector.tensor_tensor(y[q][:, 0:4, :], y[q][:, 0:4, :],
                                                norm[:, 0, :].unsqueeze(1).to_broadcast([TC, 4, D]),
                                                ALU.mult).then_inc(s["f_xw"], 1)
                run_pairs(dve, body, 3)
        s.clear()


def gate_phase(nc, g):
    with ExitStack() as ctx:
        s = Sems(nc, ctx, "g_sum g_set g_mean g_scan g_pair")

        def sb(name, shape, dt=F32):
            return ctx.enter_context(nc.sbuf_tensor("g_" + name, shape, dt))

        mean, zero, one_step = sb("mean", [128, 2, L]), sb("zero", [128, L]), sb("one", [128, 2, L])
        ones = sb("ones", [128, 128])
        Mp = [ctx.enter_context(nc.psum_tensor(f"g_M{n}", [128, 512], F32)) for n in range(2)]
        with nc.Block() as block:
            @block.tensor
            def _(pe):
                pe.wait_ge(s["g_set"], 5)
                for n in range(2):
                    for b in range(2):
                        mm = nc.tensor.matmul(Mp[n][:, 0:L], ones[:], g.gate_sum[:, n, b * L:(b + 1) * L],
                                              start=(b == 0), stop=(b == 1))
                    mm.then_inc(s["g_sum"], 1)

            @block.vector
            def _(dve):
                nc.vector.memset(ones[:], 1.0).then_inc(s["g_set"], 1)
                nc.vector.memset(zero[:], 0.0).then_inc(s["g_set"], 1)
                nc.vector.memset(g.minus[:], -1.0).then_inc(s["g_set"], 1)
                nc.vector.memset(g.decay[:, :, 0:1], 1.0).then_inc(s["g_set"], 1)
                nc.vector.memset(g.drift[:, :, 0:1], 0.0).then_inc(s["g_set"], 1)
                for n in range(2):
                    dve.wait_ge(s["g_sum"], n + 1)
                    nc.vector.tensor_scalar(mean[:, n, :], Mp[n][:, 0:L], 0.5 / (B * D), 0.5, ALU.mult,
                                            ALU.add).then_inc(s["g_mean"], 1)
                dve.wait_ge(s["g_mean"], 2)
                nc.vector.tensor_scalar(one_step[:, 0, :], mean[:, 0, :], 0.01, None, ALU.mult).then_inc(s["g_mean"], 1)
                dve.wait_ge(s["g_mean"], 3)
                nc.vector.tensor_tensor_scan(g.decay[:, 0, 1:L], mean[:, 1, 0:L - 1], zero[:, 0:L - 1], 1.0,
                                             ALU.mult, ALU.add).then_inc(s["g_scan"], 1)
                nc.vector.tensor_tensor_scan(g.drift[:, 0, 1:L], mean[:, 1, 0:L - 1], one_step[:, 0, 0:L - 1], 0.0,
                                             ALU.mult, ALU.add).then_inc(s["g_scan"], 1)
                dve.wait_ge(s["g_scan"], 2)
                for k in (g.decay, g.drift):
                    nc.vector.tensor_copy(k[:, 1, 1:L], k[:, 0, 1:L]).then_inc(s["g_pair"], 1)
                dve.wait_ge(s["g_pair"], 2)
        s.clear()


def memory_phase(nc, g, A):
    with ExitStack() as ctx:
        s = Sems(nc, ctx, "y_load y_set y_xc y_q y_sq y_max y_rinv y_qn y_qT y_q2 y_up y_gelu y_g2 y_down y_hc0 y_hc1 "
                 "y_pre y_h2 y_stats y_aggr y_ve y_rstd y_zn y_zout0 y_zout1 y_turned y_zs y_zst y_logit y_lg")

        def sb(name, shape, dt=F32):
            return ctx.enter_context(nc.sbuf_tensor("y_" + name, shape, dt))

        w = sb("w", [D, 3, D])
        router = sb("router", [D, 16])
        xc = [sb(f"xc{p}", [D, WL + 1]) for p in range(2)]
        junk, ss, rinv = sb("junk", [TL, 4, D]), sb("ss", [TL, 4]), sb("rinv", [TL, 4])
        ssm = sb("ssm", [TL, 4])
        qn = [sb(f"qn{p}", [TL, 4, D]) for p in range(2)]
        q_decay, q_drift = sb("q_decay", [D, WL]), sb("q_drift", [D, WL])
        gel = sb("gel", [D, WL])
        g_decay, g_drift = ([sb(f"{n}{p}", [D, WL + 1]) for p in range(2)] for n in ("g_decay", "g_drift"))
        hc = [sb(f"hc{p}", [TL, 4, D]) for p in range(2)]
        stats, mv, ve, rstd = sb("stats", [TL, 4, 6]), sb("mv", [TL, 4, 2]), sb("ve", [TL, 4]), sb("rstd", [TL, 4])
        zn = [sb(f"zn{p}", [TL, 4, D]) for p in range(2)]
        zs = [sb(f"zs{p}", [D, WL + 1]) for p in range(2)]
        Qp, QTp, Up, Op, ZTp, Lp = (ctx.enter_context(nc.psum_tensor("y_" + n, [128, 512], F32))
                                    for n in ("Q", "QT", "U", "O", "ZT", "L"))
        hc_in, sent = [s["y_hc0"], s["y_hc1"]], [s["y_zout0"], s["y_zout1"]]
        decay = g.decay[:].rearrange("p b l -> p (b l)")
        drift = g.drift[:].rearrange("p b l -> p (b l)")
        rows = [TL, TL - 1, TL, TL - 1]
        cols = [(t // 2) * L + (t % 2) * TL for t in range(4)]

        with nc.Block() as block:
            @block.sync
            def _(sp):
                sp.dma_start(w[:], A["memory_w"]).then_inc(s["y_load"], 16)
                sp.dma_start(router[:], A["router_w"]).then_inc(s["y_load"], 16)
                sp.wait_ge(s["y_set"], 12)

                def body(i, p, live):
                    q = 1 - p
                    if live(2):
                        wait(sp, s["y_h2"], i + 1)
                        for t in range(4):
                            sp.dma_start(hc[p][0:rows[t], t, :], g.hcat[bass.ds((i + 2) * WL + cols[t], rows[t]), :])\
                                .then_inc(hc_in[p], 16)
                    if live(1):
                        wait(sp, s["y_zn"], i + 2)
                        for t in range(4):
                            sp.dma_start(g.table[bass.ds((i + 1) * WL + cols[t], rows[t]), 0:D],
                                         zn[q][0:rows[t], t, :]).then_inc(sent[q], 16)
                run_pairs(sp, body, 3)
                for p in range(2):
                    sp.wait_ge(sent[p], 32 * PAIRS)

            @block.tensor
            def _(pe):
                pe.wait_ge(s["y_load"], 32)

                def body(i, p, live):
                    q = 1 - p
                    if live(2):
                        wait(pe, s["y_qn"], i + 3)
                        wait(pe, s["y_q2"], 2 * (i + 2))
                        for t in range(4):
                            mm = nc.tensor.transpose(QTp[:, cols[t]:cols[t] + rows[t]], qn[p][0:rows[t], t, :],
                                                     g.ident[0:rows[t], 0:rows[t]])
                        mm.then_inc(s["y_qT"], 1)
                    if live(3):
                        wait(pe, s["y_xc"], i + 4)
                        wait(pe, s["y_qn"], i + 3)
                        for t in range(4):
                            mm = nc.tensor.matmul(Qp[0:TL, t * D:(t + 1) * D], xc[q][:, cols[t]:cols[t] + TL],
                                                  w[:, 0, :], start=True, stop=True)
                        mm.then_inc(s["y_q"], 1)
                    if live(1):
                        wait(pe, s["y_g2"], 2 * (i + 2))
                        wait(pe, s["y_h2"], i + 1)
                        for t in range(4):
                            nc.tensor.matmul(Op[0:TL, t * D:(t + 1) * D], g_decay[q][:, cols[t]:cols[t] + TL],
                                             w[:, 2, :], start=True, stop=False)
                            mm = nc.tensor.matmul(Op[0:TL, t * D:(t + 1) * D], g_drift[q][:, cols[t]:cols[t] + TL],
                                                  g.minus[:], start=False, stop=True)
                        mm.then_inc(s["y_down"], 1)
                    if live(0):
                        wait(pe, s["y_zn"], i + 1)
                        wait(pe, s["y_zst"], i)
                        for t in range(4):
                            mm = nc.tensor.transpose(ZTp[:, cols[t]:cols[t] + rows[t]], zn[p][0:rows[t], t, :],
                                                     g.ident[0:rows[t], 0:rows[t]])
                        mm.then_inc(s["y_turned"], 1)
                    if live(2):
                        wait(pe, s["y_q2"], 2 * (i + 3))
                        wait(pe, s["y_gelu"], i + 2)
                        nc.tensor.matmul(Up[:, 0:WL], w[:, 1, :], q_decay[:], start=True, stop=False)
                        nc.tensor.matmul(Up[:, 0:WL], g.minus[:], q_drift[:], start=False,
                                         stop=True).then_inc(s["y_up"], 1)
                    if live(0):
                        wait(pe, s["y_zs"], i + 1)
                        wait(pe, s["y_lg"], i)
                        for t in range(4):
                            mm = nc.tensor.matmul(Lp[0:TL, t * 16:(t + 1) * 16], zs[p][:, cols[t]:cols[t] + TL],
                                                  router[:], start=True, stop=True)
                        mm.then_inc(s["y_logit"], 1)
                run_pairs(pe, body, 3)

            @block.scalar
            def _(act):
                act.wait_ge(s["y_set"], 12)

                def body(i, p, live):
                    if live(3):
                        wait(act, s["y_q"], i + 4)
                        wait(act, s["y_max"], i + 3)
                        for t in range(4):
                            a = nc.scalar.activation(junk[:, t, :], Qp[0:TL, t * D:(t + 1) * D], ACT.Square,
                                                     accum_out=ss[:, t:t + 1])
                        a.then_inc(s["y_sq"], 1)
                    if live(0):
                        wait(act, s["y_turned"], i + 1)
                        wait(act, s["y_logit"], i - 1)
                        nc.scalar.activation(zs[p][:, 0:WL], ZTp[:, 0:WL], ACT.Copy).then_inc(s["y_zs"], 1)
                        nc.scalar.activation(g.xT[:, bass.ds(i * WL, WL)], ZTp[:, 0:WL],
                                             ACT.Copy).then_inc(s["y_zst"], 1)
                    if live(2):
                        wait(act, s["y_up"], i + 3)
                        wait(act, s["y_g2"], 2 * (i + 2))
                        nc.scalar.activation(gel[:], Up[:, 0:WL], ACT.Gelu).then_inc(s["y_gelu"], 1)
                    if live(4):
                        wait(act, s["y_q"], i + 3)
                        nc.scalar.activation(xc[p][:, 0:WL], g.xT[:, bass.ds((i + 4) * WL, WL)],
                                             ACT.Copy).then_inc(s["y_xc"], 1)
                run_pairs(act, body, 4)

            @block.gpsimd
            def _(pool):
                pool.wait_ge(s["y_set"], 12)

                def body(i, p, live):
                    q = 1 - p
                    if live(1):
                        wait(pool, hc_in[q], (i + 1 - q) * 32 + 64)
                        nc.gpsimd.tensor_tensor(hc[q][:], hc[q][:], qn[q][:], ALU.add).then_inc(s["y_pre"], 1)
                    if live(3):
                        wait_alone(pool, s["y_sq"], i + 4)
                        nc.gpsimd.tensor_scalar(ssm[:], ss[:], 1e-24, None, ALU.max).then_inc(s["y_max"], 1)
                        wait(pool, s["y_max"], i + 4)
                        wait(pool, s["y_qn"], i + 3)
                        nc.gpsimd.tensor_tensor(rinv[:], ssm[:], g.neg_half[0:TL, 0:1].to_broadcast([TL, 4]),
                                                ALU.pow).then_inc(s["y_rinv"], 1)
                    if live(1):
                        wait(pool, s["y_aggr"], i + 2)
                        nc.gpsimd.tensor_tensor(ve[:], mv[:, :, 1], g.eps[0:TL, 0:1].to_broadcast([TL, 4]),
                                                ALU.add).then_inc(s["y_ve"], 1)
                        wait(pool, s["y_ve"], i + 2)
                        wait(pool, s["y_zn"], i + 1)
                        nc.gpsimd.tensor_tensor(rstd[:], ve[:], g.neg_half[0:TL, 0:1].to_broadcast([TL, 4]),
                                                ALU.pow).then_inc(s["y_rstd"], 1)
                    if live(2):
                        wait(pool, s["y_gelu"], i + 3)
                        wait(pool, s["y_down"], i + 1)
                        nc.gpsimd.tensor_tensor(g_drift[p][:, 0:WL], gel[:], drift, ALU.mult).then_inc(s["y_g2"], 1)
                run_pairs(pool, body, 3)

            @block.vector
            def _(dve):
                for p in range(2):
                    for t in (xc[p], g_decay[p], g_drift[p], zs[p]):
                        nc.vector.memset(t[:, WL:WL + 1], 0.0).then_inc(s["y_set"], 1)
                    nc.vector.memset(hc[p][:], 0.0).then_inc(s["y_set"], 1)
                    nc.vector.memset(zn[p][:], 0.0).then_inc(s["y_set"], 1)

                def body(i, p, live):
                    q = 1 - p
                    if live(2):
                        for k, (dst, c) in enumerate(((q_decay, decay), (q_drift, drift))):
                            if k == 0:
                                wait(dve, s["y_qT"], i + 3)
                                wait(dve, s["y_up"], i + 2)
                            nc.vector.tensor_tensor(dst[:], QTp[:, 0:WL], c, ALU.mult).then_inc(s["y_q2"], 1)
                    if live(1):
                        wait(dve, s["y_down"], i + 2)
                        wait(dve, s["y_pre"], i + 2)
                        h2 = g.h[0:TL, bass.ds((i + 1) * 4, 4), :]
                        nc.vector.tensor_tensor(h2, Op[0:TL, :].rearrange("p (t d) -> p t d", t=4), hc[q][:],
                                                ALU.add).then_inc(s["y_h2"], 1)
                        wait_alone(dve, s["y_h2"], i + 2)
                        for t in range(4):
                            bn = nc.vector.bn_stats(stats[:, t, :], g.h[0:TL, bass.ds((i + 1) * 4 + t, 1), :]
                                                    .rearrange("p o d -> p (o d)"))
                        bn.then_inc(s["y_stats"], 1)
                        wait_alone(dve, s["y_stats"], i + 2)
                        wait(dve, s["y_ve"], i + 1)
                        for t in range(4):
                            bn = nc.vector.bn_aggr(mv[:, t, :], stats[:, t, :])
                        bn.then_inc(s["y_aggr"], 1)
                    if live(3):
                        wait(dve, s["y_rinv"], i + 4)
                        wait(dve, s["y_qT"], i + 2)
                        wait(dve, s["y_pre"], i + 2)
                        nc.vector.tensor_tensor(qn[q][:], Qp[0:TL, :].rearrange("p (t d) -> p t d", t=4),
                                                rinv[:].unsqueeze(2).to_broadcast([TL, 4, D]),
                                                ALU.mult).then_inc(s["y_qn"], 1)
                    if live(2):
                        wait(dve, s["y_gelu"], i + 3)
                        wait(dve, s["y_down"], i + 1)
                        nc.vector.tensor_tensor(g_decay[p][:, 0:WL], gel[:], decay, ALU.mult).then_inc(s["y_g2"], 1)
                    if live(1):
                        wait(dve, s["y_aggr"], i + 2)
                        wait(dve, s["y_rstd"], i + 2)
                        wait(dve, s["y_turned"], i)
                        wait(dve, sent[q], 32 * (i + 1 - q))
                        for t in range(4):
                            x = nc.vector.tensor_scalar(zn[q][:, t, :], g.h[0:TL, bass.ds((i + 1) * 4 + t, 1), :]
                                                        .rearrange("p o d -> p (o d)"), mv[:, t, 0:1],
                                                        rstd[:, t:t + 1], ALU.subtract, ALU.mult)
                        x.then_inc(s["y_zn"], 1)
                    if live(0):
                        wait(dve, s["y_logit"], i + 1)
                        nc.vector.tensor_copy(g.logits[:, :, bass.ds(i * 2, 2), :],
                                              Lp[0:TL, 0:64].rearrange("p (b c e) -> p c b e", b=2, c=2)).then_inc(s["y_lg"], 1)
                run_pairs(dve, body, 3)
        s.clear()


E = 16
CAP = T // E
EH = 512
BLK = L
NBLK = T // BLK
TILES = 8
SLOTS = [min(TL, CAP - k * TL) for k in range(TILES)]
ROW = D + E


def router_phase(nc, g):
    QUADS = B // 4
    with ExitStack() as ctx:
        s = Sems(nc, ctx, "r_max r_sub r_exp r_sum r_inv r_prob r_turn r_copy r_out")

        def sb(name, shape, dt=F32):
            return ctx.enter_context(nc.sbuf_tensor("r_" + name, shape, dt))

        mx, total = sb("max", [TL, 2 * B]), sb("total", [TL, 2 * B])
        pT = sb("pT", [4 * E, QUADS, L])
        P = [ctx.enter_context(nc.psum_tensor(f"r_P{n}", [128, 512], F32)) for n in range(4)]
        by_chunk = g.logits
        lg = by_chunk[:].rearrange("p c b e -> p (c b) e")

        def wide(a):
            return a[:].unsqueeze(2).to_broadcast([TL, 2 * B, E])

        with nc.Block() as block:
            @block.sync
            def _(sp):
                sp.wait_ge(s["r_prob"], 1)
                for c in range(2):
                    n = TL - c
                    sp.dma_start(g.table[:, D:ROW].rearrange("(b l) e -> l b e", l=L)[c * TL:c * TL + n],
                                 by_chunk[0:n, c]).then_inc(s["r_out"], 16)
                sp.wait_ge(s["r_copy"], QUADS)
                for b in range(4):
                    sp.dma_start(g.by_expert.rearrange("e (q b l) -> b e q l", b=4, l=L)[b],
                                 pT[b * E:(b + 1) * E, :, :]).then_inc(s["r_out"], 16)
                sp.wait_ge(s["r_out"], 96)

            @block.vector
            def _(dve):
                nc.vector.tensor_reduce(mx[:], lg, AX.X, ALU.max).then_inc(s["r_max"], 1)
                dve.wait_ge(s["r_max"], 1)
                nc.vector.tensor_tensor(lg, lg, wide(mx), ALU.subtract).then_inc(s["r_sub"], 1)
                dve.wait_ge(s["r_exp"], 1)
                nc.vector.tensor_reduce(total[:], lg, AX.X, ALU.add).then_inc(s["r_sum"], 1)
                dve.wait_ge(s["r_sum"], 1)
                nc.vector.reciprocal(mx[:], total[:]).then_inc(s["r_inv"], 1)
                dve.wait_ge(s["r_inv"], 1)
                nc.vector.tensor_tensor(lg, lg, wide(mx), ALU.mult).then_inc(s["r_prob"], 1)
                for q in range(QUADS):
                    dve.wait_ge(s["r_turn"], q + 1)
                    nc.vector.tensor_copy(pT[:, q, :], P[q % 4][0:4 * E, 0:L]).then_inc(s["r_copy"], 1)

            @block.scalar
            def _(act):
                act.wait_ge(s["r_sub"], 1)
                nc.scalar.activation(lg, lg, ACT.Exp).then_inc(s["r_exp"], 1)

            @block.tensor
            def _(pe):
                pe.wait_ge(s["r_prob"], 1)
                for q in range(QUADS):
                    if q >= 4:
                        pe.wait_ge(s["r_copy"], q - 3)
                    for c in range(2):
                        n = TL - c
                        mm = nc.tensor.transpose(P[q % 4][0:4 * E, c * TL:c * TL + n],
                                                 by_chunk[0:n, c, 4 * q:4 * q + 4, :].rearrange("p b e -> p (b e)"), g.ident[0:n, 0:n])
                    mm.then_inc(s["r_turn"], 1)
        s.clear()


def choice_phase(nc, g, A):
    with ExitStack() as ctx:
        s = Sems(nc, ctx, "t_load t_set t_cand t_count t_total t_step t_thr t_bit t_gt t_tie t_pref t_off t_need "
                 "t_sel t_run t_runoff t_final t_save t_spread t_cmp t_blk t_row t_fetch0 t_fetch1 t_in0 t_in1 t_now t_idx")
        W = T // 8

        def sb(name, shape, dt=F32):
            return ctx.enter_context(nc.sbuf_tensor("t_" + name, shape, dt))

        prob, gt, tie, run, zero = (sb(n, [128, W]) for n in ("prob", "gt", "tie", "run", "zero"))
        same, ahead = sb("same", [128, 128]), sb("ahead", [128, 128])
        thr, bit, cand, step = (sb(n, [128, 1], I32) for n in ("thr", "bit", "cand", "step"))
        cnt, n_gt, n_tie, need, ends = sb("cnt", [128, 1]), sb("n_gt", [128, 1]), sb("n_tie", [128, 1]), sb("need", [128, 1]), sb("ends", [128, 8])
        slot, first_row = sb("slot", [TL, TILES]), sb("first_row", [TL, E])
        spread, cmp = sb("spread", [TL, E * NBLK]), sb("cmp", [TL, E * NBLK])
        blk, row = sb("blk", [TL, TILES, E]), sb("row", [TL, TILES, E], I32)
        fetched = [sb(f"fetched{p}", [TL, TILES, BLK]) for p in range(2)]
        inside = sb("inside", [TL, E * TILES])
        junk = sb("junk", [TL, 2, TILES, BLK])
        Tp = ctx.enter_context(nc.psum_tensor("t_T", [128, 4], F32))
        fetch, read = [s["t_fetch0"], s["t_fetch1"]], [s["t_in0"], s["t_in1"]]
        now = [sb(f"now{p}", [TL, TILES], I32) for p in range(2)]
        BITS = 30

        with nc.Block() as block:
            @block.sync
            def _(sp):
                sp.dma_start(prob[:], g.by_expert.rearrange("e (k n) -> (e k) n", k=8)).then_inc(s["t_load"], 16)
                for dst, src in ((same, "same_expert"), (ahead, "ahead"), (slot, "slot"), (first_row, "first_row")):
                    sp.dma_start(dst[:], A[src]).then_inc(s["t_load"], 16)
                sp.wait_ge(s["t_final"], 2)
                sp.dma_start(g.counts.rearrange("(p x) n -> p (x n)", x=8), run[:]).then_inc(s["t_save"], 16)
                sp.dma_start(g.ends.rearrange("o (p x) -> (o p) x", x=8), ends[:]).then_inc(s["t_save"], 16)
                sp.wait_ge(s["t_save"], 32)
                sp.dma_start(spread[:], g.ends.to_broadcast([TL, E * NBLK])).then_inc(s["t_spread"], 16)

            @block.tensor
            def _(pe):
                pe.wait_ge(s["t_load"], 80)
                def turn(i):
                    wait(pe, s["t_count"], i + 1)
                    wait(pe, s["t_step"], i)
                    nc.tensor.matmul(Tp[:, 0:1], same[:], cnt[:], start=True, stop=True).then_inc(s["t_total"], 1)
                loop(pe, BITS, turn)
                pe.wait_ge(s["t_step"], BITS)
                pe.wait_ge(s["t_pref"], 1)
                nc.tensor.matmul(Tp[:, 0:1], same[:], n_gt[:], start=True, stop=False)
                nc.tensor.matmul(Tp[:, 0:1], ahead[:], run[:, W - 1:W], start=False, stop=True).then_inc(s["t_off"], 1)
                pe.wait_ge(s["t_run"], 1)
                nc.tensor.matmul(Tp[:, 1:2], ahead[:], run[:, W - 1:W], start=True, stop=True).then_inc(s["t_runoff"], 1)

            @block.vector
            def _(dve):
                nc.vector.memset(thr[:], 0).then_inc(s["t_set"], 1)
                nc.vector.memset(bit[:], 1 << (BITS - 1)).then_inc(s["t_set"], 1)
                nc.vector.memset(zero[:], 0.0).then_inc(s["t_set"], 1)
                nc.vector.memset(g.token[:], 0).then_inc(s["t_set"], 1)
                dve.wait_ge(s["t_set"], 4)
                dve.wait_ge(s["t_load"], 80)
                def turn(i):
                    wait(dve, s["t_thr"], i)
                    wait(dve, s["t_bit"], i)
                    nc.vector.tensor_tensor(cand[:], thr[:], bit[:], ALU.bitwise_or).then_inc(s["t_cand"], 1)
                    wait(dve, s["t_cand"], i + 1)
                    wait(dve, s["t_total"], i)
                    nc.vector.tensor_scalar(gt[:], prob[:], cand[:].bitcast(F32), None, ALU.is_ge, ALU.add,
                                            accum_out=cnt[:]).then_inc(s["t_count"], 1)
                    wait(dve, s["t_total"], i + 1)
                    nc.vector.scalar_tensor_tensor(out=step[:], in0=Tp[:, 0:1], scalar=float(CAP), in1=bit[:],
                                                   op0=ALU.is_ge, op1=ALU.mult).then_inc(s["t_step"], 1)
                    wait(dve, s["t_step"], i + 1)
                    nc.vector.tensor_tensor(thr[:], thr[:], step[:], ALU.bitwise_or).then_inc(s["t_thr"], 1)
                    nc.vector.tensor_single_scalar(bit[:], bit[:], 1, ALU.logical_shift_right).then_inc(s["t_bit"], 1)
                loop(dve, BITS, turn)
                dve.wait_ge(s["t_thr"], BITS)
                at = thr[:].bitcast(F32)
                nc.vector.tensor_scalar(gt[:], prob[:], at, None, ALU.is_gt, ALU.add,
                                        accum_out=n_gt[:]).then_inc(s["t_gt"], 1)
                nc.vector.tensor_scalar(tie[:], prob[:], at, None, ALU.is_equal).then_inc(s["t_tie"], 1)
                dve.wait_ge(s["t_gt"], 1)
                dve.wait_ge(s["t_tie"], 1)
                nc.vector.tensor_tensor_scan(run[:], tie[:], zero[:], 0.0, ALU.add, ALU.add).then_inc(s["t_pref"], 1)
                dve.wait_ge(s["t_off"], 1)
                nc.vector.tensor_scalar(need[:], Tp[:, 0:1], -1.0, float(CAP), ALU.mult, ALU.add).then_inc(s["t_need"], 1)
                dve.wait_ge(s["t_need"], 1)
                dve.wait_ge(s["t_pref"], 1)
                nc.vector.scalar_tensor_tensor(out=tie[:], in0=run[:], scalar=need[:], in1=tie[:], op0=ALU.is_le,
                                               op1=ALU.mult).then_inc(s["t_sel"], 1)
                dve.wait_ge(s["t_sel"], 1)
                nc.vector.tensor_tensor_scan(run[:], gt[:], tie[:], 0.0, ALU.add, ALU.add).then_inc(s["t_run"], 1)
                dve.wait_ge(s["t_runoff"], 1)
                dve.wait_ge(s["t_run"], 1)
                nc.vector.tensor_copy(cnt[:], Tp[:, 1:2]).then_inc(s["t_sel"], 1)
                dve.wait_ge(s["t_sel"], 2)
                nc.vector.tensor_scalar(run[:], run[:], cnt[:], None, ALU.add).then_inc(s["t_final"], 1)
                dve.wait_ge(s["t_final"], 1)
                nc.vector.tensor_copy(ends[:], run[:, BLK - 1::BLK]).then_inc(s["t_final"], 1)
                dve.wait_ge(s["t_spread"], 16)
                for k in range(TILES):
                    if k:
                        dve.wait_ge(s["t_blk"], k)
                    nc.vector.tensor_scalar(cmp[:], spread[:], slot[:, k:k + 1], None, ALU.is_le).then_inc(s["t_cmp"], 1)
                    dve.wait_ge(s["t_cmp"], k + 1)
                    nc.vector.tensor_reduce(blk[:, k, :], cmp[:].rearrange("p (e n) -> p e n", e=E), AX.X,
                                            ALU.add).then_inc(s["t_blk"], 1)
                dve.wait_ge(s["t_blk"], TILES)
                nc.vector.tensor_tensor(row[:], blk[:], first_row[:].unsqueeze(1).to_broadcast([TL, TILES, E]),
                                        ALU.add).then_inc(s["t_row"], 1)
                def turn(j):
                    for p in range(2):
                        wait(dve, fetch[p], (j + 1) * (16 * TILES))
                        for k, n in enumerate(SLOTS):
                            a = nc.vector.tensor_scalar(junk[0:n, p, k, :], fetched[p][0:n, k, :], slot[0:n, k:k + 1], None,
                                                        ALU.is_le, ALU.add,
                                                        accum_out=inside[0:n, bass.ds(j * (2 * TILES) + p * TILES + k, 1)])
                        a.then_inc(read[p], 1)
                loop(dve, E // 2, turn)
                for p in range(2):
                    dve.wait_ge(read[p], E // 2)
                for k, n in enumerate(SLOTS):
                    nc.vector.scalar_tensor_tensor(out=g.token[0:n, k, :], in0=blk[0:n, k, :], scalar=float(BLK),
                                                   in1=inside[0:n, k::TILES], op0=ALU.mult, op1=ALU.add)\
                        .then_inc(s["t_idx"], 1)

            @block.gpsimd
            def _(pool):
                pool.wait_ge(s["t_save"], 32)
                pool.wait_ge(s["t_row"], 1)
                def turn(j):
                    for p in range(2):
                        wait(pool, read[p], j)
                        nc.gpsimd.tensor_copy(now[p][:], row[:, :, bass.ds(j * 2 + p, 1)]
                                              .rearrange("p k o -> p (k o)")).then_inc(s["t_now"], 1)
                        wait_alone(pool, s["t_now"], j * 2 + p + 1)
                        for k, n in enumerate(SLOTS):
                            nc.gpsimd.indirect_dma_start(
                                out=fetched[p][0:n, k, :], out_offset=None, in_=g.counts[:, :],
                                in_offset=bass.IndirectOffsetOnAxis(now[p][0:n, k:k + 1].bitcast(U32), 0))\
                                .then_inc(fetch[p], 16)
                loop(pool, E // 2, turn)
        s.clear()


def shared_phase(nc, g, A, out):
    with ExitStack() as ctx:
        s = Sems(nc, ctx, "h_load h_set h_up h_gelu h_down0 h_down1 h_bias h_sum0 h_sum1 h_out0 h_out1")

        def sb(name, shape, dt=F32):
            return ctx.enter_context(nc.sbuf_tensor("h_" + name, shape, dt))

        w1, w2, b1, b2 = sb("w1", [D, EH]), sb("w2", [128, 4, D]), sb("b1", [128, 4]), sb("b2", [TL, D])
        gel = [sb(f"gel{p}", [128, 4, WL + 1]) for p in range(2)]
        y = [sb(f"y{p}", [TL, 4, D]) for p in range(2)]
        Up = [ctx.enter_context(nc.psum_tensor(f"h_U{n}", [128, 512], F32)) for n in range(4)]
        Op = [ctx.enter_context(nc.psum_tensor(f"h_O{p}", [128, 512], F32)) for p in range(2)]
        rows = [TL, TL - 1, TL, TL - 1]
        cols = [(t // 2) * L + (t % 2) * TL for t in range(4)]
        summed, sent = [s["h_sum0"], s["h_sum1"]], [s["h_out0"], s["h_out1"]]
        down = [s["h_down0"], s["h_down1"]]

        with nc.Block() as block:
            @block.sync
            def _(sp):
                for dst, src in ((w1, "sw1"), (w2, "sw2"), (b1, "sb1"), (b2, "sb2")):
                    sp.dma_start(dst[:], A[src]).then_inc(s["h_load"], 16)
                def turn(j):
                    for p in range(2):
                        wait(sp, summed[p], j + 1)
                        for t in range(4):
                            sp.dma_start(out[bass.ds(j * (2 * WL) + p * WL + cols[t], rows[t]), :],
                                         y[p][0:rows[t], t, :]).then_inc(sent[p], 16)
                loop(sp, PAIRS // 2, turn)
                for p in range(2):
                    sp.wait_ge(sent[p], 32 * PAIRS)

            @block.tensor
            def _(pe):
                pe.wait_ge(s["h_load"], 64)
                pe.wait_ge(s["h_set"], 2)

                def body(i, p, j, first, second):
                    if first:
                        for k in range(4):
                            wait(pe, s["h_gelu"], 4 * i + k + 1)
                            nc.tensor.matmul(Up[k][:, 0:WL], w1[:, k * 128:(k + 1) * 128],
                                             g.xT[:, bass.ds((i + 1) * WL, WL)], start=True,
                                             stop=True).then_inc(s["h_up"], 1)
                    if second:
                        wait(pe, s["h_gelu"], 4 * (i + 1))
                        wait(pe, summed[p], j)
                        for t in range(4):
                            for k in range(4):
                                mm = nc.tensor.matmul(Op[p][0:TL, t * D:(t + 1) * D], gel[p][:, k, cols[t]:cols[t] + TL],
                                                      w2[:, k, :], start=(k == 0), stop=(k == 3))
                        mm.then_inc(down[p], 1)
                body(-1, 1, 0, True, False)
                def turn(j):
                    for p in range(2):
                        body(j * 2 + p, p, j, True, True)
                loop(pe, PAIRS // 2 - 1, turn)
                body(PAIRS - 2, 0, PAIRS // 2 - 1, True, True)
                body(PAIRS - 1, 1, PAIRS // 2 - 1, False, True)

            @block.scalar
            def _(act):
                act.wait_ge(s["h_load"], 64)
                def turn(j):
                    for p in range(2):
                        i = j * 2 + p
                        for k in range(4):
                            wait(act, s["h_up"], 4 * i + k + 1)
                            wait(act, down[p], j)
                            nc.scalar.activation(gel[p][:, k, 0:WL], Up[k][:, 0:WL], ACT.Gelu_apprx_tanh,
                                                 bias=b1[:, k:k + 1]).then_inc(s["h_gelu"], 1)
                loop(act, PAIRS // 2, turn)

            @block.gpsimd
            def _(pool):
                pool.wait_ge(s["h_load"], 64)
                def turn(i):
                    h2 = g.h[0:TL, bass.ds(i * 4, 4), :]
                    nc.gpsimd.tensor_tensor(h2, h2, b2[:].unsqueeze(1).to_broadcast([TL, 4, D]),
                                            ALU.add).then_inc(s["h_bias"], 1)
                loop(pool, PAIRS, turn)

            @block.vector
            def _(dve):
                for p in range(2):
                    nc.vector.memset(gel[p][:, :, WL:WL + 1], 0.0).then_inc(s["h_set"], 1)
                def turn(j):
                    for p in range(2):
                        i = j * 2 + p
                        wait(dve, down[p], j + 1)
                        wait(dve, s["h_bias"], i + 1)
                        wait(dve, sent[p], j * 64)
                        nc.vector.tensor_tensor(y[p][:], Op[p][0:TL, :].rearrange("p (t d) -> p t d", t=4),
                                                g.h[0:TL, bass.ds(i * 4, 4), :], ALU.add).then_inc(summed[p], 1)
                loop(dve, PAIRS // 2, turn)
        s.clear()


def expert_phase(nc, g, A, out):
    with ExitStack() as ctx:
        s = Sems(nc, ctx, "e_load e_set e_w0 e_w1 e_in0 e_in1 e_turned e_xT e_up e_gelu e_down e_biased e_y e_now e_done0 e_done1")

        def sb(name, shape, dt=F32):
            return ctx.enter_context(nc.sbuf_tensor("e_" + name, shape, dt))

        w1 = [sb(f"w1{p}", [D, EH]) for p in range(2)]
        w2 = [sb(f"w2{p}", [128, 4, D]) for p in range(2)]
        b1, b2 = sb("b1", [128, E, 4]), sb("b2", [TL, E, D])
        x = [sb(f"x{p}", [TL, TILES, ROW]) for p in range(2)]
        xT = sb("xT", [D, TILES * TL])
        gel = sb("gel", [128, 4, TILES * TL])
        y = [sb(f"y{p}", [TL, TILES, D]) for p in range(2)]
        Xp = [ctx.enter_context(nc.psum_tensor(f"e_X{n}", [128, 512], F32)) for n in range(2)]
        Up = [ctx.enter_context(nc.psum_tensor(f"e_U{n}", [128, 512], F32)) for n in range(4)]
        Op = [ctx.enter_context(nc.psum_tensor(f"e_O{n}", [128, 512], F32)) for n in range(2)]
        w_in, x_in = [s["e_w0"], s["e_w1"]], [s["e_in0"], s["e_in1"]]
        HALF = CAP // 2
        done, now = [s["e_done0"], s["e_done1"]], [sb(f"now{p}", [TL, TILES], I32) for p in range(2)]

        with nc.Block() as block:
            @block.sync
            def _(sp):
                sp.dma_start(b1[:], A["eb1"]).then_inc(s["e_load"], 16)
                sp.dma_start(b2[:], A["eb2"]).then_inc(s["e_load"], 16)
                def turn(j):
                    for p in range(2):
                        wait(sp, s["e_down"], 4 * j)
                        e = bass.ds(j * 2 + p, 1)
                        sp.dma_start(w1[p][:], A["ew1"][e].rearrange("o p n -> p (o n)")).then_inc(w_in[p], 16)
                        sp.dma_start(w2[p][:], A["ew2"][e].rearrange("o p k n -> p (o k) n")).then_inc(w_in[p], 16)
                loop(sp, E // 2, turn)

            @block.gpsimd
            def _(pool):
                pool.wait_ge(s["e_set"], 5)

                def gather(e, p):
                    wait(pool, s["e_y"], 2 * (e - 1))
                    wait(pool, done[p], (e - p) * (8 * TILES))
                    nc.gpsimd.tensor_copy(now[p][:], g.token[:, :, bass.ds(e, 1)].rearrange("p k o -> p (k o)"))\
                        .then_inc(s["e_now"], 1)
                    wait_alone(pool, s["e_now"], e + 1)
                    for k, n in enumerate(SLOTS):
                        nc.gpsimd.indirect_dma_start(
                            out=x[p][0:n, k, :], out_offset=None, in_=g.table[:, :],
                            in_offset=bass.IndirectOffsetOnAxis(now[p][0:n, k:k + 1].bitcast(U32), 0))\
                            .then_inc(x_in[p], 16)

                def scatter(e, p):
                    wait_alone(pool, s["e_y"], 2 * (e + 1))
                    wait(pool, done[1 - p], (e + p) * (8 * TILES))
                    for k, n in enumerate(SLOTS):
                        nc.gpsimd.indirect_dma_start(
                            out=out[:, :], out_offset=bass.IndirectOffsetOnAxis(now[p][0:n, k:k + 1].bitcast(U32), 0),
                            in_=y[p][0:n, k, :], in_offset=None, compute_op=ALU.add).then_inc(done[p], 16)

                gather(0, 0)
                def turn(j):
                    for p in range(2):
                        gather(j * 2 + p + 1, 1 - p)
                        scatter(j * 2 + p, p)
                loop(pool, E // 2 - 1, turn)
                gather(E - 1, 1)
                scatter(E - 2, 0)
                scatter(E - 1, 1)
                for p in range(2):
                    pool.wait_ge(done[p], E * 8 * TILES)

            @block.tensor
            def _(pe):
                pe.wait_ge(s["e_set"], 5)
                def turn(j):
                    for p in range(2):
                        e = j * 2 + p
                        wait(pe, x_in[p], (j + 1) * (16 * TILES))
                        wait(pe, s["e_xT"], 2 * e)
                        for k, n in enumerate(SLOTS):
                            mm = nc.tensor.transpose(Xp[k // 4][:, k % 4 * TL:k % 4 * TL + n], x[p][0:n, k, 0:D],
                                                     g.ident[0:n, 0:n])
                            if k % 4 == 3:
                                mm.then_inc(s["e_turned"], 1)
                        wait(pe, s["e_xT"], 2 * e + 2)
                        wait(pe, w_in[p], j * 32 + 32)
                        for k in range(4):
                            for m in range(2):
                                x8 = 2 * k + m
                                if x8 >= 4:
                                    wait(pe, s["e_gelu"], 8 * e + x8 - 3)
                                else:
                                    wait(pe, s["e_gelu"], 8 * e)
                                nc.tensor.matmul(Up[x8 % 4][:, 0:HALF], w1[p][:, k * 128:(k + 1) * 128],
                                                 xT[:, m * HALF:(m + 1) * HALF], start=True,
                                                 stop=True).then_inc(s["e_up"], 1)
                        wait(pe, s["e_gelu"], 8 * e + 8)
                        for t in range(TILES):
                            if t % 4 == 0:
                                wait(pe, s["e_biased"], 2 * e)
                            for k in range(4):
                                mm = nc.tensor.matmul(Op[t // 4][0:TL, t % 4 * D:(t % 4 + 1) * D],
                                                      gel[:, k, t * TL:(t + 1) * TL], w2[p][:, k, :],
                                                      start=(k == 0), stop=(k == 3))
                            if t % 4 == 3:
                                mm.then_inc(s["e_down"], 1)
                loop(pe, E // 2, turn)

            @block.scalar
            def _(act):
                act.wait_ge(s["e_load"], 32)
                act.wait_ge(s["e_set"], 5)
                def turn(j):
                    for p in range(2):
                        e = j * 2 + p
                        for h in range(2):
                            wait(act, s["e_turned"], 2 * e + h + 1)
                            wait(act, s["e_up"], 8 * e)
                            n = 4 * TL if h == 0 else CAP - 4 * TL
                            nc.scalar.activation(xT[:, h * 4 * TL:h * 4 * TL + n], Xp[h][:, 0:n],
                                                 ACT.Copy).then_inc(s["e_xT"], 1)
                        for k in range(4):
                            for m in range(2):
                                x8 = 2 * k + m
                                wait_alone(act, s["e_up"], 8 * e + x8 + 1)
                                wait(act, s["e_down"], 2 * e)
                                nc.scalar.activation(gel[:, k, m * HALF:(m + 1) * HALF], Up[x8 % 4][:, 0:HALF],
                                                     ACT.Gelu_apprx_tanh, bias=b1[:, bass.ds(e, 1), k:k + 1]
                                                     .rearrange("p o k -> p (o k)")).then_inc(s["e_gelu"], 1)
                loop(act, E // 2, turn)

            @block.vector
            def _(dve):
                for p in range(2):
                    nc.vector.memset(x[p][:, TILES - 1, :], 0.0).then_inc(s["e_set"], 1)
                    nc.vector.memset(y[p][:, TILES - 1, :], 0.0).then_inc(s["e_set"], 1)
                nc.vector.memset(gel[:, :, CAP:], 0.0).then_inc(s["e_set"], 1)
                dve.wait_ge(s["e_load"], 32)
                def turn(j):
                    for p in range(2):
                        e = j * 2 + p
                        wait(dve, x_in[p], (j + 1) * (16 * TILES))
                        wait(dve, done[p], j * (16 * TILES))
                        for h in range(2):
                            wait(dve, s["e_down"], 2 * e + h + 1)
                            part = y[p][:, 4 * h:4 * h + 4, :]
                            nc.vector.tensor_tensor(part, Op[h][0:TL, :].rearrange("p (t d) -> p t d", t=4),
                                                    b2[:, bass.ds(e, 1), :].to_broadcast([TL, 4, D]),
                                                    ALU.add).then_inc(s["e_biased"], 1)
                            wait(dve, s["e_biased"], 2 * e + h + 1)
                            nc.vector.tensor_tensor(part, part, x[p][:, 4 * h:4 * h + 4, bass.ds(e + D, 1)]
                                                    .to_broadcast([TL, 4, D]), ALU.mult).then_inc(s["e_y"], 1)
                loop(dve, E // 2, turn)
        s.clear()


def constants(np):
    p = np.arange(128)
    same = (p[:, None] // 8 == p[None, :] // 8).astype(np.float32)
    return {
        "same_expert": same, "ahead": same * (p[:, None] < p[None, :]).astype(np.float32),
        "slot": (np.arange(TILES)[None, :] * TL + np.arange(TL)[:, None]).astype(np.float32),
        "first_row": np.repeat((np.arange(E) * NBLK)[None].astype(np.float32), TL, 0),
    }


def lay_out_rest(np, txt, attn, ffn):
    a, f = ({k: np.asarray(v) for k, v in d.items()} for d in (attn, ffn))
    return {
        "txt": np.asarray(txt).reshape(B * TXT, D),
        "taps": np.ascontiguousarray(np.concatenate([a["conv_w"][:, 0, :], a["conv_b"][:, None]], 1)),
        "gate_w": np.ascontiguousarray(np.stack([a["eta_w1"], a["eta_w2"], a["alpha_w1"], a["alpha_w2"]], 1)),
        "memory_w": np.ascontiguousarray(np.stack([a["q_w"].T, a["mem_w1"], a["mem_w2"]], 1)),
        "router_w": f["gate_w"],
        "sw1": f["sw1"], "sw2": np.ascontiguousarray(f["sw2"].reshape(4, 128, D).transpose(1, 0, 2)),
        "sb1": np.ascontiguousarray(f["sb1"].reshape(4, 128).T), "sb2": np.repeat(f["sb2"][None], TL, 0),
        "ew1": f["w1"], "ew2": np.ascontiguousarray(f["w2"].reshape(E, 4, 128, D).transpose(0, 2, 1, 3)),
        "eb1": np.ascontiguousarray(f["b1"].reshape(E, 4, 128).transpose(2, 0, 1)),
        "eb2": np.ascontiguousarray(np.repeat(f["b2"][None], TL, 0)),
    }


def build(nc, A, out):
    with ExitStack() as ctx:
        g = Core()
        vit(nc, g, A, ctx)
        g.xT = ctx.enter_context(nc.sbuf_tensor("xT", [D, T], F32))
        g.logits = ctx.enter_context(nc.sbuf_tensor("logits", [TL, 2, B, E], F32))
        g.token = ctx.enter_context(nc.sbuf_tensor("token", [TL, TILES, E], I32))
        g.hcat = nc.dram_tensor("hcat", [T, D], F32).ap()
        g.table = nc.dram_tensor("table", [T, ROW], F32).ap()
        g.by_expert = nc.dram_tensor("by_expert", [E, T], F32).ap()
        g.counts = nc.dram_tensor("counts", [E * NBLK, BLK], F32).ap()
        g.ends = nc.dram_tensor("ends", [1, E * NBLK], F32).ap()
        with ExitStack() as mctx:
            g.gate_sum = mctx.enter_context(nc.sbuf_tensor("gate_sum", [D, 2, WL], F32))
            g.decay = mctx.enter_context(nc.sbuf_tensor("decay", [D, 2, L], F32))
            g.drift = mctx.enter_context(nc.sbuf_tensor("drift", [D, 2, L], F32))
            g.minus = mctx.enter_context(nc.sbuf_tensor("minus", [D, D], F32))
            fuse_phase(nc, g, A)
            gate_phase(nc, g)
            memory_phase(nc, g, A)
        router_phase(nc, g)
        choice_phase(nc, g, A)
        shared_phase(nc, g, A, out)
        expert_phase(nc, g, A, out)


def kernel(x, txt, **params):
    import numpy as np
    from concourse import bacc
    from concourse.bass_utils import run_bass_kernel_spmd

    def part(prefix):
        return {k.removeprefix(prefix): v for k, v in params.items() if k.startswith(prefix)}

    arrays = {**lay_out(np, x, part("L0_tok_")), **lay_out_rest(np, txt, part("L0_attn_"), part("L0_ffn_")),
              **constants(np)}
    nc = bacc.Bacc("TRN2", target_bir_lowering=False, num_devices=1)
    A = {k: nc.dram_tensor(f"in_{k}", v.shape, mybir.dt.from_np(v.dtype), kind="ExternalInput").ap()
         for k, v in arrays.items()}
    out = nc.dram_tensor("out", [T, D], F32, kind="ExternalOutput").ap()
    build(nc, A, out)
    r = run_bass_kernel_spmd(nc, [{f"in_{k}": v for k, v in arrays.items()}], core_ids=[0])
    return r.results[0]["out"].reshape(B, L, D)
```
